# Optimizing a Trainium2 kernel written in Bass

```python
import numpy as np
import jax
import jax.numpy as jnp

def _softmax(x, axis=-1):
    return jax.nn.softmax(x, axis=axis)

def _gelu(x):
    return jax.nn.gelu(x, approximate=True)

def _silu(x):
    return jax.nn.silu(x)

def _sigmoid(x):
    return jax.nn.sigmoid(x)

def _layernorm(x, axis=-1, eps=1e-05):
    m = jnp.mean(x, axis=axis, keepdims=True)
    v = jnp.var(x, axis=axis, keepdims=True)
    return (x - m) / jnp.sqrt(v + eps)

def _scatter_add(tgt, idx, src, axis=0):
    return tgt.at[idx].add(src)

def _segment_sum(src, seg, n):
    return jax.ops.segment_sum(src, seg, n)
kernel_name = 'mk_xattn_ffn_d2_seqx_r4_58378c'

def setup_inputs(seed: int=0):
    np.random.seed(seed)
    _w = jnp.asarray

    def _rec_inputs():
        import jax
        import jax.numpy as jnp
        _rk = jax.random.key(seed)
        x = 7.22e-05 + 1 * jax.random.normal(jax.random.fold_in(_rk, 1), (2, 1024, 256), jnp.float32)
        _lenS = 1024 - jax.random.randint(jax.random.fold_in(_rk, 7), (2,), 0, max(1, 1024 // 4) + 1, jnp.int32)
        _lenS2 = 77 - jax.random.randint(jax.random.fold_in(_rk, 8), (2,), 0, max(1, 77 // 4) + 1, jnp.int32)
        _ctx_1024P = jax.random.normal(jax.random.fold_in(_rk, 11), (2, 16, 256), jnp.float32)
        _ctx_1024c = jax.random.dirichlet(jax.random.fold_in(_rk, 511), 0.3 * jnp.ones((16,), jnp.float32), (2, 77))
        _ctx_1024t = jnp.einsum('bsk,bkd->bsd', _ctx_1024c, _ctx_1024P)
        _ctx_1024t = _ctx_1024t * jax.lax.rsqrt(jnp.mean(jnp.square(_ctx_1024t)) + 1e-12) * 0.953939
        ctx_1024 = 4.13588e-05 + 0.999923 * (_ctx_1024t + 0.3 * jax.random.normal(jax.random.fold_in(_rk, 611), (2, 77, 256), jnp.float32))
        _validS = jnp.arange(1024)[None, :] < _lenS[:, None]
        _validS2 = jnp.arange(77)[None, :] < _lenS2[:, None]
        _causal = jnp.tril(jnp.ones((1024, 1024), dtype=bool))
        mask_1x1xSxS2_ik0 = jnp.where(jnp.broadcast_to(_validS2[0:1, None, None, :], (1, 1, 1024, 77)), 0, 1).astype(jnp.int32)
        return (x, ctx_1024, mask_1x1xSxS2_ik0)
    x, ctx_1024, mask_1x1xSxS2_ik0 = _rec_inputs()

    def _L0_xattn_setup():
        import jax, jax.numpy as jnp
        import numpy as np
        D_MODEL = 256
        NUM_HEADS = 16
        D_K = D_MODEL // NUM_HEADS
        SCALE = float(np.sqrt(D_K))
        B, S = (4, 512)
        key = jax.random.key(seed)
        ks = jax.random.split(key, 12)
        q = jax.random.normal(ks[0], (B, S, D_MODEL), dtype=jnp.float32)
        k = jax.random.normal(ks[1], (B, S, D_MODEL), dtype=jnp.float32)
        v = jax.random.normal(ks[2], (B, S, D_MODEL), dtype=jnp.float32)
        mask = jnp.tril(jnp.ones((S, S), dtype=jnp.int32))[None, None]
        std = 1.0 / np.sqrt(D_MODEL)
        Wq = jax.random.normal(ks[3], (D_MODEL, D_MODEL), dtype=jnp.float32) * std
        Wk = jax.random.normal(ks[4], (D_MODEL, D_MODEL), dtype=jnp.float32) * std
        Wv = jax.random.normal(ks[5], (D_MODEL, D_MODEL), dtype=jnp.float32) * std
        Wo = jax.random.normal(ks[6], (D_MODEL, D_MODEL), dtype=jnp.float32) * std
        bq = jax.random.normal(ks[7], (D_MODEL,), dtype=jnp.float32) * std
        bk = jax.random.normal(ks[8], (D_MODEL,), dtype=jnp.float32) * std
        bv = jax.random.normal(ks[9], (D_MODEL,), dtype=jnp.float32) * std
        bo = jax.random.normal(ks[10], (D_MODEL,), dtype=jnp.float32) * std
        return {'q': q, 'k': k, 'v': v, 'mask': mask, 'Wq': Wq, 'bq': bq, 'Wk': Wk, 'bk': bk, 'Wv': Wv, 'bv': bv, 'Wo': Wo, 'bo': bo}
    _L0_xattn_all = _L0_xattn_setup()
    _L0_xattn_in = {k: v for k, v in _L0_xattn_all.items() if k in ('Wq', 'bq', 'Wk', 'bk', 'Wv', 'bv', 'Wo', 'bo')}
    del _L0_xattn_all

    def _L0_ffn_setup():
        import jax, jax.numpy as jnp
        import numpy as np
        B, N, D = (4, 1024, 256)
        E, S, F = (16, 64, 512)
        DO = 256
        EPS = 1e-05

        def _layernorm(x, g, b):
            mu = jnp.mean(x, axis=-1, keepdims=True)
            var = jnp.mean(jnp.square(x - mu), axis=-1, keepdims=True)
            return (x - mu) * jax.lax.rsqrt(var + EPS) * g + b
        key = jax.random.key(seed)
        ks = jax.random.split(key, 8)
        d = {'x': jax.random.normal(ks[0], (B, N, D), dtype=jnp.float32), 'norm_g': jnp.ones((D,), jnp.float32), 'norm_b': jnp.zeros((D,), jnp.float32), 'slot_g': jnp.ones((D,), jnp.float32), 'slot_b': jnp.zeros((D,), jnp.float32), 'scale': jnp.ones((1,), jnp.float32), 'slot_embeds': jax.random.normal(ks[1], (E, S, D), jnp.float32) / np.sqrt(D), 'Wg': jax.random.normal(ks[2], (E, D, F), jnp.float32) * np.sqrt(2.0 / (D + F)), 'bg': jnp.zeros((E, F), jnp.float32), 'Wu': jax.random.normal(ks[3], (E, D, F), jnp.float32) * np.sqrt(2.0 / (D + F)), 'bu': jnp.zeros((E, F), jnp.float32), 'Wd': jax.random.normal(ks[4], (E, F, DO), jnp.float32) * np.sqrt(2.0 / (F + DO)), 'bd': jnp.zeros((E, DO), jnp.float32)}
        return d
    _L0_ffn_all = _L0_ffn_setup()
    _L0_ffn_in = {k: v for k, v in _L0_ffn_all.items() if k in ('norm_g', 'norm_b', 'slot_g', 'slot_b', 'scale', 'slot_embeds', 'Wg', 'bg', 'Wu', 'bu', 'Wd', 'bd')}
    del _L0_ffn_all

    def _L1_xattn_setup():
        import jax, jax.numpy as jnp
        import numpy as np
        EMBED_DIM = 256
        NUM_HEAD = 16
        HEAD_DIM = EMBED_DIM // NUM_HEAD
        SCALE = HEAD_DIM ** (-0.5)
        key = jax.random.key(seed)
        ks = jax.random.split(key, 8)
        B, N, K, D = (2, 512, 512, EMBED_DIM)
        s = D ** (-0.5)
        return {'x': jax.random.normal(ks[0], (B, N, D), jnp.float32), 'ctx': jax.random.normal(ks[1], (B, K, D), jnp.float32), 'Wq': jax.random.normal(ks[2], (D, D), jnp.float32) * s, 'bq': jnp.zeros((D,), jnp.float32), 'Wkv': jax.random.normal(ks[3], (D, 2 * D), jnp.float32) * s, 'bkv': jnp.zeros((2 * D,), jnp.float32), 'Wproj': jax.random.normal(ks[4], (D, D), jnp.float32) * s, 'bproj': jnp.zeros((D,), jnp.float32)}
    _L1_xattn_all = _L1_xattn_setup()
    _L1_xattn_in = {k: v for k, v in _L1_xattn_all.items() if k in ('Wq', 'bq', 'Wkv', 'bkv', 'Wproj', 'bproj')}
    del _L1_xattn_all

    def _L1_ffn_setup():
        import jax, jax.numpy as jnp
        import numpy as np
        K = 3
        TAU = 1.0
        EPS = 1e-08

        def _route_dense(z, k, tau):
            topi = jax.lax.top_k(z, k)[1]
            topv = jnp.take_along_axis(z, topi, axis=1)
            w = jax.nn.softmax(topv / (tau + EPS), axis=1)
            N, L = z.shape
            dw = jnp.zeros((N, L), z.dtype)
            dw = dw.at[jnp.arange(N)[:, None], topi].add(w)
            return dw

        def _apply_mixture(x, dw, W):
            y = jnp.zeros((x.shape[0], W.shape[1]), x.dtype)
            for e in range(W.shape[0]):
                y = y + x @ W[e].T * dw[:, e:e + 1]
            return y
        key = jax.random.key(seed)
        ks = jax.random.split(key, 8)
        B, T, D_in, H, D_out, L, d_addr = (4, 512, 256, 1024, 256, 12, 64)

        def unitize(U):
            U = U - U.mean(axis=1, keepdims=True)
            return U / (jnp.linalg.norm(U, axis=1, keepdims=True) + EPS)
        x = jax.random.normal(ks[0], (B, T, D_in), jnp.float32)
        P_w = jax.random.normal(ks[1], (d_addr, D_in), jnp.float32) / np.sqrt(D_in)
        U1 = unitize(jax.random.normal(ks[2], (L, d_addr), jnp.float32))
        U2 = unitize(jax.random.normal(ks[3], (L, d_addr), jnp.float32))
        U3 = unitize(jax.random.normal(ks[4], (L, d_addr), jnp.float32))
        W1 = jax.random.normal(ks[5], (L, H, D_in), jnp.float32)
        W1 = W1 / jnp.linalg.norm(W1.reshape(L, -1), axis=1)[:, None, None]
        W2 = jax.random.normal(ks[6], (L, D_out, H), jnp.float32)
        W2 = W2 / jnp.linalg.norm(W2.reshape(L, -1), axis=1)[:, None, None]
        b2 = jax.random.normal(ks[7], (L, D_out), jnp.float32)
        b2 = b2 / jnp.linalg.norm(b2, axis=1, keepdims=True)
        return {'x': x, 'P_w': P_w, 'U1': U1, 'U2': U2, 'U3': U3, 'W1': W1, 'W2': W2, 'b2': b2}
    _L1_ffn_all = _L1_ffn_setup()
    _L1_ffn_in = {k: v for k, v in _L1_ffn_all.items() if k in ('P_w', 'U1', 'U2', 'U3', 'W1', 'W2', 'b2')}
    del _L1_ffn_all
    return {'x': x, 'ctx_1024': ctx_1024, 'mask_1x1xSxS2_ik0': mask_1x1xSxS2_ik0, 'L0_xattn_Wq': _L0_xattn_in['Wq'], 'L0_xattn_bq': _L0_xattn_in['bq'], 'L0_xattn_Wk': _L0_xattn_in['Wk'], 'L0_xattn_bk': _L0_xattn_in['bk'], 'L0_xattn_Wv': _L0_xattn_in['Wv'], 'L0_xattn_bv': _L0_xattn_in['bv'], 'L0_xattn_Wo': _L0_xattn_in['Wo'], 'L0_xattn_bo': _L0_xattn_in['bo'], 'L0_ffn_norm_g': _L0_ffn_in['norm_g'], 'L0_ffn_norm_b': _L0_ffn_in['norm_b'], 'L0_ffn_slot_g': _L0_ffn_in['slot_g'], 'L0_ffn_slot_b': _L0_ffn_in['slot_b'], 'L0_ffn_scale': _L0_ffn_in['scale'], 'L0_ffn_slot_embeds': _L0_ffn_in['slot_embeds'], 'L0_ffn_Wg': _L0_ffn_in['Wg'], 'L0_ffn_bg': _L0_ffn_in['bg'], 'L0_ffn_Wu': _L0_ffn_in['Wu'], 'L0_ffn_bu': _L0_ffn_in['bu'], 'L0_ffn_Wd': _L0_ffn_in['Wd'], 'L0_ffn_bd': _L0_ffn_in['bd'], 'L1_xattn_Wq': _L1_xattn_in['Wq'], 'L1_xattn_bq': _L1_xattn_in['bq'], 'L1_xattn_Wkv': _L1_xattn_in['Wkv'], 'L1_xattn_bkv': _L1_xattn_in['bkv'], 'L1_xattn_Wproj': _L1_xattn_in['Wproj'], 'L1_xattn_bproj': _L1_xattn_in['bproj'], 'L1_ffn_P_w': _L1_ffn_in['P_w'], 'L1_ffn_U1': _L1_ffn_in['U1'], 'L1_ffn_U2': _L1_ffn_in['U2'], 'L1_ffn_U3': _L1_ffn_in['U3'], 'L1_ffn_W1': _L1_ffn_in['W1'], 'L1_ffn_W2': _L1_ffn_in['W2'], 'L1_ffn_b2': _L1_ffn_in['b2']}

def reference(x, ctx_1024, mask_1x1xSxS2_ik0, L0_xattn_Wq, L0_xattn_bq, L0_xattn_Wk, L0_xattn_bk, L0_xattn_Wv, L0_xattn_bv, L0_xattn_Wo, L0_xattn_bo, L0_ffn_norm_g, L0_ffn_norm_b, L0_ffn_slot_g, L0_ffn_slot_b, L0_ffn_scale, L0_ffn_slot_embeds, L0_ffn_Wg, L0_ffn_bg, L0_ffn_Wu, L0_ffn_bu, L0_ffn_Wd, L0_ffn_bd, L1_xattn_Wq, L1_xattn_bq, L1_xattn_Wkv, L1_xattn_bkv, L1_xattn_Wproj, L1_xattn_bproj, L1_ffn_P_w, L1_ffn_U1, L1_ffn_U2, L1_ffn_U3, L1_ffn_W1, L1_ffn_W2, L1_ffn_b2):
    import jax
    import jax.numpy as jnp

    def _L0_xattn_ref(q, k, v, mask, Wq, bq, Wk, bk, Wv, bv, Wo, bo):
        import jax, jax.numpy as jnp
        import numpy as np
        D_MODEL = 256
        NUM_HEADS = 16
        D_K = D_MODEL // NUM_HEADS
        SCALE = float(np.sqrt(D_K))
        B, S = (4, 512)
        Bsz = q.shape[0]

        def proj(x, W, b):
            y = x @ W.T + b
            return y.reshape(Bsz, -1, NUM_HEADS, D_K).transpose(0, 2, 1, 3)
        qh = proj(q, Wq, bq)
        kh = proj(k, Wk, bk)
        vh = proj(v, Wv, bv)
        scores = jnp.einsum('bhqd,bhkd->bhqk', qh, kh) / SCALE
        scores = jnp.where(mask == 0, jnp.float32(-1000000000.0), scores)
        attn = jax.nn.softmax(scores, axis=-1)
        out = jnp.einsum('bhqk,bhkd->bhqd', attn, vh)
        out = out.transpose(0, 2, 1, 3).reshape(Bsz, -1, D_MODEL)
        return out @ Wo.T + bo

    def _L0_ffn_ref(x, norm_g, norm_b, slot_g, slot_b, scale, slot_embeds, Wg, bg, Wu, bu, Wd, bd):
        import jax, jax.numpy as jnp
        import numpy as np
        B, N, D = (4, 1024, 256)
        E, S, F = (16, 64, 512)
        DO = 256
        EPS = 1e-05

        def _layernorm(x, g, b):
            mu = jnp.mean(x, axis=-1, keepdims=True)
            var = jnp.mean(jnp.square(x - mu), axis=-1, keepdims=True)
            return (x - mu) * jax.lax.rsqrt(var + EPS) * g + b
        x = _layernorm(x, norm_g, norm_b)
        se = _layernorm(slot_embeds, slot_g, slot_b) * scale
        logits = jnp.einsum('bnd,esd->bnes', x, se)
        dispatch = jax.nn.softmax(logits, axis=1)
        combine = jax.nn.softmax(logits.reshape(x.shape[0], x.shape[1], -1), axis=-1)
        slots = jnp.einsum('bnd,bnes->besd', x, dispatch)
        gate = jax.nn.gelu(jnp.einsum('besd,edf->besf', slots, Wg) + bg[None, :, None, :], approximate=False)
        up = jnp.einsum('besd,edf->besf', slots, Wu) + bu[None, :, None, :]
        eout = jnp.einsum('besf,efo->beso', gate * up, Wd) + bd[None, :, None, :]
        eout = eout.reshape(eout.shape[0], -1, eout.shape[-1])
        return jnp.einsum('bns,bso->bno', combine, eout)

    def _L1_xattn_ref(x, ctx, Wq, bq, Wkv, bkv, Wproj, bproj):
        import jax, jax.numpy as jnp
        import numpy as np
        EMBED_DIM = 256
        NUM_HEAD = 16
        HEAD_DIM = EMBED_DIM // NUM_HEAD
        SCALE = HEAD_DIM ** (-0.5)
        B, N, D = x.shape
        K = ctx.shape[1]
        H, hd = (NUM_HEAD, HEAD_DIM)
        q = (x @ Wq + bq).reshape(B, N, H, hd).transpose(0, 2, 1, 3)
        kv = (ctx @ Wkv + bkv).reshape(B, K, 2, H, hd).transpose(2, 0, 3, 1, 4)
        k, v = (kv[0], kv[1])
        attn = jnp.einsum('bhnd,bhkd->bhnk', q * SCALE, k)
        attn = jax.nn.softmax(attn, axis=-1)
        out = jnp.einsum('bhnk,bhkd->bhnd', attn, v)
        out = out.transpose(0, 2, 1, 3).reshape(B, N, D)
        return out @ Wproj + bproj

    def _L1_ffn_ref(x, P_w, U1, U2, U3, W1, W2, b2):
        import jax, jax.numpy as jnp
        import numpy as np
        K = 3
        TAU = 1.0
        EPS = 1e-08

        def _route_dense(z, k, tau):
            topi = jax.lax.top_k(z, k)[1]
            topv = jnp.take_along_axis(z, topi, axis=1)
            w = jax.nn.softmax(topv / (tau + EPS), axis=1)
            N, L = z.shape
            dw = jnp.zeros((N, L), z.dtype)
            dw = dw.at[jnp.arange(N)[:, None], topi].add(w)
            return dw

        def _apply_mixture(x, dw, W):
            y = jnp.zeros((x.shape[0], W.shape[1]), x.dtype)
            for e in range(W.shape[0]):
                y = y + x @ W[e].T * dw[:, e:e + 1]
            return y
        B, T, D = x.shape
        x_flat = x.reshape(B * T, D)
        x_addr = x_flat @ P_w.T
        dw1 = _route_dense(x_addr @ U1.T, K, TAU)
        dw2 = _route_dense(x_addr @ U2.T, K, TAU)
        dw3 = _route_dense(x_addr @ U3.T, K, TAU)
        h = _apply_mixture(x_flat, dw1, W1)
        h = jax.nn.gelu(h, approximate=False)
        y = _apply_mixture(h, dw2, W2)
        y = y + dw3 @ b2
        return y.reshape(B, T, -1)
    x = x + _L0_xattn_ref(_layernorm(x, axis=-1), ctx_1024, ctx_1024, mask_1x1xSxS2_ik0, L0_xattn_Wq, L0_xattn_bq, L0_xattn_Wk, L0_xattn_bk, L0_xattn_Wv, L0_xattn_bv, L0_xattn_Wo, L0_xattn_bo)
    x = x + _L0_ffn_ref(_layernorm(x, axis=-1), L0_ffn_norm_g, L0_ffn_norm_b, L0_ffn_slot_g, L0_ffn_slot_b, L0_ffn_scale, L0_ffn_slot_embeds, L0_ffn_Wg, L0_ffn_bg, L0_ffn_Wu, L0_ffn_bu, L0_ffn_Wd, L0_ffn_bd)
    x = x + _L1_xattn_ref(_layernorm(x, axis=-1), ctx_1024, L1_xattn_Wq, L1_xattn_bq, L1_xattn_Wkv, L1_xattn_bkv, L1_xattn_Wproj, L1_xattn_bproj)
    x = x + _L1_ffn_ref(_layernorm(x, axis=-1), L1_ffn_P_w, L1_ffn_U1, L1_ffn_U2, L1_ffn_U3, L1_ffn_W1, L1_ffn_W2, L1_ffn_b2)
    return x

_drawn_inputs = setup_inputs


def setup_inputs(seed=0):
    import zlib

    import numpy as np

    out = dict(_drawn_inputs(seed))
    spreads = {'L0_ffn_norm_g': (1.0, 0.2),
     'L0_ffn_norm_b': (0.0, 0.1),
     'L0_ffn_slot_g': (1.0, 0.2),
     'L0_ffn_slot_b': (0.0, 0.1),
     'L0_ffn_bg': (0.0, 0.1),
     'L0_ffn_bu': (0.0, 0.1),
     'L0_ffn_bd': (0.0, 0.1),
     'L1_xattn_bq': (0.0, 0.295),
     'L1_xattn_bkv': (0.0, 0.1),
     'L1_xattn_bproj': (0.0, 0.1)}
    factors = {'L0_xattn_bq': 3.742,
     'L0_xattn_bk': 8.0,
     'L1_ffn_U1': 8.0,
     'L1_ffn_U2': 8.0,
     'L1_ffn_W1': 8.0,
     'L1_ffn_W2': 8.0}
    for name, (base, spread) in spreads.items():
        noise = np.random.default_rng([zlib.crc32(name.encode()), seed]).standard_normal(out[name].shape)
        drawn = base * np.exp(spread * noise) if base else spread * noise
        out[name] = jnp.asarray(drawn.astype(out[name].dtype))
    for name, factor in factors.items():
        out[name] = (out[name] * factor).astype(out[name].dtype)
    return out
```

```python
from contextlib import ExitStack

import concourse.bass as bass
from concourse import mybir

ALU = mybir.AluOpType
ACT = mybir.ActivationFunctionType
AX = mybir.AxisListType
F32 = mybir.dt.float32
I32 = mybir.dt.int32
U32 = mybir.dt.uint32

P = 128
B = 2
N = 1024
D = 256
KD = D // P
NT = N // P
S2 = 77
H = 16
DK = D // H
HC = H // KD
HG = 4
NG = H // HG
FLAT = H * S2
NCH = -(-FLAT // P)
CHR = [min(P, FLAT - c * P) for c in range(NCH)]
VH = 3
VC = DK + 1
H0 = [min(c * P // S2, H - VH) for c in range(NCH)]
PTG = [range(0, 4), range(4, 8), range(8, NCH)]
E0, SL, F0 = 16, 64, 512
NS = E0 * SL
CS = NS // P
KF = F0 // P
E1, HID = 12, 1024
TOP = 3
R = 3
DA = 64
KH = HID // P
BANK = 512
SCALE = 0.25
NEG = -1.0e9
BIG = 3.0e38


def wait(eng, sem, value):
    if isinstance(value, int) and value <= 0:
        return
    eng.wait_ge(sem, value)


class Chain:

    def __init__(self, eng, sem, per_turn):
        self.eng, self.sem, self.per_turn = eng, sem, per_turn

    def turn(self, i):
        self.base, self.n = i * self.per_turn, 0

    def step(self, ins, hold=True):
        ins.then_inc(self.sem, 1)
        self.n += 1
        if hold:
            self.eng.wait_ge(self.sem, self.base + self.n)

    def hold(self):
        self.eng.wait_ge(self.sem, self.base + self.n)

    def end(self):
        assert self.n == self.per_turn, (self.n, self.per_turn)


def build(nc, t, out):
    ctx = ExitStack()

    def sb(stack, name, shape, dt=F32):
        return stack.enter_context(nc.sbuf_tensor(name, shape, dt))

    def ps(stack, name, shape):
        return stack.enter_context(nc.psum_tensor(name, shape, F32))

    def sem(name):
        return ctx.enter_context(nc.semaphore(name))

    with ctx:
        X = sb(ctx, "X", [P, B, NT, D])
        ident = sb(ctx, "ident", [P, P])
        ones = sb(ctx, "ones", [1, P])
        loaded_x = sem("loaded_x")
        loaded_const = sem("loaded_const")
        ones_ready = sem("ones_ready")

        with nc.Block() as block:
            @block.sync
            def _(sp):
                for b in range(B):
                    sp.dma_start(X[:, b], t["x"][b].rearrange("(t p) d -> p t d", p=P)).then_inc(loaded_x, 16)
                sp.dma_start(ident[:, :], t["c_ident"]).then_inc(loaded_const, 16)
                sp.wait_ge(loaded_x, 16 * B)
                sp.wait_ge(loaded_const, 16)

            @block.vector
            def _(dve):
                nc.vector.memset(ones[:, :], 1.0).then_inc(ones_ready, 1)
                dve.wait_ge(ones_ready, 1)

        TT = B * NT
        stats = sb(ctx, "stats", [P, TT, 6])
        mean = sb(ctx, "mean", [P, TT])
        mdif = sb(ctx, "mdif", [P, TT])
        rstd = sb(ctx, "rstd", [P, TT])
        veps = sb(ctx, "veps", [P, TT])
        mhalf = sb(ctx, "mhalf", [P, TT])

        def norm_stats(a, rows, n):
            agg = sem(a + "agg")
            var = sem(a + "var")
            inv = sem(a + "inv")
            with nc.Block() as block:
                @block.vector
                def _(dve):
                    me, ve, mo, vo = (stats[:, 0:n, i] for i in (1, 2, 4, 5))
                    dve.memset(mhalf[:, 0:n], -0.5).then_inc(agg, 1)
                    with dve.Fori(0, n // 4) as q:
                        for i in range(4):
                            dve.bn_stats(stats[:, q * 4 + i, :], rows[:, q * 4 + i, :]).then_inc(agg, 1)
                    dve.wait_ge(agg, n + 1)
                    dve.tensor_tensor(mean[:, 0:n], me, mo, ALU.add).then_inc(var, 1)
                    dve.tensor_tensor(mdif[:, 0:n], me, mo, ALU.subtract).then_inc(var, 1)
                    dve.tensor_tensor(veps[:, 0:n], ve, vo, ALU.add).then_inc(var, 1)
                    dve.wait_ge(var, 3)
                    dve.tensor_scalar(mean[:, 0:n], mean[:, 0:n], 0.5, None, ALU.mult).then_inc(var, 1)
                    dve.scalar_tensor_tensor(mdif[:, 0:n], mdif[:, 0:n], 0.25, mdif[:, 0:n], ALU.mult, ALU.mult
                                             ).then_inc(var, 1)
                    dve.tensor_scalar(veps[:, 0:n], veps[:, 0:n], 1.0 / D, 1e-5, ALU.mult, ALU.add).then_inc(var, 1)
                    dve.wait_ge(var, 6)
                    dve.tensor_tensor(veps[:, 0:n], veps[:, 0:n], mdif[:, 0:n], ALU.add).then_inc(var, 1)
                    dve.wait_ge(inv, 1)

                @block.gpsimd
                def _(pool):
                    pool.wait_ge(var, 7)
                    pool.tensor_tensor(rstd[:, 0:n], veps[:, 0:n], mhalf[:, 0:n], ALU.pow).then_inc(inv, 1)

        def attention(a, wq, wk, wv, wo, bq, bk, bv, bo, masked):
            st = ExitStack()
            with st:
                Wq = sb(st, a + "Wq", [P, KD, D])
                Wk = sb(st, a + "Wk", [P, KD, D])
                Wv = sb(st, a + "Wv", [P, KD, D])
                Wo = sb(st, a + "Wo", [P, KD, D])
                bqc = sb(st, a + "bqc", [P, KD])
                bkc = sb(st, a + "bkc", [P, KD])
                bvr = sb(st, a + "bvr", [1, D])
                bor = sb(st, a + "bor", [1, D])
                ctxT = sb(st, a + "ctxT", [P, KD, B * S2])
                sel = sb(st, a + "sel", [P, FLAT])
                hmk = sb(st, a + "hmk", [P, HC])
                hmv = sb(st, a + "hmv", [P, NCH * VH])
                kT = sb(st, a + "kT", [P, KD, B * S2])
                kblk = sb(st, a + "kblk", [P, B, KD, HC, S2])
                vsb = sb(st, a + "vsb", [P, B, H, VC])
                vblk = sb(st, a + "vblk", [P, B, NCH, VH * VC])
                xn = sb(st, a + "xn", [P, B, D])
                xnT = sb(st, a + "xnT", [P, B, KD, P])
                qT = sb(st, a + "qT", [P, B, KD, P])
                sc = sb(st, a + "sc", [P, B, H, S2])
                pr = sb(st, a + "pr", [P, B, FLAT])
                mx = sb(st, a + "mx", [P, B, H])
                rsum = sb(st, a + "rsum", [P, B, H])
                pT = sb(st, a + "pT", [P, B, NCH, P])
                o = sb(st, a + "o", [P, B, H, DK])
                oT = sb(st, a + "oT", [P, B, KD, P])
                if masked:
                    mi = sb(st, a + "mi", [P, NT, S2], I32)
                    cap = sb(st, a + "cap", [P, NT, S2])
                psS = ps(st, a + "psS", [P, NG, BANK])
                psA = ps(st, a + "psA", [P, 2, 2 * P])
                psP = ps(st, a + "psP", [P, 2, BANK])
                psO = ps(st, a + "psO", [P, BANK])

                loaded = sem(a + "loaded")
                kv_mm = sem(a + "kv_mm")
                kv_sb = sem(a + "kv_sb")
                kv_blk = sem(a + "kv_blk")
                cap_step = sem(a + "cap_step")
                n_loads = 12 + (1 if masked else 0)

                with nc.Block() as block:
                    @block.sync
                    def _(sp):
                        for w, src in ((Wk, wk), (Wv, wv), (Wq, wq), (Wo, wo)):
                            sp.dma_start(w[:, :, :], src.rearrange("(k p) n -> p k n", p=P)).then_inc(loaded, 16)
                        sp.dma_start(ctxT[:, :, :], t["ctxT"].rearrange("(k p) n -> p k n", p=P)).then_inc(loaded, 16)
                        for w, src in ((bqc, bq), (bkc, bk)):
                            sp.dma_start(w[:, :], src).then_inc(loaded, 16)
                        for w, src in ((bvr, bv), (bor, bo)):
                            sp.dma_start(w[:, :], src.rearrange("(a d) -> a d", a=1)).then_inc(loaded, 16)
                        sp.dma_start(sel[0:S2, :], t["c_sel"]).then_inc(loaded, 16)
                        sp.dma_start(hmk[:, :], t["c_hmk"]).then_inc(loaded, 16)
                        sp.dma_start(hmv[:, :], t["c_hmv"]).then_inc(loaded, 16)
                        if masked:
                            sp.dma_start(mi[:, :, :], t["mask"].rearrange("a b (t p) k -> p (a b t) k", p=P)
                                         ).then_inc(loaded, 16)

                    @block.tensor
                    def _(pe):
                        pe.wait_ge(loaded, 16 * n_loads)
                        for m in range(KD):
                            for k in range(KD):
                                mm = pe.matmul(psA[:, m, 0:B * S2], Wk[:, k, m * P:(m + 1) * P], ctxT[:, k, :],
                                               start=k == 0, stop=k == KD - 1)
                        mm.then_inc(kv_mm, 1)
                        for b in range(B):
                            for k in range(KD):
                                pe.matmul(psS[0:S2, b, 0:D], ctxT[:, k, b * S2:(b + 1) * S2], Wv[:, k, :],
                                          start=k == 0, stop=False)
                            mm = pe.matmul(psS[0:S2, b, 0:D], ones[0:1, 0:S2], bvr[:, :], start=False, stop=True)
                        mm.then_inc(kv_mm, 1)
                        pe.wait_ge(kv_sb, 4 + B)
                        for b in range(B):
                            for c in range(NCH):
                                mm = pe.matmul(psP[0:CHR[c], b, c * VH * VC:(c + 1) * VH * VC],
                                               sel[0:S2, c * P:c * P + CHR[c]],
                                               vsb[0:S2, b, H0[c]:H0[c] + VH, :], start=True, stop=True)
                        mm.then_inc(kv_mm, 1)

                    @block.vector
                    def _(dve):
                        dve.wait_ge(loaded, 16 * n_loads)
                        if masked:
                            dve.tensor_scalar(cap[:, :, :], mi[:, :, :], 0, BIG, ALU.not_equal, ALU.mult
                                              ).then_inc(cap_step, 1)
                            dve.wait_ge(cap_step, 1)
                            dve.tensor_scalar(cap[:, :, :], cap[:, :, :], NEG, None, ALU.add).then_inc(cap_step, 1)
                            dve.wait_ge(cap_step, 2)
                        dve.memset(vsb[:, :, :, DK:VC], 1.0).then_inc(kv_sb, 1)
                        dve.memset(vblk[:, :, NCH - 1, :], 0.0).then_inc(kv_sb, 1)
                        dve.wait_ge(kv_mm, 1)
                        for m in range(KD):
                            dve.tensor_scalar(kT[:, m, :], psA[:, m, 0:B * S2], bkc[:, m:m + 1], SCALE,
                                              ALU.add, ALU.mult).then_inc(kv_sb, 1)
                        dve.wait_ge(kv_mm, 2)
                        for b in range(B):
                            dve.tensor_copy(vsb[0:S2, b, :, 0:DK],
                                            psS[0:S2, b, 0:D].rearrange("p (h d) -> p h d", h=H)).then_inc(kv_sb, 1)
                        dve.wait_ge(kv_sb, 4 + B)
                        for b in range(B):
                            for m in range(KD):
                                dve.tensor_tensor(
                                    kblk[:, b, m], kT[:, m:m + 1, b * S2:(b + 1) * S2].to_broadcast([P, HC, S2]),
                                    hmk[:, :].unsqueeze(2).to_broadcast([P, HC, S2]), ALU.mult).then_inc(kv_blk, 1)
                        dve.wait_ge(kv_mm, 3)
                        for b in range(B):
                            for rows, c0, c1 in ((P, 0, NCH - 1), (CHR[-1], NCH - 1, NCH)):
                                n = (c1 - c0) * VH
                                dve.tensor_tensor(
                                    vblk[0:rows, b, c0:c1, :].rearrange("p c (h v) -> p (c h) v", v=VC),
                                    psP[0:rows, b, c0 * VH * VC:c1 * VH * VC].rearrange("p (n v) -> p n v", v=VC),
                                    hmv[0:rows, c0 * VH:c1 * VH].unsqueeze(2).to_broadcast([rows, n, VC]),
                                    ALU.mult).then_inc(kv_blk, 1)
                        dve.wait_ge(kv_blk, 4 * B)

                norm_stats(a, X[:, :, :, :].rearrange("p b t d -> p (b t) d"), TT)
                xn_ready = sem(a + "xn_ready")
                xT_mm = sem(a + "xT_mm")
                xT_ready = sem(a + "xT_ready")
                q_mm = sem(a + "q_mm")
                q_ready = sem(a + "q_ready")
                s_mm = sem(a + "s_mm")
                s_read = sem(a + "s_read")
                s_ready = sem(a + "s_ready")
                p_ready = sem(a + "p_ready")
                pT_mm = sem(a + "pT_mm")
                pT_ready = sem(a + "pT_ready")
                pv_mm = sem(a + "pv_mm")
                o_ready = sem(a + "o_ready")
                y_mm = sem(a + "y_mm")
                y_done = sem(a + "y_done")
                front_step = sem(a + "front_step")
                back_step = sem(a + "back_step")
                NPT = len(PTG) + 1

                with nc.Block() as block:
                    @block.vector
                    def _(dve):
                        front = Chain(dve, front_step, B * (3 if masked else 2))
                        back = Chain(dve, back_step, B * 2)

                        def norm_in(j, s):
                            wait(dve, xT_mm, B * (j - 1) + s + 1)
                            i = s * NT + j
                            dve.tensor_scalar(xn[:, s], X[:, s, j], mean[:, bass.ds(i, 1)], rstd[:, bass.ds(i, 1)],
                                              ALU.subtract, ALU.mult).then_inc(xn_ready, 1)

                        def softmax_in(j, s):
                            u = B * j + s
                            dve.wait_ge(s_mm, u + 1)
                            raw = psS[:, :, 0:HG * S2].rearrange("p g (h k) -> p g h k", h=HG)
                            rs = sc[:, s].rearrange("p (g h) k -> p g h k", g=NG)
                            wait(dve, p_ready, B * (j - 1) + s + 1)
                            if masked:
                                for g in range(NG):
                                    ins = dve.tensor_tensor(rs[:, g], raw[:, g],
                                                            cap[:, j].unsqueeze(1).to_broadcast([P, HG, S2]), ALU.min)
                                front.step(ins)
                                dve.sem_inc(s_read, 1)
                                src = rs
                            else:
                                src = raw
                            front.step(dve.tensor_reduce(mx[:, s].rearrange("p (g h) -> p g h", g=NG), src,
                                                         AX.X, ALU.max))
                            for g in range(NG):
                                ins = dve.tensor_tensor(
                                    rs[:, g], src[:, g],
                                    mx[:, s, g * HG:(g + 1) * HG].unsqueeze(2).to_broadcast([P, HG, S2]), ALU.subtract)
                            front.step(ins)
                            if not masked:
                                dve.sem_inc(s_read, 1)
                            dve.sem_inc(s_ready, 1)

                        def normalise(j, s):
                            u = B * j + s
                            dve.wait_ge(pv_mm, u + 1)
                            acc = psO[:, 0:H * VC].rearrange("p (h v) -> p h v", v=VC)
                            back.step(dve.reciprocal(rsum[:, s, :].unsqueeze(2), acc[:, :, DK:VC]))
                            back.step(dve.tensor_tensor(o[:, s], acc[:, :, 0:DK],
                                                        rsum[:, s, :].unsqueeze(2).to_broadcast([P, H, DK]), ALU.mult))
                            dve.sem_inc(o_ready, 1)

                        def residual(j, s):
                            dve.wait_ge(y_mm, B * j + s + 1)
                            dve.tensor_tensor(X[:, s, j], psO[:, 0:D], X[:, s, j], ALU.add).then_inc(y_done, 1)

                        front.turn(0)
                        for s in range(B):
                            norm_in(0, s)
                            softmax_in(0, s)
                        front.end()
                        with dve.Fori(1, NT) as j:
                            front.turn(j)
                            back.turn(j - 1)
                            for s in range(B):
                                norm_in(j, s)
                                normalise(j - 1, s)
                                residual(j - 1, s)
                                softmax_in(j, s)
                            front.end()
                            back.end()
                        back.turn(NT - 1)
                        for s in range(B):
                            normalise(NT - 1, s)
                            residual(NT - 1, s)
                        dve.wait_ge(y_done, B * NT)

                    @block.scalar
                    def _(act):
                        def input_T(j, s):
                            act.wait_ge(xT_mm, B * j + s + 1)
                            act.activation(xnT[:, s].rearrange("p k n -> p (k n)"), psA[:, 0, :], ACT.Copy
                                           ).then_inc(xT_ready, 1)

                        def queries(j, s):
                            act.wait_ge(q_mm, B * j + s + 1)
                            for m in range(KD):
                                ins = act.activation(qT[:, s, m, :], psA[:, 1, m * P:(m + 1) * P], ACT.Identity,
                                                     bias=bqc[:, m:m + 1])
                            ins.then_inc(q_ready, 1)

                        def exponent(j, s):
                            act.wait_ge(s_ready, B * j + s + 1)
                            wait(act, pv_mm, B * (j - 1) + s + 1)
                            act.activation(pr[:, s, :], sc[:, s].rearrange("p h k -> p (h k)"), ACT.Exp
                                           ).then_inc(p_ready, 1)

                        def probs_T(j, s):
                            for g, cs in enumerate(PTG):
                                act.wait_ge(pT_mm, NPT * (B * j + s) + g + 1)
                                full = [c for c in cs if CHR[c] == P]
                                act.activation(pT[:, s, full[0]:full[-1] + 1, :].rearrange("p c n -> p (c n)"),
                                               psP[:, g % 2, 0:len(full) * P], ACT.Copy).then_inc(pT_ready, 1)
                                for c in cs:
                                    if CHR[c] < P:
                                        act.activation(pT[0:CHR[c], s, c, :],
                                                       psP[0:CHR[c], g % 2, (c - cs[0]) * P:(c - cs[0] + 1) * P],
                                                       ACT.Copy).then_inc(pT_ready, 1)

                        def output_T(j, s):
                            act.wait_ge(pT_mm, NPT * (B * j + s) + NPT)
                            act.activation(oT[:, s].rearrange("p k n -> p (k n)"), psP[:, 1, 0:KD * P], ACT.Copy
                                           ).then_inc(pT_ready, 1)

                        for s in range(B):
                            input_T(0, s)
                            queries(0, s)
                            exponent(0, s)
                        with act.Fori(1, NT) as j:
                            for s in range(B):
                                input_T(j, s)
                                probs_T(j - 1, s)
                                queries(j, s)
                                output_T(j - 1, s)
                                exponent(j, s)
                        for s in range(B):
                            probs_T(NT - 1, s)
                            output_T(NT - 1, s)

                    @block.tensor
                    def _(pe):
                        EV = [1, 2, 4]
                        NEV = 5

                        def input_T(j, s):
                            u = B * j + s
                            pe.wait_ge(xn_ready, u + 1)
                            wait(pe, xT_ready, u)
                            for k in range(KD):
                                mm = pe.transpose(psA[:, 0, k * P:(k + 1) * P], xn[:, s, k * P:(k + 1) * P], ident[:, :])
                            mm.then_inc(xT_mm, 1)

                        def queries(j, s):
                            u = B * j + s
                            pe.wait_ge(xT_ready, u + 1)
                            wait(pe, q_ready, u)
                            for m in range(KD):
                                for k in range(KD):
                                    mm = pe.matmul(psA[:, 1, m * P:(m + 1) * P], Wq[:, k, m * P:(m + 1) * P],
                                                   xnT[:, s, k, :], start=k == 0, stop=k == KD - 1)
                            mm.then_inc(q_mm, 1)

                        def scores(j, s):
                            u = B * j + s
                            pe.wait_ge(q_ready, u + 1)
                            wait(pe, s_read, u)
                            for g in range(NG):
                                m, h = divmod(g * HG, HC)
                                mm = pe.matmul(psS[:, g, 0:HG * S2], qT[:, s, m, :], kblk[:, s, m, h:h + HG, :],
                                               start=True, stop=True)
                            mm.then_inc(s_mm, 1)

                        def values(j, s):
                            u = B * j + s
                            pe.wait_ge(p_ready, u + 1)
                            for g, cs in enumerate(PTG):
                                if g >= 2:
                                    pe.wait_ge(pT_ready, NEV * u + EV[g - 2])
                                for c in cs:
                                    mm = pe.transpose(psP[0:CHR[c], g % 2, (c - cs[0]) * P:(c - cs[0] + 1) * P],
                                                      pr[:, s, c * P:c * P + CHR[c]], ident[:, :])
                                mm.then_inc(pT_mm, 1)
                            wait(pe, y_done, u)
                            for g, cs in enumerate(PTG):
                                pe.wait_ge(pT_ready, NEV * u + EV[g])
                                for c in cs:
                                    mm = pe.matmul(psO[:, H0[c] * VC:(H0[c] + VH) * VC], pT[0:CHR[c], s, c, :],
                                                   vblk[0:CHR[c], s, c, :], start=c == 0, stop=c == NCH - 1,
                                                   skip_group_check=True)
                            mm.then_inc(pv_mm, 1)

                        def project(j, s):
                            u = B * j + s
                            pe.wait_ge(o_ready, u + 1)
                            pe.wait_ge(pT_ready, NEV * u + EV[1])
                            for k in range(KD):
                                mm = pe.transpose(psP[:, 1, k * P:(k + 1) * P],
                                                  o[:, s, k * HC:(k + 1) * HC, :], ident[:, :])
                            mm.then_inc(pT_mm, 1)
                            pe.wait_ge(pT_ready, NEV * u + NEV)
                            pe.matmul(psO[:, 0:D], ones[0:1, :], bor[:, :], start=True, stop=False)
                            for k in range(KD):
                                mm = pe.matmul(psO[:, 0:D], oT[:, s, k, :], Wo[:, k, :], start=False, stop=k == KD - 1)
                            mm.then_inc(y_mm, 1)

                        for s in range(B):
                            input_T(0, s)
                            queries(0, s)
                            scores(0, s)
                        with pe.Fori(1, NT) as j:
                            for s in range(B):
                                input_T(j, s)
                                values(j - 1, s)
                                queries(j, s)
                                project(j - 1, s)
                                scores(j, s)
                        for s in range(B):
                            values(NT - 1, s)
                            project(NT - 1, s)

        def soft_mixture():
            st = ExitStack()
            with st:
                XL = sb(st, "m_XL", [P, B, NT, D + 1])
                XLf = XL[:, :, :, :].rearrange("p b t d -> p (b t) d")
                Xf = X[:, :, :, :].rearrange("p b t d -> p (b t) d")
                L = sb(st, "m_L", [P, B, NT, NS])
                cb = sb(st, "m_cb", [P, B, NS])
                nmax = sb(st, "m_nmax", [P, B, NT])
                slT = sb(st, "m_slT", [P, KD, B, NS])

                pre = ExitStack()
                with pre:
                    SE = sb(pre, "m_SE", [P, CS, D])
                    seT = sb(pre, "m_seT", [P, KD, NS])
                    gains = sb(pre, "m_gains", [P, 4, D])
                    scl = sb(pre, "m_scl", [P, 1])
                    cm = sb(pre, "m_cm", [P, B, NS])
                    xw = sb(pre, "m_xw", [P, B, D])
                    xT = sb(pre, "m_xT", [P, B, KD, P])
                    cmx = sb(pre, "m_cmx", [P, B, CS])
                    cmw = sb(pre, "m_cmw", [P, CS, P])
                    psT = ps(pre, "m_psT", [P, B, BANK])
                    psL = ps(pre, "m_psL", [P, B, NS])
                    psC = ps(pre, "m_psC", [P, NS])
                    ld = sem("m_ld")
                    with nc.Block() as block:
                        @block.sync
                        def _(sp):
                            sp.dma_start(SE[:, :, :], t["m_se"].rearrange("(c p) d -> p c d", p=P)).then_inc(ld, 16)
                            for i, n in enumerate(("m_ng", "m_nb", "m_sg", "m_sb")):
                                sp.dma_start(gains[:, i, :], t[n].partition_broadcast(P)).then_inc(ld, 16)
                            sp.dma_start(scl[:, :], t["m_scale"].partition_broadcast(P)).then_inc(ld, 16)
                            sp.wait_ge(ld, 16 * 6)
                    norm_stats("ms_", SE, CS)
                    se_step = sem("m_se_step")
                    se_ready = sem("m_se_ready")
                    se_mm = sem("m_se_mm")
                    seT_ready = sem("m_seT_ready")
                    with nc.Block() as block:
                        @block.vector
                        def _(dve):
                            for c in range(CS):
                                dve.tensor_scalar(SE[:, c], SE[:, c], mean[:, c:c + 1], rstd[:, c:c + 1],
                                                  ALU.subtract, ALU.mult).then_inc(se_step, 1)
                            dve.wait_ge(se_step, CS)
                            dve.tensor_tensor(SE[:, :, :], SE[:, :, :], gains[:, 2:3, :].to_broadcast([P, CS, D]),
                                              ALU.mult).then_inc(se_step, 1)
                            dve.wait_ge(se_step, CS + 1)
                            dve.tensor_tensor(SE[:, :, :], SE[:, :, :], gains[:, 3:4, :].to_broadcast([P, CS, D]),
                                              ALU.add).then_inc(se_step, 1)
                            dve.wait_ge(se_step, CS + 2)
                            dve.tensor_scalar(SE[:, :, :], SE[:, :, :], scl[:, :], None, ALU.mult).then_inc(se_ready, 1)

                        @block.tensor
                        def _(pe):
                            pe.wait_ge(se_ready, 1)
                            for k in range(KD):
                                for c in range(CS):
                                    mm = pe.transpose(psL[:, k, c * P:(c + 1) * P], SE[:, c, k * P:(k + 1) * P],
                                                      ident[:, :])
                            mm.then_inc(se_mm, 1)

                        @block.scalar
                        def _(act):
                            act.wait_ge(se_mm, 1)
                            for k in range(KD):
                                act.activation(seT[:, k, :], psL[:, k, :], ACT.Copy).then_inc(seT_ready, 1)
                            act.wait_ge(seT_ready, KD)

                    norm_stats("m1_", Xf, TT)
                    y_ready = sem("m_y_ready")
                    with nc.Block() as block:
                        @block.vector
                        def _(dve):
                            with dve.Fori(0, NT) as j:
                                for s in range(B):
                                    i = s * NT + j
                                    dve.tensor_scalar(XL[:, s, j, 0:D], X[:, s, j], mean[:, bass.ds(i, 1)],
                                                      rstd[:, bass.ds(i, 1)], ALU.subtract, ALU.mult
                                                      ).then_inc(y_ready, 1)
                            dve.wait_ge(y_ready, TT)
                    norm_stats("m2_", XLf[:, :, 0:D], TT)

                    xl_step = sem("m_xl_step")
                    xl_ready = sem("m_xl_ready")
                    xl_copy = sem("m_xl_copy")
                    xlT_mm = sem("m_xlT_mm")
                    xlT_ready = sem("m_xlT_ready")
                    l_mm = sem("m_l_mm")
                    l_max = sem("m_l_max")
                    l_copy = sem("m_l_copy")
                    cm_step = sem("m_cm_step")
                    cmT_mm = sem("m_cmT_mm")
                    cmw_ready = sem("m_cmw_ready")
                    cb_mm = sem("m_cb_mm")
                    cb_ready = sem("m_cb_ready")
                    with nc.Block() as block:
                        @block.vector
                        def _(dve):
                            dve.memset(cm[:, :, :], -BIG).then_inc(cm_step, 1)
                            dve.memset(XL[:, :, :, D:D + 1], 1.0).then_inc(cm_step, 1)
                            dve.wait_ge(cm_step, 2)
                            xl = Chain(dve, xl_step, B * 2)
                            with dve.Fori(0, NT) as j:
                                xl.turn(j)
                                for s in range(B):
                                    i = s * NT + j
                                    x = XL[:, s, j, 0:D]
                                    xl.step(dve.tensor_scalar(x, x, mean[:, bass.ds(i, 1)], rstd[:, bass.ds(i, 1)],
                                                              ALU.subtract, ALU.mult))
                                    xl.step(dve.tensor_tensor(x, x, gains[:, 0, :], ALU.mult))
                                    dve.wait_ge(xlT_mm, B * j)
                                    dve.wait_ge(xl_copy, B * j)
                                    dve.tensor_tensor(xw[:, s, :], x, gains[:, 1, :], ALU.add).then_inc(xl_ready, 1)
                                for s in range(B):
                                    dve.wait_ge(l_copy, B * j + s + 1)
                                    dve.tensor_reduce(nmax[:, s, bass.ds(j, 1)], L[:, s, j, :], AX.X, ALU.max
                                                      ).then_inc(l_max, 1)
                                    dve.wait_ge(cm_step, B * j + s + 2)
                                    dve.tensor_tensor(cm[:, s, :], cm[:, s, :], L[:, s, j, :], ALU.max
                                                      ).then_inc(cm_step, 1)
                                xl.end()
                            dve.wait_ge(cm_step, 2 + TT)
                            dve.wait_ge(l_max, TT)
                            dve.tensor_scalar(nmax[:, :, :], nmax[:, :, :], -1.0, None, ALU.mult).then_inc(l_max, 1)
                            for b in range(B):
                                dve.wait_ge(cmT_mm, b + 1)
                                dve.tensor_reduce(cmx[:, b, :], psC[:, :].rearrange("p (c n) -> p c n", c=CS),
                                                  AX.X, ALU.max).then_inc(cmw_ready, 1)
                                dve.wait_ge(cmw_ready, 2 * b + 1)
                                wait(dve, cb_mm, b)
                                dve.tensor_copy(cmw[:, :, :], cmx[:, b, :].unsqueeze(2).to_broadcast([P, CS, P])
                                                ).then_inc(cmw_ready, 1)
                                dve.wait_ge(cb_mm, b + 1)
                                dve.tensor_copy(cb[:, b, :], psL[:, b, :]).then_inc(cb_ready, 1)
                            dve.wait_ge(cb_ready, B)
                            dve.wait_ge(l_max, TT + 1)

                        @block.tensor
                        def _(pe):
                            with pe.Fori(0, NT) as j:
                                for s in range(B):
                                    u = B * j + s
                                    pe.wait_ge(xl_ready, u + 1)
                                    pe.wait_ge(xlT_ready, u)
                                    for k in range(KD):
                                        mm = pe.transpose(psT[:, s, k * P:(k + 1) * P],
                                                          xw[:, s, k * P:(k + 1) * P], ident[:, :])
                                    mm.then_inc(xlT_mm, 1)
                                for s in range(B):
                                    u = B * j + s
                                    pe.wait_ge(xlT_ready, u + 1)
                                    pe.wait_ge(l_copy, B * j)
                                    for q in range(NS // BANK):
                                        for k in range(KD):
                                            mm = pe.matmul(psL[:, s, q * BANK:(q + 1) * BANK], xT[:, s, k, :],
                                                           seT[:, k, q * BANK:(q + 1) * BANK],
                                                           start=k == 0, stop=k == KD - 1)
                                    mm.then_inc(l_mm, 1)
                            pe.wait_ge(cm_step, 2 + TT)
                            pe.wait_ge(l_copy, TT)
                            for b in range(B):
                                wait(pe, cmw_ready, 2 * b)
                                for c in range(CS):
                                    mm = pe.transpose(psC[:, c * P:(c + 1) * P], cm[:, b, c * P:(c + 1) * P], ident[:, :])
                                mm.then_inc(cmT_mm, 1)
                                pe.wait_ge(cmw_ready, 2 * b + 2)
                                for c in range(CS):
                                    mm = pe.matmul(psL[:, b, c * P:(c + 1) * P], cmw[:, c, :], ident[:, :],
                                                   start=True, stop=True)
                                mm.then_inc(cb_mm, 1)

                        @block.scalar
                        def _(act):
                            with act.Fori(0, NT) as j:
                                for s in range(B):
                                    u = B * j + s
                                    act.wait_ge(xlT_mm, u + 1)
                                    act.wait_ge(l_mm, B * j)
                                    act.activation(xT[:, s].rearrange("p k n -> p (k n)"), psT[:, s, 0:KD * P], ACT.Copy
                                                   ).then_inc(xlT_ready, 1)
                                    act.activation(XL[:, s, j, 0:D], xw[:, s, :], ACT.Copy).then_inc(xl_copy, 1)
                                for s in range(B):
                                    act.wait_ge(l_mm, B * j + s + 1)
                                    act.activation(L[:, s, j, :], psL[:, s, :], ACT.Copy).then_inc(l_copy, 1)
                            act.wait_ge(l_copy, TT)
                            act.wait_ge(xl_copy, TT)

                mid = ExitStack()
                with mid:
                    dsub = sb(mid, "m_dsub", [P, 2, NS])
                    ed = sb(mid, "m_ed", [P, 2, NS])
                    sl = sb(mid, "m_sl", [P, CS, D])
                    rden = sb(mid, "m_rden", [P, CS])
                    acc = ps(mid, "m_acc", [P, CS, BANK])
                    d_ready = sem("m_d_ready")
                    e_ready = sem("m_e_ready")
                    e_used = sem("m_e_used")
                    sl_step = sem("m_sl_step")
                    sl_mm = sem("m_sl_mm")
                    slT_ready = sem("m_slT_ready")
                    for b in range(B):
                        u0 = b * NT
                        with nc.Block() as block:
                            @block.vector
                            def _(dve):
                                with dve.Fori(0, NT // 2) as q:
                                    for s in range(2):
                                        dve.wait_ge(e_ready, u0 + 2 * q)
                                        dve.tensor_tensor(dsub[:, s, :], L[:, b, 2 * q + s, :], cb[:, b, :],
                                                          ALU.subtract).then_inc(d_ready, 1)
                                dve.wait_ge(e_used, u0 + NT)
                                dve.reciprocal(rden[:, :].unsqueeze(2), acc[:, :, D:D + 1]).then_inc(sl_step, 1)
                                dve.wait_ge(sl_step, b * 2 + 1)
                                dve.tensor_tensor(sl[:, :, :], acc[:, :, 0:D],
                                                  rden[:, :].unsqueeze(2).to_broadcast([P, CS, D]), ALU.mult
                                                  ).then_inc(sl_step, 1)

                            @block.scalar
                            def _(act):
                                with act.Fori(0, NT // 2) as q:
                                    for s in range(2):
                                        act.wait_ge(d_ready, u0 + 2 * q + s + 1)
                                        act.wait_ge(e_used, u0 + 2 * q)
                                        act.activation(ed[:, s, :], dsub[:, s, :], ACT.Exp).then_inc(e_ready, 1)
                                for k in range(KD):
                                    act.wait_ge(sl_mm, KD * b + k + 1)
                                    act.activation(slT[:, k, b, :].rearrange("p (h n) -> p h n", n=BANK),
                                                   acc[:, 2 * k:2 * k + 2, :], ACT.Copy).then_inc(slT_ready, 1)
                                act.wait_ge(slT_ready, KD * (b + 1))

                            @block.tensor
                            def _(pe):
                                def add_tile(q, s, start, stop):
                                    pe.wait_ge(e_ready, u0 + 2 * q + s + 1)
                                    for c in range(CS):
                                        mm = pe.matmul(acc[:, c, 0:D + 1], ed[:, s, c * P:(c + 1) * P],
                                                       XL[:, b, 2 * q + s, :], start=start, stop=stop)
                                    mm.then_inc(e_used, 1)

                                add_tile(0, 0, True, False)
                                add_tile(0, 1, False, False)
                                with pe.Fori(1, NT // 2 - 1) as q:
                                    add_tile(q, 0, False, False)
                                    add_tile(q, 1, False, False)
                                add_tile(NT // 2 - 1, 0, False, False)
                                add_tile(NT // 2 - 1, 1, False, True)
                                pe.wait_ge(sl_step, 2 * b + 2)
                                for k in range(KD):
                                    for c in range(CS):
                                        mm = pe.transpose(acc[:, 2 * k + c // 4, (c % 4) * P:(c % 4 + 1) * P],
                                                          sl[:, c, k * P:(k + 1) * P], ident[:, :])
                                    mm.then_inc(sl_mm, 1)

                post = ExitStack()
                with post:
                    eos = sb(post, "m_eos", [P, B, CS, D])
                    exps = ExitStack()
                    wg_ld = [sem(f"m_wg_ld{i}") for i in range(2)]
                    b_ld = sem("m_b_ld")
                    gu_mm = sem("m_gu_mm")
                    gu_read = sem("m_gu_read")
                    g_pre = sem("m_g_pre")
                    g_act = sem("m_g_act")
                    h_ready = sem("m_h_ready")
                    eo_mm = sem("m_eo_mm")
                    eo_ready = sem("m_eo_ready")
                    eo_moved = [sem(f"m_eo_moved{i}") for i in range(2)]
                    with exps:
                        RING = 2
                        wg = sb(exps, "m_wg", [P, RING, KD, F0])
                        wu = sb(exps, "m_wu", [P, RING, KD, F0])
                        wd = sb(exps, "m_wd", [P, RING, KF, D])
                        bgu = sb(exps, "m_bgu", [P, 2, E0, KF])
                        bdr = sb(exps, "m_bdr", [1, E0, D])
                        TOK = B * SL
                        gt = sb(exps, "m_gt", [P, 2, KF, TOK])
                        up = sb(exps, "m_up", [P, 2, KF, TOK])
                        hT = sb(exps, "m_hT", [P, 2, KF, TOK])
                        eo = sb(exps, "m_eo", [P, 2, D])
                        psG = ps(exps, "m_psG", [P, 2, 2, KF * TOK])
                        psE = ps(exps, "m_psE", [P, 2, BANK])
                        with nc.Block() as block:
                            @block.sync
                            def _(sp):
                                sp.dma_start(bgu[:, 0], t["m_bgT"]).then_inc(b_ld, 16)
                                sp.dma_start(bgu[:, 1], t["m_buT"]).then_inc(b_ld, 16)
                                sp.dma_start(bdr[:, :, :], t["m_bd"].rearrange("(a e) d -> a e d", a=1)).then_inc(b_ld, 16)
                                with sp.Fori(0, E0 // 2) as j:
                                    for s in range(2):
                                        e = 2 * j + s
                                        sp.wait_ge(eo_mm, 2 * j)
                                        sp.dma_start(wg[:, s], t["m_Wg"][e].rearrange("(k p) f -> p k f", p=P)
                                                     ).then_inc(wg_ld[s], 16)
                                        sp.dma_start(wu[:, s], t["m_Wu"][e].rearrange("(k p) f -> p k f", p=P)
                                                     ).then_inc(wg_ld[s], 16)
                                        sp.dma_start(wd[:, s], t["m_Wd"][e].rearrange("(k p) d -> p k d", p=P)
                                                     ).then_inc(wg_ld[s], 16)

                            @block.tensor
                            def _(pe):
                                pe.wait_ge(b_ld, 48)
                                with pe.Fori(0, E0 // 2) as j:
                                    for s in range(2):
                                        e = 2 * j + s
                                        pe.wait_ge(wg_ld[s], 48 * j + 48)
                                        pe.wait_ge(gu_read, 2 * (2 * j))
                                        for i, w in enumerate((wg, wu)):
                                            for f in range(KF):
                                                for k in range(KD):
                                                    mm = pe.matmul(psG[:, s, i, f * TOK:(f + 1) * TOK],
                                                                   w[:, s, k, f * P:(f + 1) * P],
                                                                   slT[:, k, :, bass.ds(e * SL, SL)],
                                                                   start=k == 0, stop=k == KD - 1)
                                        mm.then_inc(gu_mm, 1)
                                    for s in range(2):
                                        e = 2 * j + s
                                        pe.wait_ge(h_ready, e + 1)
                                        pe.wait_ge(eo_ready, 2 * j)
                                        for f in range(KF):
                                            pe.matmul(psE[:, s, 0:D], hT[:, s, f, :], wd[:, s, f, :],
                                                      start=f == 0, stop=False)
                                        pe.matmul(psE[:, s, 0:D], ones[0:1, 0:TOK], bdr[0:1, e, :], start=False, stop=True
                                                  ).then_inc(eo_mm, 1)

                            @block.vector
                            def _(dve):
                                dve.wait_ge(b_ld, 48)
                                with dve.Fori(0, E0 // 2) as j:
                                    for s in range(2):
                                        e = 2 * j + s
                                        dve.wait_ge(gu_mm, e + 1)
                                        wait(dve, g_act, 2 * j)
                                        dve.wait_ge(h_ready, 2 * j)
                                        for i, (dst, sm) in enumerate(((gt, g_pre), (up, gu_read))):
                                            ins = dve.tensor_tensor(
                                                dst[:, s], psG[:, s, i, :].rearrange("p (f n) -> p f n", f=KF),
                                                bgu[:, i, e, :].unsqueeze(2).to_broadcast([P, KF, TOK]), ALU.add)
                                            ins.then_inc(gu_read, 1)
                                    for s in range(2):
                                        e = 2 * j + s
                                        dve.wait_ge(g_act, e + 1)
                                        dve.wait_ge(eo_mm, 2 * j)
                                        dve.tensor_tensor(hT[:, s], gt[:, s], up[:, s], ALU.mult).then_inc(h_ready, 1)
                                dve.wait_ge(h_ready, E0)

                            @block.scalar
                            def _(act):
                                with act.Fori(0, E0 // 2) as j:
                                    for s in range(2):
                                        e = 2 * j + s
                                        act.wait_ge(gu_read, 2 * e + 2)
                                        act.activation(gt[:, s], gt[:, s], ACT.Gelu).then_inc(g_act, 1)
                                    for s in range(2):
                                        e = 2 * j + s
                                        act.wait_ge(eo_mm, e + 1)
                                        act.wait_ge(eo_moved[s], 32 * j)
                                        act.activation(eo[:, s, :], psE[:, s, 0:D], ACT.Copy).then_inc(eo_ready, 1)

                            @block.gpsimd
                            def _(pool):
                                with pool.Fori(0, E0 // 2) as j:
                                    for s in range(2):
                                        e = 2 * j + s
                                        pool.wait_ge(eo_ready, e + 1)
                                        for b in range(B):
                                            pool.dma_start(eos[s * SL:(s + 1) * SL, b, j, :],
                                                           eo[b * SL:(b + 1) * SL, s, :]).then_inc(eo_moved[s], 16)
                                for s in range(2):
                                    pool.wait_ge(eo_moved[s], 32 * (E0 // 2))

                    comb = ExitStack()
                    with comb:
                        ec = sb(comb, "m_ec", [P, B, NS])
                        ecT = sb(comb, "m_ecT", [P, B, CS, P])
                        den = sb(comb, "m_den", [P, B])
                        rdc = sb(comb, "m_rdc", [P, B])
                        psK = ps(comb, "m_psK", [P, B, NS])
                        psY = ps(comb, "m_psY", [P, B, BANK])
                        ec_ready = sem("m_ec_ready")
                        ec_mm = sem("m_ec_mm")
                        ecT_ready = sem("m_ecT_ready")
                        cy_mm = sem("m_cy_mm")
                        cy_step = sem("m_cy_step")
                        cy_done = sem("m_cy_done")
                        with nc.Block() as block:
                            @block.scalar
                            def _(act):
                                with act.Fori(0, NT) as j:
                                    for s in range(B):
                                        act.wait_ge(ec_mm, B * j)
                                        act.wait_ge(cy_step, B * j)
                                        act.activation(ec[:, s, :], L[:, s, j, :], ACT.Exp, bias=nmax[:, s, bass.ds(j, 1)],
                                                       accum_out=den[:, s:s + 1]).then_inc(ec_ready, 1)

                            @block.tensor
                            def _(pe):
                                with pe.Fori(0, NT) as j:
                                    for s in range(B):
                                        u = B * j + s
                                        pe.wait_ge(ec_ready, u + 1)
                                        pe.wait_ge(ecT_ready, B * j)
                                        for c in range(CS):
                                            mm = pe.transpose(psK[:, s, c * P:(c + 1) * P], ec[:, s, c * P:(c + 1) * P],
                                                              ident[:, :])
                                        mm.then_inc(ec_mm, 1)
                                    for s in range(B):
                                        u = B * j + s
                                        pe.wait_ge(ecT_ready, u + 1)
                                        pe.wait_ge(cy_done, B * j)
                                        for c in range(CS):
                                            mm = pe.matmul(psY[:, s, 0:D], ecT[:, s, c, :], eos[:, s, c, :],
                                                           start=c == 0, stop=c == CS - 1)
                                        mm.then_inc(cy_mm, 1)

                            @block.vector
                            def _(dve):
                                with dve.Fori(0, NT) as j:
                                    for s in range(B):
                                        u = B * j + s
                                        dve.wait_ge(ec_mm, u + 1)
                                        dve.wait_ge(cy_mm, B * j)
                                        dve.tensor_copy(ecT[:, s].rearrange("p c n -> p (c n)"), psK[:, s, :]
                                                        ).then_inc(ecT_ready, 1)
                                    for s in range(B):
                                        u = B * j + s
                                        dve.wait_ge(ec_ready, u + 1)
                                        dve.wait_ge(cy_done, u)
                                        dve.reciprocal(rdc[:, s:s + 1], den[:, s:s + 1]).then_inc(cy_step, 1)
                                        dve.wait_ge(cy_step, u + 1)
                                        dve.wait_ge(cy_mm, u + 1)
                                        dve.scalar_tensor_tensor(X[:, s, j], psY[:, s, 0:D], rdc[:, s:s + 1], X[:, s, j],
                                                                 ALU.mult, ALU.add).then_inc(cy_done, 1)
                                dve.wait_ge(cy_done, TT)

        def top3_mixture():
            st = ExitStack()
            with st:
                xnT = sb(st, "f_xnT", [P, KD, TT, P])
                RE = TT * R
                dw = sb(st, "f_dw", [P, TT, R, E1])
                Xf = X[:, :, :, :].rearrange("p b t d -> p (b t) d")
                norm_stats("f_", Xf, TT)

                rt = ExitStack()
                with rt:
                    Pw = sb(rt, "f_Pw", [P, KD, DA])
                    U = sb(rt, "f_U", [DA, R * E1])
                    iota = sb(rt, "f_iota", [P, E1])
                    xn = sb(rt, "f_xn", [P, 2, D])
                    aT = sb(rt, "f_aT", [DA, 2, P])
                    Z = sb(rt, "f_Z", [P, TT, R * E1])
                    Zr = Z[:, :, :].rearrange("p t (r e) -> p (t r) e", r=R)
                    tmp = sb(rt, "f_tmp", [P, RE, E1])
                    hot = sb(rt, "f_hot", [P, TOP, RE, E1])
                    top = sb(rt, "f_top", [P, TOP, RE])
                    first = sb(rt, "f_first", [P, RE])
                    den = sb(rt, "f_den", [P, RE])
                    psT = ps(rt, "f_psT", [P, 2, BANK])
                    psA = ps(rt, "f_psA", [DA, 2, BANK])
                    psZ = ps(rt, "f_psZ", [P, 2, BANK])
                    ld = sem("f_ld")
                    xn_ready = sem("f_xn_ready")
                    xT_mm = sem("f_xT_mm")
                    xT_ready = sem("f_xT_ready")
                    a_mm = sem("f_a_mm")
                    a_ready = sem("f_a_ready")
                    z_mm = sem("f_z_mm")
                    z_ready = sem("f_z_ready")
                    r_step = sem("f_r_step")
                    gap_ready = sem("f_gap_ready")
                    exp_ready = sem("f_exp_ready")
                    with nc.Block() as block:
                        @block.sync
                        def _(sp):
                            sp.dma_start(Pw[:, :, :], t["f_PwT"].rearrange("(k p) a -> p k a", p=P)).then_inc(ld, 16)
                            sp.dma_start(U[:, :], t["f_UT"]).then_inc(ld, 16)
                            sp.dma_start(iota[:, :], t["c_iota"].partition_broadcast(P)).then_inc(ld, 16)

                        @block.vector
                        def _(dve):
                            with dve.Fori(0, TT // 2) as j:
                                for s in range(2):
                                    i = 2 * j + s
                                    dve.wait_ge(xT_mm, 2 * j)
                                    dve.tensor_scalar(xn[:, s, :], Xf[:, i, :], mean[:, bass.ds(i, 1)],
                                                      rstd[:, bass.ds(i, 1)], ALU.subtract, ALU.mult).then_inc(xn_ready, 1)
                                for s in range(2):
                                    i = 2 * j + s
                                    dve.wait_ge(z_mm, i + 1)
                                    dve.tensor_copy(Z[:, i, :], psZ[:, s, 0:R * E1]).then_inc(z_ready, 1)
                            dve.wait_ge(ld, 48)
                            dve.wait_ge(z_ready, TT)
                            one = Chain(dve, r_step, 0)
                            one.turn(0)

                            def over(v):
                                return v.unsqueeze(2).to_broadcast([P, RE, E1])

                            for k in range(TOP):
                                one.step(dve.tensor_reduce(top[:, k, :], Zr, AX.X, ALU.max))
                                one.step(dve.tensor_tensor(tmp[:, :, :], Zr, over(top[:, k, :]), ALU.is_equal))
                                one.step(dve.scalar_tensor_tensor(tmp[:, :, :], tmp[:, :, :], -float(E1),
                                                                  iota[:, :].unsqueeze(1).to_broadcast([P, RE, E1]),
                                                                  ALU.mult, ALU.add))
                                one.step(dve.tensor_reduce(first[:, :], tmp[:, :, :], AX.X, ALU.min))
                                one.step(dve.tensor_tensor(hot[:, k], tmp[:, :, :], over(first[:, :]), ALU.is_equal))
                                one.step(dve.scalar_tensor_tensor(Zr, hot[:, k], -BIG, Zr, ALU.mult, ALU.add))
                            for k in range(1, TOP):
                                one.step(dve.tensor_tensor(top[:, k, :], top[:, k, :], top[:, 0, :], ALU.subtract))
                            one.step(dve.memset(top[:, 0, :], 0.0))
                            dve.sem_inc(gap_ready, 1)
                            dve.wait_ge(exp_ready, 1)
                            one.step(dve.tensor_tensor(den[:, :], top[:, 0, :], top[:, 1, :], ALU.add))
                            one.step(dve.tensor_tensor(den[:, :], den[:, :], top[:, 2, :], ALU.add))
                            one.step(dve.reciprocal(den[:, :], den[:, :]))
                            for k in range(TOP):
                                one.step(dve.tensor_tensor(top[:, k, :], top[:, k, :], den[:, :], ALU.mult))
                                one.step(dve.tensor_tensor(hot[:, k], hot[:, k], over(top[:, k, :]), ALU.mult))
                            dwf = dw[:, :, :, :].rearrange("p t r e -> p (t r) e")
                            one.step(dve.tensor_tensor(dwf, hot[:, 0], hot[:, 1], ALU.add))
                            one.step(dve.tensor_tensor(dwf, dwf, hot[:, 2], ALU.add))

                        @block.scalar
                        def _(act):
                            with act.Fori(0, TT // 2) as j:
                                for s in range(2):
                                    act.wait_ge(xT_mm, 2 * j + s + 1)
                                    act.activation(xnT[:, :, 2 * j + s, :],
                                                   psT[:, s, 0:KD * P].rearrange("p (k n) -> p k n", k=KD), ACT.Copy
                                                   ).then_inc(xT_ready, 1)
                                for s in range(2):
                                    act.wait_ge(a_mm, 2 * j + s + 1)
                                    act.wait_ge(z_mm, 2 * j)
                                    act.activation(aT[:, s, :], psA[:, s, 0:P], ACT.Copy).then_inc(a_ready, 1)
                            act.wait_ge(gap_ready, 1)
                            act.activation(top[:, :, :].rearrange("p k n -> p (k n)"),
                                           top[:, :, :].rearrange("p k n -> p (k n)"), ACT.Exp).then_inc(exp_ready, 1)

                        @block.tensor
                        def _(pe):
                            pe.wait_ge(ld, 48)
                            with pe.Fori(0, TT // 2) as j:
                                for s in range(2):
                                    pe.wait_ge(xn_ready, 2 * j + s + 1)
                                    pe.wait_ge(xT_ready, 2 * j)
                                    for k in range(KD):
                                        mm = pe.transpose(psT[:, s, k * P:(k + 1) * P], xn[:, s, k * P:(k + 1) * P],
                                                          ident[:, :])
                                    mm.then_inc(xT_mm, 1)
                                for s in range(2):
                                    pe.wait_ge(xT_ready, 2 * j + s + 1)
                                    pe.wait_ge(a_ready, 2 * j)
                                    for k in range(KD):
                                        mm = pe.matmul(psA[:, s, 0:P], Pw[:, k, :], xnT[:, k, 2 * j + s, :],
                                                       start=k == 0, stop=k == KD - 1)
                                    mm.then_inc(a_mm, 1)
                                for s in range(2):
                                    pe.wait_ge(a_ready, 2 * j + s + 1)
                                    pe.wait_ge(z_ready, 2 * j)
                                    pe.matmul(psZ[:, s, 0:R * E1], aT[:, s, :], U[:, :], start=True, stop=True
                                              ).then_inc(z_mm, 1)

                W = sb(st, "f_W", [P, E1 * KD * HID])
                h = sb(st, "f_h", [P, TT, HID])
                first = ExitStack()
                with first:
                    W1 = W[:, :].rearrange("p (e k h) -> p e k h", e=E1, k=KD)
                    xs = sb(first, "f_xs", [P, 2, KD, P])
                    NB = 8
                    PT_ = E1 * HID // BANK
                    psH = ps(first, "f_psH", [P, NB, BANK])
                    w1_ld = sem("f_w1_ld")
                    xs_ready = sem("f_xs_ready")
                    h_mm = sem("f_h_mm")
                    h_add = sem("f_h_add")
                    with nc.Block() as block:
                        @block.sync
                        def _(sp):
                            for e in range(E1):
                                sp.dma_start(W1[:, e], t["f_W1T"][e].rearrange("(k p) h -> p k h", p=P)).then_inc(w1_ld, 16)

                        @block.scalar
                        def _(act):
                            with act.Fori(0, TT // 2) as j:
                                for s in range(2):
                                    i = 2 * j + s
                                    act.wait_ge(h_mm, PT_ * 2 * j)
                                    act.activation(xs[:, s], xnT[:, :, i, :], ACT.Copy).then_inc(xs_ready, 1)

                        @block.tensor
                        def _(pe):
                            pe.wait_ge(w1_ld, 16 * E1)
                            with pe.Fori(0, TT // 2) as j:
                                for s in range(2):
                                    i = 2 * j + s
                                    pe.wait_ge(xs_ready, i + 1)
                                    for e in range(E1):
                                        for q in range(HID // BANK):
                                            n = e * (HID // BANK) + q
                                            pe.wait_ge(h_add, PT_ * i + n + 1)
                                            for k in range(KD):
                                                mm = pe.matmul(psH[:, n % NB, :], xs[:, s, k, :],
                                                               W1[:, e, k, q * BANK:(q + 1) * BANK],
                                                               start=k == 0, stop=k == KD - 1)
                                            mm.then_inc(h_mm, 1)

                        @block.vector
                        def _(dve):
                            dve.sem_inc(h_add, NB)
                            with dve.Fori(0, TT // 2) as j:
                                for s in range(2):
                                    i = 2 * j + s
                                    for e in range(E1):
                                        for q in range(HID // BANK):
                                            n = e * (HID // BANK) + q
                                            hq = h[:, i, q * BANK:(q + 1) * BANK]
                                            dve.wait_ge(h_mm, PT_ * i + n + 1)
                                            if e == 0:
                                                ins = dve.tensor_scalar(hq, psH[:, n % NB, :], dw[:, i, 0, e:e + 1], None,
                                                                        ALU.mult)
                                            else:
                                                dve.wait_ge(h_add, NB + PT_ * i + n - 1)
                                                ins = dve.scalar_tensor_tensor(hq, psH[:, n % NB, :], dw[:, i, 0, e:e + 1],
                                                                               hq, ALU.mult, ALU.add)
                                            ins.then_inc(h_add, 1)

                second = ExitStack()
                with second:
                    W2 = W[:, :].rearrange("p (k e d) -> p k e d", k=KH, e=E1)
                    b2 = sb(second, "f_b2", [E1, D])
                    hg = sb(second, "f_hg", [P, HID])
                    dw3 = sb(second, "f_dw3", [P, E1])
                    hT = sb(second, "f_hT", [P, KH, P])
                    dwT = sb(second, "f_dwT", [E1, P])
                    NB2 = 3
                    EP = E1 // 2
                    psT = ps(second, "f2_psT", [P, HID])
                    psB = ps(second, "f2_psB", [P, BANK])
                    psY = ps(second, "f2_psY", [P, NB2, BANK])
                    w2_ld = sem("f_w2_ld")
                    hg_ready = sem("f_hg_ready")
                    hT_mm = sem("f_hT_mm")
                    hT_ready = sem("f_hT_ready")
                    dw3_ready = sem("f_dw3_ready")
                    dwT_mm = sem("f_dwT_mm")
                    dwT_ready = sem("f_dwT_ready")
                    b_mm = sem("f_b_mm")
                    b_add = sem("f_b_add")
                    y_mm = sem("f_y_mm")
                    y_add = sem("f_y_add")
                    with nc.Block() as block:
                        @block.sync
                        def _(sp):
                            for k in range(KH):
                                sp.dma_start(W2[:, k], t["f_W2T"][k]).then_inc(w2_ld, 16)
                            sp.dma_start(b2[:, :], t["f_b2"]).then_inc(w2_ld, 16)

                        @block.tensor
                        def _(pe):
                            pe.wait_ge(w2_ld, 16 * (KH + 1))
                            with pe.Fori(0, TT) as i:
                                pe.wait_ge(hg_ready, i + 1)
                                for k in range(KH):
                                    mm = pe.transpose(psT[:, k * P:(k + 1) * P], hg[:, k * P:(k + 1) * P], ident[:, :])
                                mm.then_inc(hT_mm, 1)
                                pe.wait_ge(b_add, i)
                                pe.wait_ge(dw3_ready, i + 1)
                                pe.transpose(psB[0:E1, 0:P], dw3[:, :], ident[:, :]).then_inc(dwT_mm, 1)
                                pe.wait_ge(dwT_ready, i + 1)
                                pe.matmul(psB[:, P:P + D], dwT[:, :], b2[:, :], start=True, stop=True).then_inc(b_mm, 1)
                                pe.wait_ge(hT_ready, i + 1)
                                for n in range(EP):
                                    pe.wait_ge(y_add, EP * i + n + 1)
                                    for k in range(KH):
                                        mm = pe.matmul(psY[:, n % NB2, :], hT[:, k, :], W2[:, k, 2 * n:2 * n + 2, :],
                                                       start=k == 0, stop=k == KH - 1)
                                    mm.then_inc(y_mm, 1)

                        @block.scalar
                        def _(act):
                            with act.Fori(0, TT) as i:
                                act.wait_ge(dwT_mm, i)
                                act.activation(dw3[:, :], dw[:, i, 2, :], ACT.Copy).then_inc(dw3_ready, 1)
                                act.wait_ge(hT_ready, i)
                                act.activation(hg[:, :], h[:, i, :], ACT.Gelu).then_inc(hg_ready, 1)
                                act.wait_ge(hT_mm, i + 1)
                                act.wait_ge(y_mm, EP * i)
                                act.activation(hT[:, :, :].rearrange("p k n -> p (k n)"), psT[:, :], ACT.Copy
                                               ).then_inc(hT_ready, 1)
                                act.wait_ge(dwT_mm, i + 1)
                                act.activation(dwT[:, :], psB[0:E1, 0:P], ACT.Copy).then_inc(dwT_ready, 1)

                        @block.vector
                        def _(dve):
                            dve.sem_inc(y_add, NB2)
                            ych = Chain(dve, sem("f_y_step"), 1 + E1)
                            with dve.Fori(0, TT) as i:
                                ych.turn(i)
                                dve.wait_ge(b_mm, i + 1)
                                ych.step(dve.tensor_tensor(Xf[:, i, :], psB[:, P:P + D], Xf[:, i, :], ALU.add))
                                dve.sem_inc(b_add, 1)
                                for n in range(EP):
                                    dve.wait_ge(y_mm, EP * i + n + 1)
                                    for v in range(2):
                                        ych.step(dve.scalar_tensor_tensor(
                                            Xf[:, i, :], psY[:, n % NB2, v * D:(v + 1) * D],
                                            dw[:, i, 1, 2 * n + v:2 * n + v + 1], Xf[:, i, :], ALU.mult, ALU.add))
                                    dve.sem_inc(y_add, 1)
                                ych.end()

        attention("a0_", t["a0_WqT"], t["a0_WkT"], t["a0_WvT"], t["a0_WoT"], t["a0_bq"], t["a0_bk"], t["a0_bv"],
                  t["a0_bo"], True)
        soft_mixture()
        attention("a1_", t["a1_Wq"], t["a1_Wk"], t["a1_Wv"], t["a1_Wo"], t["a1_bq"], t["a1_bk"], t["a1_bv"],
                  t["a1_bo"], False)
        top3_mixture()
        stored = sem("stored")
        with nc.Block() as block:
            @block.sync
            def _(sp):
                for b in range(B):
                    sp.dma_start(out[b].rearrange("(t p) d -> p t d", p=P), X[:, b]).then_inc(stored, 16)
                sp.wait_ge(stored, 16 * B)


def kernel(**inputs):
    import numpy as np
    import concourse.bacc as bacc
    from concourse.bass_utils import run_bass_kernel_spmd

    def flip(a):
        return np.ascontiguousarray(np.swapaxes(np.asarray(a), -1, -2))

    def keep(a):
        return np.ascontiguousarray(np.asarray(a))

    def columns(a):
        return flip(np.asarray(a).reshape(-1, P))

    def hidden(a):
        return keep(np.asarray(a).reshape(E0, KF, P).transpose(2, 0, 1))

    flat = np.arange(FLAT)
    hmv = np.zeros((P, NCH, VH), np.float32)
    for c in range(NCH):
        for v in range(VH):
            hmv[:CHR[c], c, v] = (flat[c * P:c * P + CHR[c]] // S2 == H0[c] + v)
    arrays = {
        "x": keep(inputs["x"]),
        "ctxT": flip(np.asarray(inputs["ctx_1024"]).reshape(B * S2, D)),
        "mask": keep(inputs["mask_1x1xSxS2_ik0"]),
        "a0_WqT": flip(inputs["L0_xattn_Wq"]), "a0_WkT": flip(inputs["L0_xattn_Wk"]),
        "a0_WvT": flip(inputs["L0_xattn_Wv"]), "a0_WoT": flip(inputs["L0_xattn_Wo"]),
        "a0_bq": columns(inputs["L0_xattn_bq"]), "a0_bk": columns(inputs["L0_xattn_bk"]),
        "a0_bv": keep(inputs["L0_xattn_bv"]), "a0_bo": keep(inputs["L0_xattn_bo"]),
        "a1_Wq": keep(inputs["L1_xattn_Wq"]), "a1_Wk": keep(inputs["L1_xattn_Wkv"][:, :D]),
        "a1_Wv": keep(inputs["L1_xattn_Wkv"][:, D:]), "a1_Wo": keep(inputs["L1_xattn_Wproj"]),
        "a1_bq": columns(inputs["L1_xattn_bq"]), "a1_bk": columns(inputs["L1_xattn_bkv"][:D]),
        "a1_bv": keep(inputs["L1_xattn_bkv"][D:]), "a1_bo": keep(inputs["L1_xattn_bproj"]),
        "m_ng": keep(inputs["L0_ffn_norm_g"]), "m_nb": keep(inputs["L0_ffn_norm_b"]),
        "m_sg": keep(inputs["L0_ffn_slot_g"]), "m_sb": keep(inputs["L0_ffn_slot_b"]),
        "m_scale": keep(inputs["L0_ffn_scale"]),
        "m_se": keep(np.asarray(inputs["L0_ffn_slot_embeds"]).reshape(NS, D)),
        "m_Wg": keep(inputs["L0_ffn_Wg"]), "m_Wu": keep(inputs["L0_ffn_Wu"]), "m_Wd": keep(inputs["L0_ffn_Wd"]),
        "m_bgT": hidden(inputs["L0_ffn_bg"]), "m_buT": hidden(inputs["L0_ffn_bu"]), "m_bd": keep(inputs["L0_ffn_bd"]),
        "f_PwT": flip(inputs["L1_ffn_P_w"]),
        "f_UT": flip(np.concatenate([np.asarray(inputs["L1_ffn_U%d" % i]) for i in (1, 2, 3)])),
        "f_W1T": flip(inputs["L1_ffn_W1"]),
        "f_W2T": keep(np.asarray(inputs["L1_ffn_W2"]).reshape(E1, D, KH, P).transpose(2, 3, 0, 1)),
        "f_b2": keep(inputs["L1_ffn_b2"]),
        "c_iota": np.arange(E1, dtype=np.float32),
        "c_ident": np.eye(P, dtype=np.float32),
        "c_sel": (flat[None, :] % S2 == np.arange(S2)[:, None]).astype(np.float32),
        "c_hmk": (np.arange(P)[:, None] // DK == np.arange(HC)[None, :]).astype(np.float32),
        "c_hmv": hmv.reshape(P, NCH * VH),
    }
    nc = bacc.Bacc("TRN2", target_bir_lowering=False, num_devices=1)
    aps = {n: nc.dram_tensor("in_" + n, a.shape, mybir.dt.from_np(a.dtype), kind="ExternalInput").ap()
           for n, a in arrays.items()}
    out = nc.dram_tensor("out", (B, N, D), F32, kind="ExternalOutput").ap()
    build(nc, aps, out)
    r = run_bass_kernel_spmd(nc, [{"in_" + n: a for n, a in arrays.items()}], core_ids=[0])
    return r.results[0]["out"]
```

```python
from contextlib import ExitStack, contextmanager

import concourse.bass as bass
from concourse import mybir

ALU = mybir.AluOpType
ACT = mybir.ActivationFunctionType
AX = mybir.AxisListType
F32 = mybir.dt.float32
I32 = mybir.dt.int32
U32 = mybir.dt.uint32

P = 128
B = 2
N = 1024
D = 256
KD = D // P
NT = N // P
S2 = 77
H = 16
DK = D // H
HC = H // KD
HG = 4
NG = H // HG
FLAT = H * S2
NCH = -(-FLAT // P)
CHR = [min(P, FLAT - c * P) for c in range(NCH)]
VH = 3
VC = DK + 1
H0 = [min(c * P // S2, H - VH) for c in range(NCH)]
PTG = [range(0, 4), range(4, 8), range(8, NCH)]
E0, SL, F0 = 16, 64, 512
NS = E0 * SL
CS = NS // P
KF = F0 // P
E1, HID = 12, 1024
TOP = 3
LT = (B * N * TOP + E1 * (P - 1)) // P
R = 3
DA = 64
KH = HID // P
RING = 4
GR = 4
BANK = 512
SCALE = 0.25
NEG = -1.0e9
BIG = 3.0e38


def wait(eng, sem, value):
    if isinstance(value, int) and value <= 0:
        return
    eng.wait_ge(sem, value)


def before(j, s, n):
    return (j, s - n) if s >= n else (j - 1, s - n + 2)


def after(j, s, n):
    return (j, s + n) if s + n < 2 else (j + 1, s + n - 2)


def pair_steps(eng, pairs, step):
    for s in range(2):
        step(0, s, s >= 1, True, True)
    with eng.Fori(1, pairs - 1) as j:
        for s in range(2):
            step(j, s, True, True, True)
    for s in range(2):
        step(pairs - 1, s, True, s == 0, False)


class Chain:

    def __init__(self, eng, sem, per_turn):
        self.eng, self.sem, self.per_turn = eng, sem, per_turn

    def turn(self, i):
        self.base, self.n = i * self.per_turn, 0

    def step(self, ins, hold=True):
        ins.then_inc(self.sem, 1)
        self.n += 1
        if hold:
            self.eng.wait_ge(self.sem, self.base + self.n)

    def hold(self):
        self.eng.wait_ge(self.sem, self.base + self.n)

    def end(self):
        assert self.n == self.per_turn, (self.n, self.per_turn)


def build(nc, t, out):
    xn_d = nc.dram_tensor("xn_d", (B * N, D), F32, kind="Internal").ap()
    p1_rows = nc.dram_tensor("p1_d", (LT * P, HID), F32, kind="Internal").ap()
    p1_d = p1_rows.rearrange("(i p) h -> i p h", p=P)
    h_rows = nc.dram_tensor("h_d", (B * N, HID), F32, kind="Internal").ap()
    h_d = h_rows.rearrange("(i p) h -> i p h", p=P)
    p2_rows = nc.dram_tensor("p2_d", (B * N * TOP + LT * P, D), F32, kind="Internal").ap()
    p2_d = p2_rows[0:B * N * TOP, :].rearrange("(k i p) d -> i p k d", k=TOP, p=P)
    out_tiles = out.rearrange("b (t p) d -> (b t) p d", p=P)
    ctx = ExitStack()

    def sb(stack, name, shape, dt=F32):
        return stack.enter_context(nc.sbuf_tensor(name, shape, dt))

    def ps(stack, name, shape):
        return stack.enter_context(nc.psum_tensor(name, shape, F32))

    scopes = [(ctx, [])]

    def sem(name):
        stack, names = scopes[-1]
        names.append(stack.enter_context(nc.semaphore(name)))
        return names[-1]

    @contextmanager
    def stage():
        scopes.append((ExitStack(), []))
        yield
        stack, names = scopes.pop()
        with nc.Block() as block:
            @block.sync
            def _(sp):
                for n in names:
                    sp.sem_clear(n)
        stack.close()

    with ctx:
        X = sb(ctx, "X", [P, B, NT, D])
        ident = sb(ctx, "ident", [P, P])
        ones = sb(ctx, "ones", [1, P])
        ctxT = sb(ctx, "ctxT", [P, KD, B * S2])
        sel = sb(ctx, "sel", [P, FLAT])
        hmk = sb(ctx, "hmk", [P, HC])
        hmv = sb(ctx, "hmv", [P, NCH * VH])

        def attention_weights(stack, a):
            w = sb(stack, a + "W", [P, 4, KD, D])
            return [w] + [w[:, i] for i in range(4)] + [sb(stack, a + n, [P, KD]) for n in ("bk", "bq")]

        loaded_x = sem("loaded_x")
        loaded_const = sem("loaded_const")
        loaded_se = sem("loaded_se")
        loaded_att = [sem("loaded_a0"), sem("loaded_a1")]
        ones_ready = sem("ones_ready")
        N_CONST, N_SE, N_ATT = 5, 6, 6
        a1_weights = attention_weights(ctx, "a1_")
        TT = B * NT
        stats = sb(ctx, "stats", [P, TT, 6])
        mean = sb(ctx, "mean", [P, TT])
        mdif = sb(ctx, "mdif", [P, TT])
        rstd = sb(ctx, "rstd", [P, TT])
        veps = sb(ctx, "veps", [P, TT])
        mhalf = sb(ctx, "mhalf", [P, TT])
        vars_ = sb(ctx, "vars", [P, TT])
        slots = ExitStack()
        seT = sb(slots, "m_seT", [P, KD, NS])
        gains = sb(slots, "m_gains", [P, 2, D])
        a0_st = ExitStack()
        att = [attention_weights(a0_st, "a0_"), a1_weights]
        se_st = ExitStack()
        sgains = sb(se_st, "m_sgains", [P, 2, D])
        SE = sb(se_st, "m_SE", [P, CS, D])
        scl = sb(se_st, "m_scl", [P, 1])

        with nc.Block() as block:
            @block.sync
            def _(sp):
                def attention_loads(l):
                    a = f"a{l}_"
                    T = "T" if l == 0 else ""
                    for w, n in zip(att[l][1:5], ("Wk", "Wv", "Wq", "Wo")):
                        sp.dma_start(w[:, :, :], t[a + n + T].rearrange("(k p) n -> p k n", p=P)).then_inc(loaded_att[l], 16)
                    for w, n in zip(att[l][5:7], ("bk", "bq")):
                        sp.dma_start(w[:, :], t[a + n]).then_inc(loaded_att[l], 16)

                sp.dma_start(ctxT[:, :, :], t["ctxT"].rearrange("(k p) n -> p k n", p=P)).then_inc(loaded_const, 16)
                sp.dma_start(sel[0:S2, :], t["c_sel"]).then_inc(loaded_const, 16)
                sp.dma_start(hmk[:, :], t["c_hmk"]).then_inc(loaded_const, 16)
                sp.dma_start(hmv[:, :], t["c_hmv"]).then_inc(loaded_const, 16)
                sp.dma_start(ident[:, :], t["c_ident"]).then_inc(loaded_const, 16)
                attention_loads(0)
                attention_loads(1)

            @block.scalar
            def _(act):
                act.dma_start(SE[:, :, :], t["m_se"].rearrange("(c p) d -> p c d", p=P)).then_inc(loaded_se, 16)
                for place, n in zip((sgains[:, 0], sgains[:, 1], gains[:, 0], gains[:, 1]), ("m_sg", "m_sb", "m_ng", "m_nb")):
                    act.dma_start(place, t[n].partition_broadcast(P)).then_inc(loaded_se, 16)
                act.dma_start(scl[:, :], t["m_scale"].partition_broadcast(P)).then_inc(loaded_se, 16)
                for b in range(B):
                    act.dma_start(X[:, b], t["x"][b].rearrange("(t p) d -> p t d", p=P)).then_inc(loaded_x, 16)

            @block.vector
            def _(dve):
                nc.vector.memset(ones[:, :], 1.0).then_inc(ones_ready, 1)
                dve.wait_ge(ones_ready, 1)

        def bn_tiles(dve, rows, n, done):
            with dve.Fori(0, n // 4) as q:
                for i in range(4):
                    dve.bn_stats(stats[:, q * 4 + i, :], rows[:, q * 4 + i, :]).then_inc(done, 1)
            dve.wait_ge(done, n)

        def norm_factors(a, n, twice=False):
            var = sem(a + "var")
            inv = sem(a + "inv")

            def begin(dve):
                me, ve, mo, vo = (stats[:, 0:n, i] for i in (1, 2, 4, 5))
                dve.memset(mhalf[:, 0:n], -0.5).then_inc(var, 1)
                dve.tensor_tensor(mean[:, 0:n], me, mo, ALU.add).then_inc(var, 1)
                dve.tensor_tensor(mdif[:, 0:n], me, mo, ALU.subtract).then_inc(var, 1)
                dve.tensor_tensor(veps[:, 0:n], ve, vo, ALU.add).then_inc(var, 1)
                dve.wait_ge(var, 4)
                dve.tensor_scalar(mean[:, 0:n], mean[:, 0:n], 0.5, None, ALU.mult).then_inc(var, 1)
                dve.scalar_tensor_tensor(mdif[:, 0:n], mdif[:, 0:n], 0.25, mdif[:, 0:n], ALU.mult, ALU.mult
                                         ).then_inc(var, 1)
                dve.wait_ge(var, 6)
                dve.scalar_tensor_tensor(vars_[:, 0:n], veps[:, 0:n], 1.0 / D, mdif[:, 0:n], ALU.mult, ALU.add
                                         ).then_inc(var, 1)
                dve.wait_ge(var, 7)
                dve.tensor_scalar(veps[:, 0:n], vars_[:, 0:n], 1e-5, None, ALU.add).then_inc(var, 1)

            def end(dve):
                dve.wait_ge(inv, 1)
                if twice:
                    dve.tensor_tensor(veps[:, 0:n], rstd[:, 0:n], rstd[:, 0:n], ALU.mult).then_inc(var, 1)
                    dve.wait_ge(var, 9)
                    dve.tensor_tensor(veps[:, 0:n], veps[:, 0:n], vars_[:, 0:n], ALU.mult).then_inc(var, 1)
                    dve.wait_ge(var, 10)
                    dve.tensor_scalar(veps[:, 0:n], veps[:, 0:n], 1e-5, None, ALU.add).then_inc(var, 1)
                    dve.wait_ge(inv, 2)
                    dve.tensor_tensor(rstd[:, 0:n], rstd[:, 0:n], veps[:, 0:n], ALU.mult).then_inc(var, 1)
                    dve.wait_ge(var, 12)

            def power(pool):
                pool.wait_ge(var, 8)
                pool.tensor_tensor(rstd[:, 0:n], veps[:, 0:n], mhalf[:, 0:n], ALU.pow).then_inc(inv, 1)
                if twice:
                    pool.wait_ge(var, 11)
                    pool.tensor_tensor(veps[:, 0:n], veps[:, 0:n], mhalf[:, 0:n], ALU.pow).then_inc(inv, 1)

            return begin, end, power

        with se_st, stage():
            seps = ExitStack()
            with seps:
                psSE = ps(seps, "m_psSE", [P, KD, NS])
                begin, end, power = norm_factors("ms_", CS)
                se_stat = sem("m_se_stat")
                x_stat = sem("x_stat")
                se_step = sem("m_se_step")
                se_ready = sem("m_se_ready")
                se_mm = sem("m_se_mm")
                seT_ready = sem("m_seT_ready")
                with nc.Block() as block:
                    @block.vector
                    def _(dve):
                        dve.wait_ge(loaded_se, 16 * N_SE)
                        bn_tiles(dve, SE, CS, se_stat)
                        begin(dve)
                        for i in range(2):
                            dve.tensor_scalar(sgains[:, i, :], sgains[:, i, :], scl[:, :], None, ALU.mult).then_inc(se_step, 1)
                        end(dve)
                        for c in range(CS):
                            dve.tensor_scalar(SE[:, c], SE[:, c], mean[:, c:c + 1], rstd[:, c:c + 1],
                                              ALU.subtract, ALU.mult).then_inc(se_step, 1)
                        dve.wait_ge(se_step, 2 + CS)
                        dve.tensor_tensor(SE[:, :, :], SE[:, :, :], sgains[:, 0:1, :].to_broadcast([P, CS, D]),
                                          ALU.mult).then_inc(se_step, 1)
                        dve.wait_ge(se_step, 2 + CS + 1)
                        dve.tensor_tensor(SE[:, :, :], SE[:, :, :], sgains[:, 1:2, :].to_broadcast([P, CS, D]),
                                          ALU.add).then_inc(se_ready, 1)
                        dve.wait_ge(loaded_x, 16 * B)
                        bn_tiles(dve, X[:, :, :, :].rearrange("p b t d -> p (b t) d"), TT, x_stat)

                    @block.gpsimd
                    def _(pool):
                        power(pool)

                    @block.tensor
                    def _(pe):
                        pe.wait_ge(loaded_const, 16 * N_CONST)
                        pe.wait_ge(se_ready, 1)
                        for k in range(KD):
                            for c in range(CS):
                                mm = pe.transpose(psSE[:, k, c * P:(c + 1) * P], SE[:, c, k * P:(k + 1) * P],
                                                  ident[:, :])
                        mm.then_inc(se_mm, 1)

                    @block.scalar
                    def _(act):
                        act.wait_ge(se_mm, 1)
                        for k in range(KD):
                            act.activation(seT[:, k, :], psSE[:, k, :], ACT.Copy).then_inc(seT_ready, 1)
                        act.wait_ge(seT_ready, KD)

        def attention(a, layer, masked, prefetch=None):
            _, Wk, Wv, Wq, Wo, bkc, bqc = att[layer]
            st = ExitStack()
            with st:
                bvr = sb(st, a + "bvr", [1, D])
                bob = sb(st, a + "bob", [P, D])
                kT = sb(st, a + "kT", [P, KD, B * S2])
                kblk = sb(st, a + "kblk", [P, B, KD, HC, S2])
                vsb = sb(st, a + "vsb", [P, B, H, VC])
                vblk = sb(st, a + "vblk", [P, B, NCH, VH * VC])
                xn = sb(st, a + "xn", [P, B, D])
                xnT = sb(st, a + "xnT", [P, B, KD, P])
                qT = sb(st, a + "qT", [P, B, KD, P])
                sc = sb(st, a + "sc", [P, B, H, S2])
                pr = sb(st, a + "pr", [P, B, FLAT])
                mx = sb(st, a + "mx", [P, B, H])
                rsum = sb(st, a + "rsum", [P, B, H])
                pT = sb(st, a + "pT", [P, B, NCH, P])
                o = sb(st, a + "o", [P, B, H, DK])
                oT = sb(st, a + "oT", [P, B, KD, P])
                if masked:
                    mi = sb(st, a + "mi", [P, NT, S2], I32)
                    cap = sb(st, a + "cap", [P, NT, S2])
                psS = ps(st, a + "psS", [P, NG, BANK])
                psA = ps(st, a + "psA", [P, 2, 2 * P])
                psP = ps(st, a + "psP", [P, 2, BANK])
                psO = ps(st, a + "psO", [P, BANK])

                mask_ld = sem(a + "mask_ld")
                bias_ld = sem(a + "bias_ld")
                kv_mm = sem(a + "kv_mm")
                kv_sb = sem(a + "kv_sb")
                kv_blk = sem(a + "kv_blk")
                cap_step = sem(a + "cap_step")

                begin, end, power = norm_factors(a, TT)
                with nc.Block() as block:
                    @block.sync
                    def _(sp):
                        sp.dma_start(bvr[:, :], t[a + "bv"].rearrange("(a d) -> a d", a=1)).then_inc(bias_ld, 16)
                        sp.dma_start(bob[:, :], t[a + "bo"].partition_broadcast(P)).then_inc(bias_ld, 16)
                        if masked:
                            sp.dma_start(mi[:, :, :], t["mask"].rearrange("a b (t p) k -> p (a b t) k", p=P)
                                         ).then_inc(mask_ld, 16)
                        if prefetch is not None:
                            prefetch(sp)

                    @block.tensor
                    def _(pe):
                        pe.wait_ge(loaded_const, 16 * N_CONST)
                        pe.wait_ge(loaded_att[layer], 16 * N_ATT)
                        pe.wait_ge(bias_ld, 32)
                        for m in range(KD):
                            for k in range(KD):
                                mm = pe.matmul(psA[:, m, 0:B * S2], Wk[:, k, m * P:(m + 1) * P], ctxT[:, k, :],
                                               start=k == 0, stop=k == KD - 1)
                        mm.then_inc(kv_mm, 1)
                        for b in range(B):
                            for k in range(KD):
                                pe.matmul(psS[0:S2, b, 0:D], ctxT[:, k, b * S2:(b + 1) * S2], Wv[:, k, :],
                                          start=k == 0, stop=False)
                            mm = pe.matmul(psS[0:S2, b, 0:D], ones[0:1, 0:S2], bvr[:, :], start=False, stop=True)
                        mm.then_inc(kv_mm, 1)
                        pe.wait_ge(kv_sb, 4 + B)
                        for b in range(B):
                            for c in range(NCH):
                                mm = pe.matmul(psP[0:CHR[c], b, c * VH * VC:(c + 1) * VH * VC],
                                               sel[0:S2, c * P:c * P + CHR[c]],
                                               vsb[0:S2, b, H0[c]:H0[c] + VH, :], start=True, stop=True)
                        mm.then_inc(kv_mm, 1)

                    @block.vector
                    def _(dve):
                        begin(dve)
                        dve.wait_ge(loaded_const, 16 * N_CONST)
                        dve.wait_ge(loaded_att[layer], 16 * N_ATT)
                        if masked:
                            dve.wait_ge(mask_ld, 16)
                            dve.tensor_scalar(cap[:, :, :], mi[:, :, :], 0, BIG, ALU.not_equal, ALU.mult
                                              ).then_inc(cap_step, 1)
                            dve.wait_ge(cap_step, 1)
                            dve.tensor_scalar(cap[:, :, :], cap[:, :, :], NEG, None, ALU.add).then_inc(cap_step, 1)
                            dve.wait_ge(cap_step, 2)
                        dve.memset(vsb[:, :, :, DK:VC], 1.0).then_inc(kv_sb, 1)
                        dve.memset(vblk[:, :, NCH - 1, :], 0.0).then_inc(kv_sb, 1)
                        dve.wait_ge(kv_mm, 1)
                        for m in range(KD):
                            dve.tensor_scalar(kT[:, m, :], psA[:, m, 0:B * S2], bkc[:, m:m + 1], SCALE,
                                              ALU.add, ALU.mult).then_inc(kv_sb, 1)
                        dve.wait_ge(kv_mm, 2)
                        for b in range(B):
                            dve.tensor_copy(vsb[0:S2, b, :, 0:DK],
                                            psS[0:S2, b, 0:D].rearrange("p (h d) -> p h d", h=H)).then_inc(kv_sb, 1)
                        dve.wait_ge(kv_sb, 4 + B)
                        for b in range(B):
                            for m in range(KD):
                                dve.tensor_tensor(
                                    kblk[:, b, m], kT[:, m:m + 1, b * S2:(b + 1) * S2].to_broadcast([P, HC, S2]),
                                    hmk[:, :].unsqueeze(2).to_broadcast([P, HC, S2]), ALU.mult).then_inc(kv_blk, 1)
                        dve.wait_ge(kv_mm, 3)
                        for b in range(B):
                            for rows, c0, c1 in ((P, 0, NCH - 1), (CHR[-1], NCH - 1, NCH)):
                                n = (c1 - c0) * VH
                                dve.tensor_tensor(
                                    vblk[0:rows, b, c0:c1, :].rearrange("p c (h v) -> p (c h) v", v=VC),
                                    psP[0:rows, b, c0 * VH * VC:c1 * VH * VC].rearrange("p (n v) -> p n v", v=VC),
                                    hmv[0:rows, c0 * VH:c1 * VH].unsqueeze(2).to_broadcast([rows, n, VC]),
                                    ALU.mult).then_inc(kv_blk, 1)
                        dve.wait_ge(kv_blk, 4 * B)
                        end(dve)

                    @block.gpsimd
                    def _(pool):
                        power(pool)

                xn_ready = sem(a + "xn_ready")
                xT_mm = sem(a + "xT_mm")
                xT_ready = sem(a + "xT_ready")
                q_mm = sem(a + "q_mm")
                q_ready = sem(a + "q_ready")
                s_mm = sem(a + "s_mm")
                s_read = sem(a + "s_read")
                s_ready = sem(a + "s_ready")
                p_ready = sem(a + "p_ready")
                pT_mm = sem(a + "pT_mm")
                pT_ready = sem(a + "pT_ready")
                pv_mm = sem(a + "pv_mm")
                o_ready = sem(a + "o_ready")
                y_mm = sem(a + "y_mm")
                y_done = sem(a + "y_done")
                front_step = sem(a + "front_step")
                back_step = sem(a + "back_step")
                oT_mm = sem(a + "oT_mm")
                oT_ready = sem(a + "oT_ready")
                stat_done = sem(a + "stat_done")
                xb_ready = sem(a + "xb_ready")

                with nc.Block() as block:
                    def steps(eng, step):
                        for j in range(2):
                            for s in range(B):
                                step(j, s, B * j + s >= 1, j >= 1, True, True)
                        with eng.Fori(2, NT - 1) as j:
                            for s in range(B):
                                step(j, s, True, True, True, True)
                        for s in range(B):
                            step(NT - 1, s, True, True, s < B - 1, False)

                    @block.vector
                    def _(dve):
                        front = Chain(dve, front_step, 3 if masked else 2)
                        back = Chain(dve, back_step, 1)

                        def norm_in(j, s, u):
                            i = s * NT + j
                            wait(dve, xT_mm, u - 1)
                            dve.tensor_scalar(xn[:, s], X[:, s, j], mean[:, bass.ds(i, 1)], rstd[:, bass.ds(i, 1)],
                                              ALU.subtract, ALU.mult).then_inc(xn_ready, 1)

                        def softmax_in(j, s, u):
                            front.turn(u)
                            dve.wait_ge(s_mm, u + 1)
                            raw = psS[:, :, 0:HG * S2].rearrange("p g (h k) -> p g h k", h=HG)
                            rs = sc[:, s].rearrange("p (g h) k -> p g h k", g=NG)
                            wait(dve, p_ready, u - 1)
                            src = raw
                            if masked:
                                for g in range(NG):
                                    ins = dve.tensor_tensor(rs[:, g], raw[:, g],
                                                            cap[:, j].unsqueeze(1).to_broadcast([P, HG, S2]), ALU.min)
                                front.step(ins)
                                dve.sem_inc(s_read, 1)
                                src = rs
                            front.step(dve.tensor_reduce(mx[:, s].rearrange("p (g h) -> p g h", g=NG), src,
                                                         AX.X, ALU.max))
                            ins = dve.tensor_tensor(
                                rs, src, mx[:, s].rearrange("p (g h) -> p g h", g=NG).unsqueeze(3)
                                .to_broadcast([P, NG, HG, S2]), ALU.subtract)
                            front.step(ins)
                            if not masked:
                                dve.sem_inc(s_read, 1)
                            dve.sem_inc(s_ready, 1)

                        def normalise(j, s, u):
                            back.turn(u)
                            dve.wait_ge(pv_mm, u + 1)
                            acc = psO[:, 0:H * VC].rearrange("p (h v) -> p h v", v=VC)
                            wait(dve, o_ready, u - 1)
                            back.step(dve.reciprocal(rsum[:, s, :].unsqueeze(2), acc[:, :, DK:VC]))
                            wait(dve, oT_mm, u - 1)
                            dve.tensor_tensor(o[:, s], acc[:, :, 0:DK],
                                              rsum[:, s, :].unsqueeze(2).to_broadcast([P, H, DK]), ALU.mult
                                              ).then_inc(o_ready, 1)

                        def residual(j, s, u):
                            dve.wait_ge(y_mm, u + 1)
                            dve.wait_ge(xb_ready, u + 1)
                            dve.tensor_tensor(X[:, s, j], psO[:, 0:D], X[:, s, j], ALU.add).then_inc(y_done, 1)

                        def stat(j, s, u):
                            dve.wait_ge(y_done, u + 1)
                            dve.bn_stats(stats[:, s * NT + j, :], X[:, s, j]).then_inc(stat_done, 1)

                        def step(j, s, v, w, n, a):
                            u = B * j + s
                            softmax_in(j, s, u)
                            if v:
                                normalise(*before(j, s, 1), u - 1)
                            if a:
                                norm_in(*after(j, s, 2), u + 2)
                            if w:
                                residual(*before(j, s, 2), u - 2)
                                stat(*before(j, s, 2), u - 2)

                        for s in range(B):
                            norm_in(0, s, s)
                        steps(dve, step)
                        U = B * NT
                        normalise(NT - 1, B - 1, U - 1)
                        for s in range(B):
                            residual(NT - 1, s, U - B + s)
                            stat(NT - 1, s, U - B + s)
                        dve.wait_ge(stat_done, U)

                    @block.gpsimd
                    def _(pool):
                        with pool.Fori(0, NT) as j:
                            for s in range(B):
                                pool.wait_ge(xn_ready, B * j + s + 1)
                                pool.tensor_tensor(X[:, s, j], X[:, s, j], bob[:, :], ALU.add).then_inc(xb_ready, 1)

                    @block.scalar
                    def _(act):
                        def input_T(j, s, u):
                            act.wait_ge(xT_mm, u + 1)
                            wait(act, q_mm, u - 1)
                            act.activation(xnT[:, s].rearrange("p k n -> p (k n)"), psA[:, 0, :], ACT.Copy
                                           ).then_inc(xT_ready, 1)

                        def queries(j, s, u):
                            act.wait_ge(q_mm, u + 1)
                            wait(act, s_mm, u - 1)
                            for m in range(KD):
                                ins = act.activation(qT[:, s, m, :], psA[:, 1, m * P:(m + 1) * P], ACT.Identity,
                                                     bias=bqc[:, m:m + 1])
                            ins.then_inc(q_ready, 1)

                        def exponent(j, s, u):
                            act.wait_ge(s_ready, u + 1)
                            wait(act, pT_mm, 3 * (u - 1))
                            act.activation(pr[:, s, :], sc[:, s].rearrange("p h k -> p (h k)"), ACT.Exp
                                           ).then_inc(p_ready, 1)

                        def probs_T(j, s, u, g):
                            cs = PTG[g]
                            act.wait_ge(pT_mm, 3 * u + g + 1)
                            wait(act, pv_mm, u - 1)
                            full = [c for c in cs if CHR[c] == P]
                            act.activation(pT[:, s, full[0]:full[-1] + 1, :].rearrange("p c n -> p (c n)"),
                                           psP[:, g % 2 if g < 2 else 1, 0:len(full) * P], ACT.Copy).then_inc(pT_ready, 1)
                            for c in cs:
                                if CHR[c] < P:
                                    act.activation(pT[0:CHR[c], s, c, :],
                                                   psP[0:CHR[c], 1, (c - cs[0]) * P:(c - cs[0] + 1) * P],
                                                   ACT.Copy).then_inc(pT_ready, 1)

                        def output_T(j, s, u):
                            act.wait_ge(oT_mm, u + 1)
                            wait(act, y_mm, u - 1)
                            act.activation(oT[:, s].rearrange("p k n -> p (k n)"), psP[:, 0, 0:KD * P], ACT.Copy
                                           ).then_inc(oT_ready, 1)

                        def step(j, s, v, w, n, a):
                            u = B * j + s
                            if v:
                                probs_T(*before(j, s, 1), u - 1, 0)
                                probs_T(*before(j, s, 1), u - 1, 1)
                            if n:
                                input_T(*after(j, s, 1), u + 1)
                            if w:
                                output_T(*before(j, s, 2), u - 2)
                            if v:
                                probs_T(*before(j, s, 1), u - 1, 2)
                            if n:
                                queries(*after(j, s, 1), u + 1)
                            exponent(j, s, u)

                        input_T(0, 0, 0)
                        queries(0, 0, 0)
                        steps(act, step)
                        U = B * NT
                        probs_T(NT - 1, B - 1, U - 1, 0)
                        probs_T(NT - 1, B - 1, U - 1, 1)
                        output_T(NT - 1, 0, U - 2)
                        probs_T(NT - 1, B - 1, U - 1, 2)
                        output_T(NT - 1, B - 1, U - 1)

                    @block.tensor
                    def _(pe):
                        EV = [1, 2, 4]

                        def input_T(j, s, u):
                            pe.wait_ge(xn_ready, u + 1)
                            wait(pe, q_ready, u)
                            for k in range(KD):
                                mm = pe.transpose(psA[:, 0, k * P:(k + 1) * P], xn[:, s, k * P:(k + 1) * P], ident[:, :])
                            mm.then_inc(xT_mm, 1)

                        def queries(j, s, u):
                            pe.wait_ge(xT_ready, u + 1)
                            for m in range(KD):
                                for k in range(KD):
                                    mm = pe.matmul(psA[:, 1, m * P:(m + 1) * P], Wq[:, k, m * P:(m + 1) * P],
                                                   xnT[:, s, k, :], start=k == 0, stop=k == KD - 1)
                            mm.then_inc(q_mm, 1)

                        def scores(j, s, u):
                            pe.wait_ge(q_ready, u + 1)
                            wait(pe, s_read, u)
                            for g in range(NG):
                                m, h = divmod(g * HG, HC)
                                mm = pe.matmul(psS[:, g, 0:HG * S2], qT[:, s, m, :], kblk[:, s, m, h:h + HG, :],
                                               start=True, stop=True)
                            mm.then_inc(s_mm, 1)

                        def probs_T(j, s, u, g):
                            if g == 0:
                                pe.wait_ge(p_ready, u + 1)
                                wait(pe, oT_ready, u - 1)
                            if g == 1:
                                wait(pe, pT_ready, 4 * u)
                            if g == 2:
                                pe.wait_ge(pT_ready, 4 * u + EV[1])
                            cs = PTG[g]
                            for c in cs:
                                mm = pe.transpose(psP[0:CHR[c], g if g < 2 else 1, (c - cs[0]) * P:(c - cs[0] + 1) * P],
                                                  pr[:, s, c * P:c * P + CHR[c]], ident[:, :])
                            mm.then_inc(pT_mm, 1)

                        def values(j, s, u):
                            wait(pe, y_done, u - 1)
                            for g, cs in enumerate(PTG):
                                pe.wait_ge(pT_ready, 4 * u + EV[g])
                                for c in cs:
                                    mm = pe.matmul(psO[:, H0[c] * VC:(H0[c] + VH) * VC], pT[0:CHR[c], s, c, :],
                                                   vblk[0:CHR[c], s, c, :], start=c == 0, stop=c == NCH - 1,
                                                   skip_group_check=True)
                            mm.then_inc(pv_mm, 1)

                        def output_T(j, s, u, ev):
                            pe.wait_ge(o_ready, u + 1)
                            pe.wait_ge(pT_ready, ev)
                            for k in range(KD):
                                mm = pe.transpose(psP[:, 0, k * P:(k + 1) * P], o[:, s, k * HC:(k + 1) * HC, :],
                                                  ident[:, :])
                            mm.then_inc(oT_mm, 1)

                        def project(j, s, u, o_read):
                            pe.wait_ge(oT_ready, u + 1)
                            pe.wait_ge(o_ready, o_read)
                            for k in range(KD):
                                mm = pe.matmul(psO[:, 0:D], oT[:, s, k, :], Wo[:, k, :], start=k == 0, stop=k == KD - 1)
                            mm.then_inc(y_mm, 1)

                        def step(j, s, v, w, n, a):
                            u = B * j + s
                            scores(j, s, u)
                            if v:
                                probs_T(*before(j, s, 1), u - 1, 0)
                                probs_T(*before(j, s, 1), u - 1, 1)
                            if n:
                                input_T(*after(j, s, 1), u + 1)
                            if w:
                                output_T(*before(j, s, 2), u - 2, 4 * (u - 1) + EV[0])
                            if v:
                                probs_T(*before(j, s, 1), u - 1, 2)
                                values(*before(j, s, 1), u - 1)
                            if n:
                                queries(*after(j, s, 1), u + 1)
                            if w:
                                project(*before(j, s, 2), u - 2, u)

                        input_T(0, 0, 0)
                        queries(0, 0, 0)
                        steps(pe, step)
                        U = B * NT
                        probs_T(NT - 1, B - 1, U - 1, 0)
                        probs_T(NT - 1, B - 1, U - 1, 1)
                        output_T(NT - 1, 0, U - 2, 4 * (U - 1) + EV[0])
                        probs_T(NT - 1, B - 1, U - 1, 2)
                        values(NT - 1, B - 1, U - 1)
                        project(NT - 1, 0, U - 2, U)
                        output_T(NT - 1, B - 1, U - 1, 4 * U)
                        pe.wait_ge(y_done, U - 1)
                        project(NT - 1, B - 1, U - 1, U)

        def soft_mixture():
            st = ExitStack()
            with st:
                L = sb(st, "m_L", [P, B, NT, NS])
                nmax = sb(st, "m_nmax", [P, B, NT])
                slT = sb(st, "m_slT", [P, KD, B, NS])
                wg = sb(st, "m_wg", [P, RING, KD, F0])
                wu = sb(st, "m_wu", [P, RING, KD, F0])
                wd = sb(st, "m_wd", [P, RING, KF, D])
                bgu = sb(st, "m_bgu", [P, 2, E0, KF])
                bdr = sb(st, "m_bdr", [1, RING, D])
                tok = ExitStack()
                XL = sb(tok, "m_XL", [P, B, NT, D + 1])
                cb = sb(tok, "m_cb", [P, B, NS])
                wg_ld = [sem(f"m_wg_ld{i}") for i in range(RING)]
                b_ld = sem("m_b_ld")
                begin, end, power = norm_factors("m_", TT, twice=True)

                def load_expert(sp, e, s):
                    sp.dma_start(wg[:, s], t["m_Wg"][e].rearrange("(k p) f -> p k f", p=P)).then_inc(wg_ld[s], 16)
                    sp.dma_start(wu[:, s], t["m_Wu"][e].rearrange("(k p) f -> p k f", p=P)).then_inc(wg_ld[s], 16)
                    sp.dma_start(wd[:, s], t["m_Wd"][e].rearrange("(k p) d -> p k d", p=P)).then_inc(wg_ld[s], 16)
                    sp.dma_start(bdr[:, s, :], t["m_bd"].rearrange("(a e) d -> a e d", a=1)[:, e, :]).then_inc(wg_ld[s], 16)

                pre = ExitStack()
                with pre:
                    cm = slT[:, 0]
                    rest = slT[:, 1].rearrange("p b n -> p (b n)")
                    tn, xw = (rest[:, i * B * D:(i + 1) * B * D].rearrange("p (b d) -> p b d", b=B) for i in range(2))
                    cmw = [rest[:, b * NS:(b + 1) * NS].rearrange("p (c n) -> p c n", c=CS) for b in range(B)]
                    xT = sb(pre, "m_xT", [P, B, KD, P])
                    cmx = sb(pre, "m_cmx", [P, B, CS])
                    psT = ps(pre, "m_psT", [P, B, BANK])
                    psL = ps(pre, "m_psL", [P, B, NS])
                    psC = ps(pre, "m_psC", [P, NS])
                    cmT = [psC[:, :], psL[:, 1, :]]
                    tn_ready = sem("m_tn_ready")
                    xl_step = sem("m_xl_step")
                    xl_ready = sem("m_xl_ready")
                    xl_copy = sem("m_xl_copy")
                    xlT_mm = sem("m_xlT_mm")
                    xlT_ready = sem("m_xlT_ready")
                    l_mm = sem("m_l_mm")
                    l_max = sem("m_l_max")
                    l_copy = sem("m_l_copy")
                    cm_step = sem("m_cm_step")
                    cmT_mm = sem("m_cmT_mm")
                    cmw_ready = sem("m_cmw_ready")
                    cb_mm = sem("m_cb_mm")
                    cb_ready = sem("m_cb_ready")
                    with nc.Block() as block:
                        @block.sync
                        def _(sp):
                            sp.dma_start(bgu[:, 0], t["m_bgT"]).then_inc(b_ld, 16)
                            sp.dma_start(bgu[:, 1], t["m_buT"]).then_inc(b_ld, 16)
                            for e in range(RING):
                                load_expert(sp, e, e)

                        @block.vector
                        def _(dve):
                            def norm_in(j, s, u):
                                i = s * NT + j
                                wait(dve, xl_ready, u - 1)
                                dve.tensor_scalar(tn[:, s], X[:, s, j], mean[:, bass.ds(i, 1)], rstd[:, bass.ds(i, 1)],
                                                  ALU.subtract, ALU.mult).then_inc(tn_ready, 1)

                            def maxima(j, s, u):
                                dve.wait_ge(l_copy, u + 1)
                                dve.tensor_reduce(nmax[:, s, bass.ds(j, 1)], L[:, s, j, :], AX.X, ALU.max
                                                  ).then_inc(l_max, 1)
                                dve.wait_ge(cm_step, u + 2)
                                dve.tensor_tensor(cm[:, s, :], cm[:, s, :], L[:, s, j, :], ALU.max).then_inc(cm_step, 1)

                            def step(j, s, v, n, a):
                                if a:
                                    norm_in(*after(j, s, 2), B * j + s + 2)
                                maxima(j, s, B * j + s)

                            begin(dve)
                            dve.memset(cm[:, :, :], -BIG).then_inc(cm_step, 1)
                            dve.memset(XL[:, :, :, D:D + 1], 1.0).then_inc(cm_step, 1)
                            end(dve)
                            dve.wait_ge(cm_step, 2)
                            for s in range(B):
                                norm_in(0, s, s)
                            pair_steps(dve, NT, step)
                            dve.wait_ge(cm_step, 2 + TT)
                            dve.wait_ge(l_max, TT)
                            dve.tensor_scalar(nmax[:, :, :], nmax[:, :, :], -1.0, None, ALU.mult).then_inc(l_max, 1)
                            for b in range(B):
                                dve.wait_ge(cmT_mm, b + 1)
                                dve.tensor_reduce(cmx[:, b, :], cmT[b].rearrange("p (c n) -> p c n", c=CS),
                                                  AX.X, ALU.max).then_inc(cmw_ready, 1)
                                dve.wait_ge(cmw_ready, 2 * b + 1)
                                dve.tensor_copy(cmw[b], cmx[:, b, :].unsqueeze(2).to_broadcast([P, CS, P])
                                                ).then_inc(cmw_ready, 1)
                            dve.wait_ge(l_max, TT + 1)

                        @block.gpsimd
                        def _(pool):
                            gain = Chain(pool, xl_step, B)

                            def affine(j, s, u):
                                pool.wait_ge(tn_ready, u + 1)
                                gain.step(pool.tensor_tensor(tn[:, s], tn[:, s], gains[:, 0, :], ALU.mult))
                                wait(pool, xlT_mm, u - 1)
                                wait(pool, xl_copy, u - 1)
                                pool.tensor_tensor(xw[:, s], tn[:, s], gains[:, 1, :], ALU.add).then_inc(xl_ready, 1)

                            power(pool)
                            gain.turn(0)
                            for s in range(B):
                                affine(0, s, s)
                            with pool.Fori(1, NT) as j:
                                gain.turn(j)
                                for s in range(B):
                                    affine(j, s, B * j + s)

                        @block.tensor
                        def _(pe):
                            def input_T(j, s, u):
                                pe.wait_ge(xl_ready, u + 1)
                                wait(pe, xlT_ready, u - 1)
                                for k in range(KD):
                                    mm = pe.transpose(psT[:, s, k * P:(k + 1) * P],
                                                      xw[:, s, k * P:(k + 1) * P], ident[:, :])
                                mm.then_inc(xlT_mm, 1)

                            def logits(j, s, u):
                                pe.wait_ge(xlT_ready, u + 1)
                                wait(pe, l_copy, u - 1)
                                for q in range(NS // BANK):
                                    for k in range(KD):
                                        mm = pe.matmul(psL[:, s, q * BANK:(q + 1) * BANK], xT[:, s, k, :],
                                                       seT[:, k, q * BANK:(q + 1) * BANK],
                                                       start=k == 0, stop=k == KD - 1)
                                mm.then_inc(l_mm, 1)

                            def step(j, s, v, n, a):
                                if n:
                                    input_T(*after(j, s, 1), B * j + s + 1)
                                logits(j, s, B * j + s)

                            input_T(0, 0, 0)
                            pair_steps(pe, NT, step)
                            pe.wait_ge(cm_step, 2 + TT)
                            pe.wait_ge(l_copy, TT)
                            for b in range(B):
                                for c in range(CS):
                                    mm = pe.transpose(cmT[b][:, c * P:(c + 1) * P], cm[:, b, c * P:(c + 1) * P], ident[:, :])
                                mm.then_inc(cmT_mm, 1)
                            for b in range(B):
                                pe.wait_ge(cmw_ready, 2 * b + 2)
                                wait(pe, cb_ready, b)
                                for c in range(CS):
                                    mm = pe.matmul(psL[:, 0, c * P:(c + 1) * P], cmw[b][:, c, :], ident[:, :],
                                                   start=True, stop=True)
                                mm.then_inc(cb_mm, 1)

                        @block.scalar
                        def _(act):
                            def input_T(j, s, u):
                                act.wait_ge(xlT_mm, u + 1)
                                wait(act, l_mm, u - 1)
                                act.activation(xT[:, s].rearrange("p k n -> p (k n)"), psT[:, s, 0:KD * P], ACT.Copy
                                               ).then_inc(xlT_ready, 1)
                                act.activation(XL[:, s, j, 0:D], xw[:, s, :], ACT.Copy).then_inc(xl_copy, 1)

                            def logits(j, s, u):
                                act.wait_ge(l_mm, u + 1)
                                act.activation(L[:, s, j, :], psL[:, s, :], ACT.Copy).then_inc(l_copy, 1)

                            def step(j, s, v, n, a):
                                if n:
                                    input_T(*after(j, s, 1), B * j + s + 1)
                                logits(j, s, B * j + s)

                            input_T(0, 0, 0)
                            pair_steps(act, NT, step)
                            act.wait_ge(l_copy, TT)
                            act.wait_ge(xl_copy, TT)
                            for b in range(B):
                                act.wait_ge(cb_mm, b + 1)
                                act.activation(cb[:, b, :], psL[:, 0, :], ACT.Copy).then_inc(cb_ready, 1)
                            act.wait_ge(cb_ready, B)

                mid = ExitStack()
                with mid:
                    ed = sb(mid, "m_ed", [P, 2, NS])
                    sl = seT[:, :, :].rearrange("p k n -> p (k n)").rearrange("p (c d) -> p c d", c=CS)
                    rden = sb(mid, "m_rden", [P, CS])
                    acc = ps(mid, "m_acc", [P, CS, BANK])
                    d_ready = sem("m_d_ready")
                    e_ready = sem("m_e_ready")
                    e_used = sem("m_e_used")
                    sl_step = sem("m_sl_step")
                    sl_mm = sem("m_sl_mm")
                    slT_ready = sem("m_slT_ready")
                    with nc.Block() as block:
                        @block.vector
                        def _(dve):
                            def shift(b, j, s, u):
                                wait(dve, e_used, u - 1)
                                dve.tensor_tensor(ed[:, s, :], L[:, b, j, :], cb[:, b, :], ALU.subtract
                                                  ).then_inc(d_ready, 1)

                            for b in range(B):
                                u0 = b * NT
                                for s in range(2):
                                    if b == 0:
                                        shift(b, s, s, s)
                                with dve.Fori(1, NT // 2) as q:
                                    for s in range(2):
                                        shift(b, 2 * q + s, s, u0 + 2 * q + s)
                                if b < B - 1:
                                    for s in range(2):
                                        shift(b + 1, s, s, u0 + NT + s)
                                dve.wait_ge(e_used, u0 + NT)
                                dve.reciprocal(rden[:, :].unsqueeze(2), acc[:, :, D:D + 1]).then_inc(sl_step, 1)
                                dve.wait_ge(sl_step, b * 2 + 1)
                                wait(dve, sl_mm, KD * b)
                                dve.tensor_tensor(sl[:, :, :], acc[:, :, 0:D],
                                                  rden[:, :].unsqueeze(2).to_broadcast([P, CS, D]), ALU.mult
                                                  ).then_inc(sl_step, 1)

                        @block.scalar
                        def _(act):
                            def exponent(s, u):
                                act.wait_ge(d_ready, u + 1)
                                act.activation(ed[:, s, :], ed[:, s, :], ACT.Exp).then_inc(e_ready, 1)

                            for b in range(B):
                                u0 = b * NT
                                for s in range(2):
                                    if b == 0:
                                        exponent(s, s)
                                with act.Fori(1, NT // 2) as q:
                                    for s in range(2):
                                        exponent(s, u0 + 2 * q + s)
                                if b < B - 1:
                                    for s in range(2):
                                        exponent(s, u0 + NT + s)
                                for k in range(KD):
                                    act.wait_ge(sl_mm, KD * b + k + 1)
                                    act.activation(slT[:, k, b, :].rearrange("p (h n) -> p h n", n=BANK),
                                                   acc[:, 2 * k:2 * k + 2, :], ACT.Copy).then_inc(slT_ready, 1)
                            act.wait_ge(slT_ready, KD * B)

                        @block.tensor
                        def _(pe):
                            def add_tile(b, j, s, u, start, stop):
                                pe.wait_ge(e_ready, u + 1)
                                for c in range(CS):
                                    mm = pe.matmul(acc[:, c, 0:D + 1], ed[:, s, c * P:(c + 1) * P],
                                                   XL[:, b, j, :], start=start, stop=stop)
                                mm.then_inc(e_used, 1)

                            for b in range(B):
                                u0 = b * NT
                                wait(pe, slT_ready, KD * b)
                                add_tile(b, 0, 0, u0, True, False)
                                add_tile(b, 1, 1, u0 + 1, False, False)
                                with pe.Fori(1, NT // 2 - 1) as q:
                                    for s in range(2):
                                        add_tile(b, 2 * q + s, s, u0 + 2 * q + s, False, False)
                                add_tile(b, NT - 2, 0, u0 + NT - 2, False, False)
                                add_tile(b, NT - 1, 1, u0 + NT - 1, False, True)
                                pe.wait_ge(sl_step, 2 * b + 2)
                                for k in range(KD):
                                    for c in range(CS):
                                        mm = pe.transpose(acc[:, 2 * k + c // 4, (c % 4) * P:(c % 4 + 1) * P],
                                                          sl[:, c, k * P:(k + 1) * P], ident[:, :])
                                    mm.then_inc(sl_mm, 1)

                tok.close()
                post = ExitStack()
                with post:
                    eos = sb(post, "m_eos", [P, B, CS, D])
                    exps = ExitStack()
                    gu_mm = sem("m_gu_mm")
                    gu_read = sem("m_gu_read")
                    g_act = sem("m_g_act")
                    h_ready = sem("m_h_ready")
                    eo_mm = sem("m_eo_mm")
                    eo_ready = sem("m_eo_ready")
                    eo_moved = [sem(f"m_eo_moved{i}") for i in range(2)]
                    with exps:
                        TOK = B * SL
                        gt = sb(exps, "m_gt", [P, 2, KF, TOK])
                        up = sb(exps, "m_up", [P, 2, KF, TOK])
                        eo = sb(exps, "m_eo", [P, 2, D])
                        psG = ps(exps, "m_psG", [P, 2, 2, KF * TOK])
                        psE = ps(exps, "m_psE", [P, 2, BANK])
                        with nc.Block() as block:
                            def experts(eng, body):
                                for s in range(RING):
                                    body(s, 0, s)
                                with eng.Fori(1, E0 // RING - 1) as q:
                                    for s in range(RING):
                                        body(RING * q + s, q, s)
                                for s in range(RING):
                                    body(E0 - RING + s, E0 // RING - 1, s)

                            @block.sync
                            def _(sp):
                                def fetch(e, q, s):
                                    sp.wait_ge(eo_mm, e - RING + 1)
                                    load_expert(sp, e, s)

                                with sp.Fori(1, E0 // RING) as q:
                                    for s in range(RING):
                                        fetch(RING * q + s, q, s)

                            @block.tensor
                            def _(pe):
                                def gate_up(e, q, s):
                                    pe.wait_ge(wg_ld[s], 64 * q + 64)
                                    wait(pe, gu_read, 2 * (e - 1))
                                    for i, w in enumerate((wg, wu)):
                                        for f in range(KF):
                                            for k in range(KD):
                                                mm = pe.matmul(psG[:, s % 2, i, f * TOK:(f + 1) * TOK],
                                                               w[:, s, k, f * P:(f + 1) * P],
                                                               slT[:, k, :, bass.ds(e * SL, SL)],
                                                               start=k == 0, stop=k == KD - 1)
                                        mm.then_inc(gu_mm, 1)

                                def down(e, q, s):
                                    pe.wait_ge(h_ready, e + 1)
                                    wait(pe, eo_ready, e - 1)
                                    for f in range(KF):
                                        pe.matmul(psE[:, s % 2, 0:D], gt[:, s % 2, f, :], wd[:, s, f, :],
                                                  start=f == 0, stop=False)
                                    pe.matmul(psE[:, s % 2, 0:D], ones[0:1, 0:TOK], bdr[0:1, s, :], start=False, stop=True
                                              ).then_inc(eo_mm, 1)

                                def body(e, q, s):
                                    if not (isinstance(e, int) and e == E0 - 1):
                                        gate_up(e + 1, *((q, s + 1) if s + 1 < RING else (q + 1, 0)))
                                    down(e, q, s)

                                gate_up(0, 0, 0)
                                experts(pe, body)

                            @block.vector
                            def _(dve):
                                def biases(e, s):
                                    for i, dst in enumerate((gt, up)):
                                        dve.wait_ge(gu_mm, 2 * e + i + 1)
                                        wait(dve, eo_mm, e - 1)
                                        dve.tensor_tensor(
                                            dst[:, s % 2], psG[:, s % 2, i, :].rearrange("p (f n) -> p f n", f=KF),
                                            bgu[:, i, e, :].unsqueeze(2).to_broadcast([P, KF, TOK]), ALU.add
                                            ).then_inc(gu_read, 1)

                                def gated(e, s):
                                    dve.wait_ge(g_act, e + 1)
                                    dve.wait_ge(gu_read, 2 * e + 2)
                                    dve.tensor_tensor(gt[:, s % 2], gt[:, s % 2], up[:, s % 2], ALU.mult
                                                      ).then_inc(h_ready, 1)

                                def body(e, q, s):
                                    biases(e, s)
                                    gated(e, s)

                                dve.wait_ge(b_ld, 32)
                                experts(dve, body)
                                dve.wait_ge(h_ready, E0)

                            @block.scalar
                            def _(act):
                                def gelu(e, s):
                                    act.wait_ge(gu_read, 2 * e + 1)
                                    act.activation(gt[:, s % 2], gt[:, s % 2], ACT.Gelu).then_inc(g_act, 1)

                                def outputs(e, n, s):
                                    act.wait_ge(eo_mm, e + 1)
                                    wait(act, eo_moved[s % 2], 32 * n)
                                    act.activation(eo[:, s % 2, :], psE[:, s % 2, 0:D], ACT.Copy).then_inc(eo_ready, 1)

                                def body(e, q, s):
                                    gelu(e, s)
                                    if not (isinstance(e, int) and e == 0):
                                        n = RING // 2 * q + s // 2
                                        outputs(e - 1, n if s % 2 else n - 1, s - 1)

                                experts(act, body)
                                outputs(E0 - 1, E0 // 2 - 1, RING - 1)

                            @block.gpsimd
                            def _(pool):
                                with pool.Fori(0, E0 // 2) as j:
                                    for s in range(2):
                                        e = 2 * j + s
                                        pool.wait_ge(eo_ready, e + 1)
                                        for b in range(B):
                                            pool.dma_start(eos[s * SL:(s + 1) * SL, b, j, :],
                                                           eo[b * SL:(b + 1) * SL, s, :]).then_inc(eo_moved[s], 16)
                                for s in range(2):
                                    pool.wait_ge(eo_moved[s], 32 * (E0 // 2))

                    comb = ExitStack()
                    with comb:
                        ec = wg[:, 0:B].rearrange("p b k f -> p b (k f)")
                        ecT = wu[:, 0:B].rearrange("p b k f -> p b (k f)").rearrange("p b (c n) -> p b c n", c=CS)
                        den = sb(comb, "m_den", [P, B])
                        rdc = sb(comb, "m_rdc", [P, B])
                        psK = ps(comb, "m_psK", [P, B, NS])
                        psY = ps(comb, "m_psY", [P, B, BANK])
                        ec_ready = sem("m_ec_ready")
                        ec_mm = sem("m_ec_mm")
                        ecT_ready = sem("m_ecT_ready")
                        cy_mm = sem("m_cy_mm")
                        cy_step = sem("m_cy_step")
                        cy_done = sem("m_cy_done")
                        cy_stat = sem("m_cy_stat")
                        with nc.Block() as block:
                            @block.scalar
                            def _(act):
                                def exponent(j, s, u):
                                    wait(act, ec_mm, u - 1)
                                    wait(act, cy_step, u - 1)
                                    act.activation(ec[:, s, :], L[:, s, j, :], ACT.Exp, bias=nmax[:, s, bass.ds(j, 1)],
                                                   accum_out=den[:, s:s + 1]).then_inc(ec_ready, 1)

                                for s in range(B):
                                    exponent(0, s, s)
                                with act.Fori(1, NT) as j:
                                    for s in range(B):
                                        exponent(j, s, B * j + s)

                            @block.tensor
                            def _(pe):
                                def weights_T(j, s, u):
                                    pe.wait_ge(ec_ready, u + 1)
                                    wait(pe, ecT_ready, u - 1)
                                    for c in range(CS):
                                        mm = pe.transpose(psK[:, s, c * P:(c + 1) * P], ec[:, s, c * P:(c + 1) * P],
                                                          ident[:, :])
                                    mm.then_inc(ec_mm, 1)

                                def outputs(j, s, u):
                                    pe.wait_ge(ecT_ready, u + 1)
                                    wait(pe, cy_done, u - 1)
                                    for c in range(CS):
                                        mm = pe.matmul(psY[:, s, 0:D], ecT[:, s, c, :], eos[:, s, c, :],
                                                       start=c == 0, stop=c == CS - 1)
                                    mm.then_inc(cy_mm, 1)

                                def step(j, s, v, n, a):
                                    if n:
                                        weights_T(*after(j, s, 1), B * j + s + 1)
                                    outputs(j, s, B * j + s)

                                weights_T(0, 0, 0)
                                pair_steps(pe, NT, step)

                            @block.vector
                            def _(dve):
                                def weights_T(j, s, u):
                                    dve.wait_ge(ec_mm, u + 1)
                                    wait(dve, cy_mm, u - 1)
                                    dve.tensor_copy(ecT[:, s].rearrange("p c n -> p (c n)"), psK[:, s, :]
                                                    ).then_inc(ecT_ready, 1)

                                def residual(j, s, u):
                                    dve.wait_ge(ec_ready, u + 1)
                                    wait(dve, cy_done, u - 1)
                                    dve.reciprocal(rdc[:, s:s + 1], den[:, s:s + 1]).then_inc(cy_step, 1)
                                    dve.wait_ge(cy_step, u + 1)
                                    dve.wait_ge(cy_mm, u + 1)
                                    dve.scalar_tensor_tensor(X[:, s, j], psY[:, s, 0:D], rdc[:, s:s + 1], X[:, s, j],
                                                             ALU.mult, ALU.add).then_inc(cy_done, 1)

                                def stat(j, s, u):
                                    dve.wait_ge(cy_done, u + 1)
                                    dve.bn_stats(stats[:, s * NT + j, :], X[:, s, j]).then_inc(cy_stat, 1)

                                def step(j, s, v, n, a):
                                    u = B * j + s
                                    if n:
                                        weights_T(*after(j, s, 1), u + 1)
                                    residual(j, s, u)
                                    if v:
                                        stat(*before(j, s, 1), u - 1)

                                weights_T(0, 0, 0)
                                pair_steps(dve, NT, step)
                                stat(NT - 1, B - 1, TT - 1)
                                dve.wait_ge(cy_stat, TT)

        def top3_mixture(W1, W2, w1_ld, w2_ld):
            st = ExitStack()
            Xf = X[:, :, :, :].rearrange("p b t d -> p (b t) d")
            begin, end, power = norm_factors("f_", TT)
            with st:
                wt = sb(st, "f_wt", [P, R, TOP, TT])
                rows = sb(st, "f_rows", [P, TOP, TT], U32)
                toks = sb(st, "f_toks", [P, 2, LT], U32)
                owner = sb(st, "f_owner", [1, 2, LT], I32)
                dwb = sb(st, "f_dwb", [P, TT, E1])
                Z = sb(st, "f_Z", [P, R, TT, E1])
                hot = sb(st, "f_hot", [P, 2, TOP, TT, E1])
                iota = sb(st, "f_iota", [P, P])
                below = sb(st, "f_below", [P, P])
                allone = sb(st, "f_allone", [P, P])
                tokid = sb(st, "f_tokid", [P, TT, TOP])
                spare = sb(st, "f_spare", [P, LT])
                dest = sb(st, "f_dest", [P, LT], U32)
                pair = sb(st, "f_pair", [P, LT])
                pairi = sb(st, "f_pairi", [P, 2, LT], I32)
                tmp = sb(st, "f_tmp", [P, TOP, TT, E1])
                first = sb(st, "f_first", [P, TT])
                chosen = sb(st, "f_chosen", [P, TT, E1])
                place = sb(st, "f_place", [P, TT, E1])
                tiles = [sb(st, f"f_tiles{i}", [P, TT + 1, E1]) for i in range(2)]
                cnt = sb(st, "f_cnt", [P, E1])
                cnti = sb(st, "f_cnti", [P, E1], I32)
                start = [sb(st, f"f_start{i}", [P, E1 + 1, 1]) for i in range(2)]
                past = sb(st, "f_past", [P, LT, E1])
                own = sb(st, "f_own", [P, LT])
                pk = sb(st, "f_pk", [P, TOP, TT])
                pki = sb(st, "f_pki", [P, TOP, TT], I32)
                part = sb(st, "f_part", [P, 2, TOP, TT], I32)
                pdiv = sb(st, "f_pdiv", [P, TOP, TT])
                pmod = sb(st, "f_pmod", [P, TOP, TT])
                at_row = sb(st, "f_at_row", [P, 2, TOP, P])
                at_tile = sb(st, "f_at_tile", [P, 2, TOP, LT])

                def over(v):
                    return v.unsqueeze(2).to_broadcast([P, TT, E1])

                def pick(dve, one, r, h):
                    for k in range(TOP):
                        top, z, eq = wt[:, r, k, :], Z[:, r], tmp[:, 0]
                        one.step(dve.tensor_reduce(top, z, AX.X, ALU.max))
                        one.step(dve.tensor_tensor(eq, z, over(top), ALU.is_equal))
                        one.step(dve.scalar_tensor_tensor(eq, eq, -float(E1),
                                                          iota[:, 0:E1].unsqueeze(1).to_broadcast([P, TT, E1]),
                                                          ALU.mult, ALU.add))
                        one.step(dve.tensor_reduce(first[:, :], eq, AX.X, ALU.min))
                        one.step(dve.tensor_tensor(hot[:, h, k], eq, over(first[:, :]), ALU.is_equal))
                        if k < TOP - 1:
                            one.step(dve.scalar_tensor_tensor(z, hot[:, h, k], -BIG, z, ALU.mult, ALU.add))

                def running(dve, one, ab, n):
                    a, b = ab
                    d = 1
                    while d < n - 1:
                        one.step(dve.tensor_copy(b[:, 0:d], a[:, 0:d]), hold=False)
                        one.step(dve.tensor_tensor(b[:, d:n], a[:, d:n], a[:, 0:n - d], ALU.add))
                        a, b = b, a
                        d *= 2
                    return a

                def lists(dve, one, r, counts, count_mm):
                    nb = TT * E1
                    dve.wait_ge(count_mm, 1)
                    one.step(dve.memset(tiles[0][:, 0, :], 0.0), hold=False)
                    one.step(dve.memset(start[0][:, 0:1, :], 0.0), hold=False)
                    one.step(dve.tensor_copy(tiles[0][:, 1:TT + 1, :],
                                             counts[:, nb:2 * nb].rearrange("p (t e) -> p t e", t=TT)))
                    before_tile = running(dve, one, tiles, TT + 1)
                    one.step(dve.tensor_scalar(cnt[:, :], before_tile[:, TT, :], float(P - 1), None, ALU.add))
                    one.step(dve.tensor_copy(cnti[:, :], cnt[:, :]))
                    one.step(dve.tensor_scalar(cnti[:, :], cnti[:, :], 7, None, ALU.arith_shift_right))
                    one.step(dve.tensor_copy(start[0][:, 1:E1 + 1, :], cnti[:, :].unsqueeze(2)))
                    begin = running(dve, one, start, E1 + 1)
                    one.step(dve.tensor_tensor(place[:, :, :], counts[:, 0:nb].rearrange("p (t e) -> p t e", t=TT),
                                               before_tile[:, 0:TT, :], ALU.add))
                    one.step(dve.scalar_tensor_tensor(
                        place[:, :, :], begin[:, 0:E1, 0].unsqueeze(1).to_broadcast([P, TT, E1]), float(P),
                        place[:, :, :], ALU.mult, ALU.add))
                    one.step(dve.tensor_tensor(tmp[:, :, :, :], hot[:, 0],
                                               place[:, :, :].unsqueeze(1).to_broadcast([P, TOP, TT, E1]), ALU.mult))
                    one.step(dve.tensor_reduce(pk[:, :, :], tmp[:, :, :, :], AX.X, ALU.add))
                    one.step(dve.tensor_copy(pki[:, :, :], pk[:, :, :]))
                    if r == 0:
                        one.step(dve.tensor_copy(rows[:, :, :], pki[:, :, :]), hold=False)
                    one.step(dve.tensor_scalar(part[:, 0], pki[:, :, :], 7, None, ALU.arith_shift_right), hold=False)
                    one.step(dve.tensor_scalar(part[:, 1], pki[:, :, :], P - 1, None, ALU.bitwise_and))
                    one.step(dve.tensor_copy(pdiv[:, :, :], part[:, 0]), hold=False)
                    one.step(dve.tensor_copy(pmod[:, :, :], part[:, 1]), hold=False)
                    one.step(dve.tensor_tensor(
                        past[:, :, :], iota[:, 0:LT].unsqueeze(2).to_broadcast([P, LT, E1]),
                        begin[:, 1:E1 + 1, 0].unsqueeze(1).to_broadcast([P, LT, E1]), ALU.is_ge))
                    one.step(dve.tensor_reduce(own[:, :], past[:, :, :], AX.X, ALU.add))
                    one.step(dve.tensor_scalar(own[:, :], own[:, :], float(E1 - 1), None, ALU.min))
                    one.step(dve.tensor_copy(owner[:, r, :], own[0:1, :]))

                def choose(dve, one, chosen_ready):
                    one.step(dve.tensor_tensor(chosen[:, :, :], hot[:, 0, 0], hot[:, 0, 1], ALU.add))
                    one.step(dve.tensor_tensor(chosen[:, :, :], chosen[:, :, :], hot[:, 0, 2], ALU.add))
                    dve.sem_inc(chosen_ready, 1)

                def count(pe, counts, chosen_ready, count_mm):
                    pe.wait_ge(chosen_ready, 1)
                    ct = chosen[:, :, :].rearrange("p t e -> p (t e)")
                    nb = TT * E1
                    pe.matmul(counts[:, 0:nb], below[:, :], ct, start=True, stop=True)
                    pe.matmul(counts[:, nb:2 * nb], allone[:, :], ct, start=True, stop=True).then_inc(count_mm, 1)

                def match(dve, at, i, s, at_used, at_ready):
                    wait(dve, at_used, i - 1)
                    at.step(dve.tensor_tensor(
                        at_tile[:, s], iota[:, 0:LT].unsqueeze(1).to_broadcast([P, TOP, LT]),
                        pdiv[:, :, bass.ds(i, 1)].to_broadcast([P, TOP, LT]), ALU.is_equal), hold=False)
                    at.step(dve.tensor_tensor(
                        at_row[:, s], iota[:, :].unsqueeze(1).to_broadcast([P, TOP, P]),
                        pmod[:, :, bass.ds(i, 1)].to_broadcast([P, TOP, P]), ALU.is_equal), hold=False)
                    dve.wait_ge(at.sem, at.base + at.n - 1)
                    dve.tensor_tensor(at_tile[:, s], at_tile[:, s], tokid[:, i, :].unsqueeze(2).to_broadcast([P, TOP, LT]),
                                      ALU.mult).then_inc(at_ready, 1)

                def found_tokens(dve, one, r, found):
                    one.step(dve.tensor_scalar(pair[:, :], found[:, 0:LT], -1.0, None, ALU.add))
                    one.step(dve.tensor_copy(pairi[:, 0], pair[:, :]))
                    one.step(dve.tensor_scalar(pairi[:, 1], pairi[:, 0], B * N - 1, None, ALU.bitwise_and))
                    one.step(dve.tensor_copy(toks[:, r, :], pairi[:, 1]))
                    if r == 1:
                        one.step(dve.scalar_tensor_tensor(own[:, :], found[:, 0:LT], 0.0, spare[:, :],
                                                          ALU.is_equal, ALU.mult))
                        one.step(dve.tensor_tensor(pair[:, :], pair[:, :], own[:, :], ALU.add))
                        one.step(dve.tensor_copy(pairi[:, 0], pair[:, :]))
                        one.step(dve.tensor_copy(dest[:, :], pairi[:, 0]))

                def add_tokens(pe, i, s, found, at_ready, at_used, start, stop):
                    pe.wait_ge(at_ready, i + 1)
                    for k in range(TOP):
                        mm = pe.matmul(found[:, 0:LT], at_row[:, s, k, :], at_tile[:, s, k, :],
                                       start=start and k == 0, stop=stop and k == TOP - 1)
                    mm.then_inc(at_used, 1)

                def add_all(pe, found, at_ready, at_used):
                    add_tokens(pe, 0, 0, found, at_ready, at_used, True, False)
                    add_tokens(pe, 1, 1, found, at_ready, at_used, False, False)
                    with pe.Fori(1, TT // 2 - 1) as j:
                        for s in range(2):
                            add_tokens(pe, 2 * j + s, s, found, at_ready, at_used, False, False)
                    add_tokens(pe, TT - 2, 0, found, at_ready, at_used, False, False)
                    add_tokens(pe, TT - 1, 1, found, at_ready, at_used, False, True)

                rt = ExitStack()
                with rt:
                    Pw = sb(rt, "f_Pw", [P, KD, DA])
                    U = sb(rt, "f_U", [DA, R * E1])
                    xn = sb(rt, "f_xn", [P, TT, D])
                    xw = sb(rt, "f_xw", [P, 2, D])
                    xT = sb(rt, "f_xT", [P, 2, KD, P])
                    aT = sb(rt, "f_aT", [DA, 2, P])
                    psT = ps(rt, "f_psT", [P, 2, BANK])
                    psA = ps(rt, "f_psA", [DA, 2, BANK])
                    psZ = ps(rt, "f_psZ", [P, 2, BANK])
                    psN = ps(rt, "f_psN", [P, BANK])
                    psF = ps(rt, "f_psF", [P, BANK])
                    ld = sem("f_ld")
                    xn_ready = sem("f_xn_ready")
                    xw_ready = sem("f_xw_ready")
                    xn_stored = sem("f_xn_stored")
                    xT_mm = sem("f_xT_mm")
                    xT_ready = sem("f_xT_ready")
                    a_mm = sem("f_a_mm")
                    a_ready = sem("f_a_ready")
                    z_mm = sem("f_z_mm")
                    z_ready = sem("f_z_ready")
                    r_step = sem("f_r_step")
                    at_step = sem("f_at_step")
                    chosen_ready = sem("f_chosen_ready")
                    count_mm = sem("f_count_mm")
                    at_ready = sem("f_at_ready")
                    at_used = sem("f_at_used")
                    with nc.Block() as block:
                        @block.sync
                        def _(sp):
                            sp.dma_start(Pw[:, :, :], t["f_PwT"].rearrange("(k p) a -> p k a", p=P)).then_inc(ld, 16)
                            sp.dma_start(U[:, :], t["f_UT"]).then_inc(ld, 16)
                            sp.dma_start(iota[:, :], t["c_iota"].partition_broadcast(P)).then_inc(ld, 16)
                            sp.dma_start(below[:, :], t["c_below"]).then_inc(ld, 16)
                            sp.dma_start(tokid[:, :, :], t["c_tokid"]).then_inc(ld, 16)
                            sp.dma_start(spare[:, :], t["c_spare"]).then_inc(ld, 16)
                            sp.wait_ge(xn_ready, TT)
                            sp.dma_start(xn_d.rearrange("(t p) d -> p t d", p=P), xn[:, :, :]).then_inc(xn_stored, 16)
                            sp.wait_ge(xn_stored, 16)

                        @block.vector
                        def _(dve):
                            def norm_in(j, s, u):
                                wait(dve, xT_mm, u - 1)
                                wait(dve, xn_ready, u - 1)
                                dve.tensor_scalar(xw[:, s, :], Xf[:, u, :], mean[:, bass.ds(u, 1)],
                                                  rstd[:, bass.ds(u, 1)], ALU.subtract, ALU.mult).then_inc(xw_ready, 1)

                            def scores(j, s, u):
                                dve.wait_ge(z_mm, u + 1)
                                dve.tensor_copy(Z[:, :, u, :], psZ[:, s, 0:R * E1].rearrange("p (r e) -> p r e", r=R)
                                                ).then_inc(z_ready, 1)

                            def step(j, s, v, n, a):
                                u = 2 * j + s
                                if a:
                                    norm_in(*after(j, s, 2), u + 2)
                                if v:
                                    scores(*before(j, s, 1), u - 1)

                            begin(dve)
                            end(dve)
                            for s in range(2):
                                norm_in(0, s, s)
                            pair_steps(dve, TT // 2, step)
                            scores(TT // 2 - 1, 1, TT - 1)
                            dve.wait_ge(ld, 97)
                            dve.wait_ge(z_ready, TT)
                            one = Chain(dve, r_step, 0)
                            one.turn(0)
                            pick(dve, one, 0, 0)
                            choose(dve, one, chosen_ready)
                            lists(dve, one, 0, psN, count_mm)
                            at = Chain(dve, at_step, 2 * 2)
                            at.turn(0)
                            for s in range(2):
                                match(dve, at, s, s, at_used, at_ready)
                            with dve.Fori(1, TT // 2) as j:
                                at.turn(j)
                                for s in range(2):
                                    match(dve, at, 2 * j + s, s, at_used, at_ready)
                                at.end()
                            dve.wait_ge(at_used, TT)
                            found_tokens(dve, one, 0, psF)

                        @block.scalar
                        def _(act):
                            def input_T(j, s, u):
                                act.wait_ge(xT_mm, u + 1)
                                wait(act, a_mm, u - 1)
                                act.activation(xT[:, s].rearrange("p k n -> p (k n)"), psT[:, s, 0:KD * P], ACT.Copy
                                               ).then_inc(xT_ready, 1)

                            def addresses(j, s, u):
                                act.wait_ge(a_mm, u + 1)
                                wait(act, z_mm, u - 1)
                                act.activation(aT[:, s, :], psA[:, s, 0:P], ACT.Copy).then_inc(a_ready, 1)

                            def step(j, s, v, n, a):
                                u = 2 * j + s
                                if n:
                                    input_T(*after(j, s, 1), u + 1)
                                addresses(j, s, u)

                            input_T(0, 0, 0)
                            pair_steps(act, TT // 2, step)

                        @block.gpsimd
                        def _(pool):
                            power(pool)
                            pool.memset(allone[:, :], 1.0).then_inc(ld, 1)
                            with pool.Fori(0, TT // 2) as j:
                                for s in range(2):
                                    u = 2 * j + s
                                    pool.wait_ge(xw_ready, u + 1)
                                    pool.tensor_copy(xn[:, u, :], xw[:, s, :]).then_inc(xn_ready, 1)

                        @block.tensor
                        def _(pe):
                            def input_T(j, s, u):
                                pe.wait_ge(xw_ready, u + 1)
                                wait(pe, xT_ready, u - 1)
                                for k in range(KD):
                                    mm = pe.transpose(psT[:, s, k * P:(k + 1) * P], xw[:, s, k * P:(k + 1) * P],
                                                      ident[:, :])
                                mm.then_inc(xT_mm, 1)

                            def addresses(j, s, u):
                                pe.wait_ge(xT_ready, u + 1)
                                wait(pe, a_ready, u - 1)
                                for k in range(KD):
                                    mm = pe.matmul(psA[:, s, 0:P], Pw[:, k, :], xT[:, s, k, :],
                                                   start=k == 0, stop=k == KD - 1)
                                mm.then_inc(a_mm, 1)

                            def scores(j, s, u):
                                pe.wait_ge(a_ready, u + 1)
                                wait(pe, z_ready, u - 1)
                                pe.matmul(psZ[:, s, 0:R * E1], aT[:, s, :], U[:, :], start=True, stop=True
                                          ).then_inc(z_mm, 1)

                            def step(j, s, v, n, a):
                                u = 2 * j + s
                                if n:
                                    input_T(*after(j, s, 1), u + 1)
                                addresses(j, s, u)
                                if v:
                                    scores(*before(j, s, 1), u - 1)

                            pe.wait_ge(ld, 97)
                            input_T(0, 0, 0)
                            pair_steps(pe, TT // 2, step)
                            scores(TT // 2 - 1, 1, TT - 1)
                            count(pe, psN, chosen_ready, count_mm)
                            add_all(pe, psF, at_ready, at_used)

                QUAD = 4

                def list_tiles(eng, body):
                    for s in range(QUAD):
                        body(s, 0, s)
                    with eng.Fori(1, LT // QUAD) as q:
                        for s in range(QUAD):
                            body(QUAD * q + s, q, s)
                    for s in range(LT % QUAD):
                        body(LT - LT % QUAD + s, LT // QUAD, s)

                def uses(s):
                    return -(-(LT - s) // QUAD)

                def following(q, s):
                    return (q, s + 1) if s + 1 < QUAD else (q + 1, 0)

                first_st = ExitStack()
                with first_st:
                    den = sb(first_st, "f_den", [P, R, TT])
                    r1_step = sem("f1_r_step")
                    gap_ready = sem("f1_gap_ready")
                    exp_ready = sem("f1_exp_ready")
                    chosen_ready = sem("f2_chosen_ready")
                    xg = sb(first_st, "f_xg", [P, QUAD, D])
                    ix = sb(first_st, "f1_ix", [P, QUAD], U32)
                    xT = sb(first_st, "f1_xT", [P, 2, KD, P])
                    po = sb(first_st, "f_po", [P, QUAD, HID])
                    psT = ps(first_st, "f1_psT", [P, 2, BANK])
                    psH = ps(first_st, "f1_psH", [P, 2, HID])
                    ix_ready = sem("f1_ix_ready")
                    xg_ld = [sem(f"f_xg_ld{i}") for i in range(QUAD)]
                    xT_mm = sem("f1_xT_mm")
                    xT_ready = sem("f1_xT_ready")
                    h_mm = sem("f1_h_mm")
                    po_ready = sem("f_po_ready")
                    po_stored = [sem(f"f_po_stored{i}") for i in range(QUAD)]
                    with nc.Block() as block:
                        @block.gpsimd
                        def _(pool):
                            def gather(i, q, s):
                                wait(pool, xT_mm, i - QUAD + 1)
                                pool.tensor_copy(ix[:, s:s + 1], toks[:, 0, bass.ds(i, 1)]).then_inc(ix_ready, 1)
                                pool.wait_ge(ix_ready, i + 1)
                                pool.nop(nofuse=True)
                                pool.indirect_dma_start(xg[:, s, :], None, xn_d, bass.IndirectOffsetOnAxis(
                                    ap=ix[:, s:s + 1], axis=0)).then_inc(xg_ld[s], 16)

                            list_tiles(pool, gather)

                        @block.tensor
                        def _(pe):
                            def turn(i, q, s):
                                pe.wait_ge(xg_ld[s], 16 * q + 16)
                                wait(pe, xT_ready, i - 1)
                                for k in range(KD):
                                    mm = pe.transpose(psT[:, s % 2, k * P:(k + 1) * P], xg[:, s, k * P:(k + 1) * P],
                                                      ident[:, :])
                                mm.then_inc(xT_mm, 1)

                            def multiply(i, q, s):
                                e = pe.value_load(owner[0:1, 0, bass.ds(i, 1)], min_val=0, max_val=E1 - 1)
                                pe.wait_ge(xT_ready, i + 1)
                                wait(pe, po_ready, i - 1)
                                for c in range(HID // BANK):
                                    for k in range(KD):
                                        mm = pe.matmul(psH[:, s % 2, c * BANK:(c + 1) * BANK], xT[:, s % 2, k, :],
                                                       W1[:, e, k, c * BANK:(c + 1) * BANK], start=k == 0, stop=k == KD - 1)
                                mm.then_inc(h_mm, 1)

                            def tile(i, q, s):
                                if not (isinstance(i, int) and i == LT - 1):
                                    turn(i + 1, *following(q, s))
                                multiply(i, q, s)

                            pe.wait_ge(w1_ld, 16 * E1)
                            turn(0, 0, 0)
                            list_tiles(pe, tile)

                        @block.scalar
                        def _(act):
                            def tokens_T(i, q, s):
                                act.wait_ge(xT_mm, i + 1)
                                wait(act, h_mm, i - 1)
                                act.activation(xT[:, s % 2].rearrange("p k n -> p (k n)"), psT[:, s % 2, 0:KD * P],
                                               ACT.Copy).then_inc(xT_ready, 1)

                            def products(i, q, s):
                                act.wait_ge(h_mm, i + 1)
                                wait(act, po_stored[s], 16 * q)
                                act.activation(po[:, s, :], psH[:, s % 2, :], ACT.Copy).then_inc(po_ready, 1)

                            def tile(i, q, s):
                                if not (isinstance(i, int) and i == LT - 1):
                                    tokens_T(i + 1, *following(q, s))
                                products(i, q, s)

                            tokens_T(0, 0, 0)
                            list_tiles(act, tile)
                            act.wait_ge(gap_ready, 1)
                            flat = wt[:, :, :, :].rearrange("p r k t -> p (r k t)")
                            act.activation(flat, flat, ACT.Exp).then_inc(exp_ready, 1)

                        @block.vector
                        def _(dve):
                            one = Chain(dve, r1_step, 0)
                            one.turn(0)
                            pick(dve, one, 1, 0)
                            pick(dve, one, 2, 1)
                            choose(dve, one, chosen_ready)
                            for k in range(1, TOP):
                                one.step(dve.tensor_tensor(wt[:, :, k, :], wt[:, :, k, :], wt[:, :, 0, :], ALU.subtract),
                                         hold=False)
                            one.hold()
                            one.step(dve.memset(wt[:, :, 0, :], 0.0))
                            dve.sem_inc(gap_ready, 1)
                            dve.wait_ge(exp_ready, 1)
                            one.step(dve.tensor_tensor(den[:, :, :], wt[:, :, 0, :], wt[:, :, 1, :], ALU.add))
                            one.step(dve.tensor_tensor(den[:, :, :], den[:, :, :], wt[:, :, 2, :], ALU.add))
                            one.step(dve.reciprocal(den[:, :, :], den[:, :, :]))
                            for k in range(TOP):
                                one.step(dve.tensor_tensor(wt[:, :, k, :], wt[:, :, k, :], den[:, :, :], ALU.mult),
                                         hold=False)
                            one.hold()
                            for k in range(TOP):
                                one.step(dve.tensor_tensor(tmp[:, k], hot[:, 1, k], over(wt[:, 2, k, :]), ALU.mult),
                                         hold=False)
                            one.hold()
                            one.step(dve.tensor_tensor(dwb[:, :, :], tmp[:, 0], tmp[:, 1], ALU.add))
                            one.step(dve.tensor_tensor(dwb[:, :, :], dwb[:, :, :], tmp[:, 2], ALU.add))

                        @block.sync
                        def _(sp):
                            def store(i, q, s):
                                sp.wait_ge(po_ready, i + 1)
                                sp.dma_start(p1_d[i], po[:, s, :]).then_inc(po_stored[s], 16)

                            list_tiles(sp, store)
                            for s in range(QUAD):
                                sp.wait_ge(po_stored[s], 16 * uses(s))

                W2_FIRST = 3

                def load_w2(eng, e0, e1):
                    for e in range(e0, e1):
                        wait(eng, w2_ld, 16 * e)
                        eng.dma_start(W2[:, e], t["f_W2T"][e]).then_inc(w2_ld, 16)

                comb = ExitStack()
                with comb:
                    g = sb(comb, "f_g", [P, GR, TOP, HID])
                    hs = att[1][0][:, :, :, :].rearrange("p w k d -> p (w k d)").rearrange("p (s h) -> p s h", s=2)
                    ix = sb(comb, "f_ix", [P, GR, TOP], U32)
                    b2 = sb(comb, "f_b2", [E1, D])
                    dw3 = sb(comb, "f_dw3", [P, 2, E1])
                    dwT = sb(comb, "f_dwT", [E1, 2, P])
                    psD = ps(comb, "f_psD", [P, 2, BANK])
                    psB = ps(comb, "f_psB", [P, 2, BANK])
                    b2_ld = sem("f_b2_ld")
                    dw3_ready = sem("f_dw3_ready")
                    dwT_mm = sem("f_dwT_mm")
                    dwT_ready = sem("f_dwT_ready")
                    b_mm = sem("f_b_mm")
                    b_done = sem("f_b_done")
                    psN = ps(comb, "f2_psN", [P, BANK])
                    psF = ps(comb, "f2_psF", [P, BANK])
                    ix_ready = sem("f_ix_ready")
                    g_ld = [sem(f"f_g_ld{i}") for i in range(GR)]
                    s_step = sem("f_s_step")
                    r_step = sem("f2_r_step")
                    at_step = sem("f2_at_step")
                    count_mm = sem("f2_count_mm")
                    at_ready = sem("f2_at_ready")
                    at_used = sem("f2_at_used")
                    hs_ready = sem("f_hs_ready")
                    hs_stored = [sem(f"f_hs_stored{i}") for i in range(2)]
                    with nc.Block() as block:
                        @block.gpsimd
                        def _(pool):
                            def gather(i, s):
                                wait(pool, hs_ready, i - GR + 1)
                                pool.tensor_copy(ix[:, s, :], rows[:, :, i]).then_inc(ix_ready, 1)
                                pool.wait_ge(ix_ready, i + 1)
                                pool.nop(nofuse=True)
                                for k in range(TOP):
                                    pool.indirect_dma_start(
                                        g[:, s, k, :], None, p1_rows, bass.IndirectOffsetOnAxis(
                                            ap=ix[:, s, k:k + 1], axis=0)).then_inc(g_ld[s], 16)

                            for s in range(GR):
                                gather(s, s)
                            with pool.Fori(1, TT // GR) as q:
                                for s in range(GR):
                                    gather(GR * q + s, s)

                        @block.vector
                        def _(dve):
                            one = Chain(dve, r_step, 0)
                            one.turn(0)
                            lists(dve, one, 1, psN, count_mm)
                            sums = Chain(dve, s_step, GR * 2)
                            at = Chain(dve, at_step, GR * 2)

                            def tile(i, q, s):
                                dve.wait_ge(g_ld[s], 16 * TOP * (q + 1))
                                n = GR // 2 * q + s // 2
                                wait(dve, hs_stored[s % 2], 16 * n)
                                h = hs[:, s % 2, :]
                                sums.step(dve.tensor_scalar(h, g[:, s, 0, :], wt[:, 0, 0, bass.ds(i, 1)], None, ALU.mult))
                                sums.step(dve.scalar_tensor_tensor(h, g[:, s, 1, :], wt[:, 0, 1, bass.ds(i, 1)], h,
                                                                   ALU.mult, ALU.add))
                                dve.scalar_tensor_tensor(h, g[:, s, 2, :], wt[:, 0, 2, bass.ds(i, 1)], h,
                                                         ALU.mult, ALU.add).then_inc(hs_ready, 1)
                                match(dve, at, i, s % 2, at_used, at_ready)
                                dve.wait_ge(b_mm, i + 1)
                                dve.tensor_tensor(Xf[:, i, :], psB[:, s % 2, 0:D], Xf[:, i, :], ALU.add
                                                  ).then_inc(b_done, 1)

                            sums.turn(0)
                            at.turn(0)
                            for s in range(GR):
                                tile(s, 0, s)
                            with dve.Fori(1, TT // GR) as q:
                                sums.turn(q)
                                at.turn(q)
                                for s in range(GR):
                                    tile(GR * q + s, q, s)
                                sums.end()
                                at.end()
                            dve.wait_ge(b_done, TT)
                            dve.wait_ge(at_used, TT)
                            found_tokens(dve, one, 1, psF)

                        @block.tensor
                        def _(pe):
                            def pair(j, start, stop):
                                for s in range(2):
                                    pe.wait_ge(dw3_ready, 2 * j + s + 1)
                                    pe.transpose(psD[0:E1, s, 0:P], dw3[:, s, :], ident[:, :]).then_inc(dwT_mm, 1)
                                for s in range(2):
                                    i = 2 * j + s
                                    pe.wait_ge(dwT_ready, i + 1)
                                    wait(pe, b_done, i - 1)
                                    pe.matmul(psB[:, s, 0:D], dwT[:, s, :], b2[:, :], start=True, stop=True).then_inc(b_mm, 1)
                                    add_tokens(pe, i, s, psF, at_ready, at_used, start and s == 0, stop and s == 1)

                            count(pe, psN, chosen_ready, count_mm)
                            pe.wait_ge(b2_ld, 16)
                            pair(0, True, False)
                            with pe.Fori(1, TT // 2 - 1) as j:
                                pair(j, False, False)
                            pair(TT // 2 - 1, False, True)

                        @block.sync
                        def _(sp):
                            sp.dma_start(b2[:, :], t["f_b2"]).then_inc(b2_ld, 16)
                            with sp.Fori(0, TT // 2) as j:
                                for s in range(2):
                                    sp.wait_ge(hs_ready, 2 * j + s + 1)
                                    sp.dma_start(h_d[2 * j + s], hs[:, s, :]).then_inc(hs_stored[s], 16)
                            for s in range(2):
                                sp.wait_ge(hs_stored[s], 16 * (TT // 2))

                        @block.scalar
                        def _(act):
                            def pair(j):
                                for s in range(2):
                                    i = 2 * j + s
                                    wait(act, dwT_mm, i - 1)
                                    act.activation(dw3[:, s, :], dwb[:, i, :], ACT.Copy).then_inc(dw3_ready, 1)
                                for s in range(2):
                                    i = 2 * j + s
                                    act.wait_ge(dwT_mm, i + 1)
                                    wait(act, b_mm, i - 1)
                                    act.activation(dwT[:, s, :], psD[0:E1, s, 0:P], ACT.Copy).then_inc(dwT_ready, 1)

                            load_w2(act, 0, W2_FIRST)
                            pair(0)
                            with act.Fori(1, TT // 2) as j:
                                pair(j)

                sec = ExitStack()
                with sec:
                    hg = sb(sec, "f_hg", [P, QUAD, HID])
                    ix = sb(sec, "f2_ix", [P, QUAD], U32)
                    hT = sb(sec, "f_hT", [P, 2, KH, P])
                    yo = sb(sec, "f_yo", [P, QUAD, D])
                    ox = sb(sec, "f_ox", [P, QUAD], U32)
                    ox_ready = sem("f_ox_ready")
                    psT = ps(sec, "f2_psT", [P, 2, HID])
                    psY = ps(sec, "f2_psY", [P, 2, BANK])
                    ix_ready = sem("f2_ix_ready")
                    hg_ld = [sem(f"f_hg_ld{i}") for i in range(QUAD)]
                    hT_mm = sem("f_hT_mm")
                    hT_ready = sem("f_hT_ready")
                    y_mm = sem("f_y_mm")
                    yo_ready = sem("f_yo_ready")
                    yo_stored = [sem(f"f_yo_stored{i}") for i in range(QUAD)]
                    with nc.Block() as block:
                        @block.gpsimd
                        def _(pool):
                            def gather(i, q, s):
                                wait(pool, hT_mm, i - QUAD + 1)
                                pool.tensor_copy(ix[:, s:s + 1], toks[:, 1, bass.ds(i, 1)]).then_inc(ix_ready, 1)
                                pool.wait_ge(ix_ready, i + 1)
                                pool.nop(nofuse=True)
                                pool.indirect_dma_start(hg[:, s, :], None, h_rows, bass.IndirectOffsetOnAxis(
                                    ap=ix[:, s:s + 1], axis=0)).then_inc(hg_ld[s], 16)

                            def store(i, q, s):
                                pool.wait_ge(yo_ready, i + 1)
                                wait(pool, yo_stored[s], 16 * q)
                                pool.tensor_copy(ox[:, s:s + 1], dest[:, bass.ds(i, 1)]).then_inc(ox_ready, 1)
                                pool.wait_ge(ox_ready, i + 1)
                                pool.nop(nofuse=True)
                                pool.indirect_dma_start(p2_rows, bass.IndirectOffsetOnAxis(ap=ox[:, s:s + 1], axis=0),
                                                        yo[:, s, :], None).then_inc(yo_stored[s], 16)

                            def tile(i, q, s):
                                gather(i, q, s)
                                if not (isinstance(i, int) and i < QUAD):
                                    store(i - QUAD, q - 1, s)

                            list_tiles(pool, tile)
                            for i in range(LT - QUAD, LT):
                                store(i, i // QUAD, i % QUAD)
                            for s in range(QUAD):
                                pool.wait_ge(yo_stored[s], 16 * uses(s))

                        @block.tensor
                        def _(pe):
                            def turn(i, q, s):
                                pe.wait_ge(hg_ld[s], 16 * q + 16)
                                wait(pe, hT_ready, i - 1)
                                for k in range(KH):
                                    mm = pe.transpose(psT[:, s % 2, k * P:(k + 1) * P], hg[:, s, k * P:(k + 1) * P],
                                                      ident[:, :])
                                mm.then_inc(hT_mm, 1)

                            def multiply(i, q, s):
                                e = pe.value_load(owner[0:1, 1, bass.ds(i, 1)], min_val=0, max_val=E1 - 1)
                                pe.wait_ge(w2_ld, e * 16 + 16)
                                pe.wait_ge(hT_ready, i + 1)
                                wait(pe, yo_ready, i - 1)
                                for k in range(KH):
                                    mm = pe.matmul(psY[:, s % 2, 0:D], hT[:, s % 2, k, :], W2[:, e, k, :],
                                                   start=k == 0, stop=k == KH - 1)
                                mm.then_inc(y_mm, 1)

                            def tile(i, q, s):
                                if not (isinstance(i, int) and i == LT - 1):
                                    turn(i + 1, *following(q, s))
                                multiply(i, q, s)

                            turn(0, 0, 0)
                            list_tiles(pe, tile)

                        @block.scalar
                        def _(act):
                            def evacuate(i, q, s):
                                act.wait_ge(hT_mm, i + 1)
                                wait(act, y_mm, i - 1)
                                act.activation(hT[:, s % 2].rearrange("p k n -> p (k n)"), psT[:, s % 2, :], ACT.Gelu
                                               ).then_inc(hT_ready, 1)

                            list_tiles(act, evacuate)

                        @block.vector
                        def _(dve):
                            def evacuate(i, q, s):
                                dve.wait_ge(y_mm, i + 1)
                                wait(dve, yo_stored[s], 16 * q)
                                dve.tensor_copy(yo[:, s, :], psY[:, s % 2, 0:D]).then_inc(yo_ready, 1)

                            list_tiles(dve, evacuate)

                        @block.sync
                        def _(sp):
                            load_w2(sp, W2_FIRST, E1)

                fin = ExitStack()
                with fin:
                    g = sb(fin, "f_gy", [P, QUAD, TOP, D])
                    gy_ld = [sem(f"f_gy_ld{i}") for i in range(QUAD)]
                    o_step = sem("f_o_step")
                    o_ready = sem("f_o_ready")
                    stored = sem("f_stored")
                    with nc.Block() as block:
                        def quads(eng, body):
                            body(0)
                            with eng.Fori(1, TT // QUAD) as q:
                                body(q)

                        @block.sync
                        def _(sp):
                            def body(q):
                                for s in range(QUAD):
                                    i = QUAD * q + s
                                    wait(sp, o_ready, i - QUAD + 1)
                                    sp.dma_start(g[:, s], p2_d[i]).then_inc(gy_ld[s], 16)

                            quads(sp, body)

                        @block.vector
                        def _(dve):
                            adds = Chain(dve, o_step, QUAD * (TOP - 1))

                            def body(q):
                                adds.turn(q)
                                for pair in ((0, 1), (2, 3)):
                                    for s in pair:
                                        dve.wait_ge(gy_ld[s], 16 * (q + 1))
                                    for k in range(TOP):
                                        for s in pair:
                                            i = QUAD * q + s
                                            ins = dve.scalar_tensor_tensor(Xf[:, i, :], g[:, s, k, :],
                                                                           wt[:, 1, k, bass.ds(i, 1)], Xf[:, i, :],
                                                                           ALU.mult, ALU.add)
                                            if k < TOP - 1:
                                                adds.step(ins, hold=False)
                                            else:
                                                ins.then_inc(o_ready, 1)
                                        if k < TOP - 1:
                                            adds.hold()
                                adds.end()

                            quads(dve, body)

                        @block.scalar
                        def _(act):
                            with act.Fori(0, TT) as i:
                                act.wait_ge(o_ready, i + 1)
                                act.dma_start(out_tiles[i], Xf[:, i, :]).then_inc(stored, 16)
                            act.wait_ge(stored, 16 * TT)

        with a0_st, stage():
            attention("a0_", 0, True)
        with slots, stage():
            soft_mixture()
        W = sb(ctx, "W", [P, E1 * KD * HID])
        W1 = W[:, :].rearrange("p (e k h) -> p e k h", e=E1, k=KD)
        W2 = W[:, :].rearrange("p (e k d) -> p e k d", e=E1, k=KH)
        w1_ld = sem("f_w1_ld")
        w2_ld = sem("f_w2_ld")

        def load_w1(sp):
            for e in range(E1):
                sp.dma_start(W1[:, e], t["f_W1T"][e].rearrange("(k p) h -> p k h", p=P)).then_inc(w1_ld, 16)

        with stage():
            attention("a1_", 1, False, load_w1)
        with stage():
            top3_mixture(W1, W2, w1_ld, w2_ld)


def kernel(**inputs):
    import numpy as np
    import concourse.bacc as bacc
    from concourse.bass_utils import run_bass_kernel_spmd

    def flip(a):
        return np.ascontiguousarray(np.swapaxes(np.asarray(a), -1, -2))

    def keep(a):
        return np.ascontiguousarray(np.asarray(a))

    def columns(a):
        return flip(np.asarray(a).reshape(-1, P))

    def hidden(a):
        return keep(np.asarray(a).reshape(E0, KF, P).transpose(2, 0, 1))

    flat = np.arange(FLAT)
    hmv = np.zeros((P, NCH, VH), np.float32)
    for c in range(NCH):
        for v in range(VH):
            hmv[:CHR[c], c, v] = (flat[c * P:c * P + CHR[c]] // S2 == H0[c] + v)
    arrays = {
        "x": keep(inputs["x"]),
        "ctxT": flip(np.asarray(inputs["ctx_1024"]).reshape(B * S2, D)),
        "mask": keep(inputs["mask_1x1xSxS2_ik0"]),
        "a0_WqT": flip(inputs["L0_xattn_Wq"]), "a0_WkT": flip(inputs["L0_xattn_Wk"]),
        "a0_WvT": flip(inputs["L0_xattn_Wv"]), "a0_WoT": flip(inputs["L0_xattn_Wo"]),
        "a0_bq": columns(inputs["L0_xattn_bq"]), "a0_bk": columns(inputs["L0_xattn_bk"]),
        "a0_bv": keep(inputs["L0_xattn_bv"]), "a0_bo": keep(inputs["L0_xattn_bo"]),
        "a1_Wq": keep(inputs["L1_xattn_Wq"]), "a1_Wk": keep(inputs["L1_xattn_Wkv"][:, :D]),
        "a1_Wv": keep(inputs["L1_xattn_Wkv"][:, D:]), "a1_Wo": keep(inputs["L1_xattn_Wproj"]),
        "a1_bq": columns(inputs["L1_xattn_bq"]), "a1_bk": columns(inputs["L1_xattn_bkv"][:D]),
        "a1_bv": keep(inputs["L1_xattn_bkv"][D:]), "a1_bo": keep(inputs["L1_xattn_bproj"]),
        "m_ng": keep(inputs["L0_ffn_norm_g"]), "m_nb": keep(inputs["L0_ffn_norm_b"]),
        "m_sg": keep(inputs["L0_ffn_slot_g"]), "m_sb": keep(inputs["L0_ffn_slot_b"]),
        "m_scale": keep(inputs["L0_ffn_scale"]),
        "m_se": keep(np.asarray(inputs["L0_ffn_slot_embeds"]).reshape(NS, D)),
        "m_Wg": keep(inputs["L0_ffn_Wg"]), "m_Wu": keep(inputs["L0_ffn_Wu"]), "m_Wd": keep(inputs["L0_ffn_Wd"]),
        "m_bgT": hidden(inputs["L0_ffn_bg"]), "m_buT": hidden(inputs["L0_ffn_bu"]), "m_bd": keep(inputs["L0_ffn_bd"]),
        "f_PwT": flip(inputs["L1_ffn_P_w"]),
        "f_UT": flip(np.concatenate([np.asarray(inputs["L1_ffn_U%d" % i]) for i in (1, 2, 3)])),
        "f_W1T": flip(inputs["L1_ffn_W1"]),
        "f_W2T": keep(np.asarray(inputs["L1_ffn_W2"]).reshape(E1, D, KH, P).transpose(0, 3, 2, 1)),
        "f_b2": keep(inputs["L1_ffn_b2"]),
        "c_iota": np.arange(P, dtype=np.float32),
        "c_below": np.triu(np.ones((P, P), np.float32), 1),
        "c_tokid": np.ascontiguousarray(np.arange(1, 1 + B * N * TOP, dtype=np.float32).reshape(TOP, B * NT, P).transpose(2, 1, 0)),
        "c_spare": np.arange(1 + B * N * TOP, 1 + B * N * TOP + LT * P, dtype=np.float32).reshape(LT, P).T.copy(),
        "c_ident": np.eye(P, dtype=np.float32),
        "c_sel": (flat[None, :] % S2 == np.arange(S2)[:, None]).astype(np.float32),
        "c_hmk": (np.arange(P)[:, None] // DK == np.arange(HC)[None, :]).astype(np.float32),
        "c_hmv": hmv.reshape(P, NCH * VH),
    }
    nc = bacc.Bacc("TRN2", target_bir_lowering=False, num_devices=1)
    aps = {n: nc.dram_tensor("in_" + n, a.shape, mybir.dt.from_np(a.dtype), kind="ExternalInput").ap()
           for n, a in arrays.items()}
    out = nc.dram_tensor("out", (B, N, D), F32, kind="ExternalOutput").ap()
    build(nc, aps, out)
    r = run_bass_kernel_spmd(nc, [{"in_" + n: a for n, a in arrays.items()}], core_ids=[0])
    return r.results[0]["out"]
```

```python
from contextlib import ExitStack, contextmanager

import concourse.bass as bass
from concourse import mybir

ALU = mybir.AluOpType
ACT = mybir.ActivationFunctionType
AX = mybir.AxisListType
F32 = mybir.dt.float32
BF16 = mybir.dt.bfloat16
I32 = mybir.dt.int32
U32 = mybir.dt.uint32

P = 128
B = 2
N = 1024
D = 256
KD = D // P
NT = N // P
S2 = 77
H = 16
DK = D // H
HC = H // KD
HG = 4
NG = H // HG
BANK = 512
FLAT = H * S2
NCH = -(-FLAT // P)
CHR = [min(P, FLAT - c * P) for c in range(NCH)]
VH = 3
VC = DK + 1
H0 = [min(c * P // S2, H - VH) for c in range(NCH)]
VCH = B * VH * VC
CPB = BANK // VCH
VPARTS = [(P, 0, CPB), (P, CPB, NCH - 1), (CHR[-1], NCH - 1, NCH)]
EPS = 1e-5
PTG = [range(0, 2), range(2, 6), range(6, NCH)]
E0, SL, F0 = 16, 64, 512
NS = E0 * SL
CS = NS // P
KF = F0 // P
E1, HID = 12, 1024
TOP = 3
LT = (B * N * TOP + E1 * (P - 1)) // P
R = 3
DA = 64
KH = HID // P
RING = 4
DIGIT = 32
AR = 4
GR = 4
SCALE = 0.25
NEG = -1.0e9
BIG = 3.0e38


def wait(eng, sem, value):
    if isinstance(value, int) and value <= 0:
        return
    eng.wait_ge(sem, value)


def before(j, s, n, slots=2):
    return (j, s - n) if s >= n else (j - 1, s - n + slots)


def after(j, s, n, slots=2):
    return (j, s + n) if s + n < slots else (j + 1, s + n - slots)


def tile_steps(eng, turns, step, slots=2):
    for s in range(slots):
        step(0, s, s >= 1, True, True)
    with eng.Fori(1, turns - 1) as j:
        for s in range(slots):
            step(j, s, True, True, True)
    for s in range(slots):
        step(turns - 1, s, True, s < slots - 1, s < slots - 2)


class Chain:

    def __init__(self, eng, sem, per_turn):
        self.eng, self.sem, self.per_turn = eng, sem, per_turn

    def turn(self, i):
        self.base, self.n = i * self.per_turn, 0

    def step(self, ins, hold=True):
        ins.then_inc(self.sem, 1)
        self.n += 1
        if hold:
            self.eng.wait_ge(self.sem, self.base + self.n)

    def hold(self):
        self.eng.wait_ge(self.sem, self.base + self.n)

    def end(self):
        assert self.n == self.per_turn, (self.n, self.per_turn)


def build(nc, t, out):
    xn_d = nc.dram_tensor("xn_d", (B * N, D), F32, kind="Internal").ap()
    p1_rows = nc.dram_tensor("p1_d", (LT * P, HID), F32, kind="Internal").ap()
    p1_d = p1_rows.rearrange("(i p) h -> i p h", p=P)
    h_rows = nc.dram_tensor("h_d", (B * N, HID), F32, kind="Internal").ap()
    h_d = h_rows.rearrange("(i p) h -> i p h", p=P)
    p2_rows = nc.dram_tensor("p2_d", (B * N * TOP + LT * P, D), F32, kind="Internal").ap()
    p2_d = p2_rows[0:B * N * TOP, :].rearrange("(k i p) d -> i p k d", k=TOP, p=P)
    out_tiles = out.rearrange("b (t p) d -> (b t) p d", p=P)
    ctx = ExitStack()

    def sb(stack, name, shape, dt=F32):
        return stack.enter_context(nc.sbuf_tensor(name, shape, dt))

    def ps(stack, name, shape):
        return stack.enter_context(nc.psum_tensor(name, shape, F32))

    scopes = [(ctx, [])]

    def sem(name):
        stack, names = scopes[-1]
        names.append(stack.enter_context(nc.semaphore(name)))
        return names[-1]

    @contextmanager
    def stage():
        scopes.append((ExitStack(), []))
        yield
        stack, names = scopes.pop()
        with nc.Block() as block:
            @block.sync
            def _(sp):
                for n in names:
                    sp.sem_clear(n)
        stack.close()

    with ctx:
        X = sb(ctx, "X", [P, B, NT, D])
        ident = sb(ctx, "ident", [P, P])
        ones = sb(ctx, "ones", [1, P])
        ctxT = sb(ctx, "ctxT", [P, KD, B * S2])
        sel = sb(ctx, "sel", [P, FLAT])
        hmk = sb(ctx, "hmk", [P, HC])
        hmv = sb(ctx, "hmv", [P, NCH * VH])

        def attention_weights(stack, a):
            w = sb(stack, a + "W", [P, 4, KD, D])
            return [w] + [w[:, i] for i in range(4)] + [sb(stack, a + n, shape) for n, shape in (
                ("bk", [P, KD]), ("bq", [P, KD]), ("bvr", [1, D]))]

        loaded_x = sem("loaded_x")
        loaded_const = sem("loaded_const")
        loaded_se = sem("loaded_se")
        loaded_gains = sem("loaded_gains")
        loaded_att = [sem("loaded_a0"), sem("loaded_a1")]
        ones_ready = sem("ones_ready")
        N_CONST, N_SE, N_ATT = 5, 5, 7
        a1_weights = attention_weights(ctx, "a1_")
        TT = B * NT
        stats = sb(ctx, "stats", [P, TT, 6])
        mean = sb(ctx, "mean", [P, TT])
        mdif = sb(ctx, "mdif", [P, TT])
        rstd = sb(ctx, "rstd", [P, TT])
        veps = sb(ctx, "veps", [P, TT])
        mhalf = sb(ctx, "mhalf", [P, TT])
        vars_ = sb(ctx, "vars", [P, TT])
        slots = ExitStack()
        seT = sb(slots, "m_seT", [P, KD, NS])
        gains = sb(slots, "m_gains", [P, 2, D])
        a0_st = ExitStack()
        att = [attention_weights(a0_st, "a0_"), a1_weights]
        se_st = ExitStack()
        sgains = sb(se_st, "m_sgains", [P, 2, D])
        SE = sb(se_st, "m_SE", [P, CS, D])
        scl = sb(se_st, "m_scl", [P, 1])

        def slot_loads(act):
            act.dma_start(SE[:, :, :], t["m_se"].rearrange("(c p) d -> p c d", p=P)).then_inc(loaded_se, 16)
            for place, n in zip((sgains[:, 0], sgains[:, 1], gains[:, 0], gains[:, 1]), ("m_sg", "m_sb", "m_ng", "m_nb")):
                act.dma_start(place, t[n].partition_broadcast(P)).then_inc(loaded_gains, 16)
            act.dma_start(scl[:, :], t["m_scale"].partition_broadcast(P)).then_inc(loaded_gains, 16)

        def input_loads(sp):
            def attention_loads(l):
                a = f"a{l}_"
                T = "T" if l == 0 else ""
                for w, n in zip(att[l][1:5], ("Wk", "Wv", "Wq", "Wo")):
                    sp.dma_start(w[:, :, :], t[a + n + T].rearrange("(k p) n -> p k n", p=P)).then_inc(loaded_att[l], 16)
                for w, n in zip(att[l][5:7], ("bk", "bq")):
                    sp.dma_start(w[:, :], t[a + n]).then_inc(loaded_att[l], 16)
                sp.dma_start(att[l][7][:, :], t[a + "bv"].rearrange("(a d) -> a d", a=1)).then_inc(loaded_att[l], 16)

            sp.dma_start(ctxT[:, :, :], t["ctxT"].rearrange("(k p) n -> p k n", p=P)).then_inc(loaded_const, 16)
            sp.dma_start(sel[0:S2, :], t["c_sel"]).then_inc(loaded_const, 16)
            sp.dma_start(hmk[:, :], t["c_hmk"]).then_inc(loaded_const, 16)
            sp.dma_start(hmv[:, :], t["c_hmv"]).then_inc(loaded_const, 16)
            sp.dma_start(ident[:, :], t["c_ident"]).then_inc(loaded_const, 16)
            attention_loads(0)
            for b in range(B):
                sp.dma_start(X[:, b], t["x"][b].rearrange("(t p) d -> p t d", p=P)).then_inc(loaded_x, 16)
            return lambda: attention_loads(1)

        def bn_tiles(dve, rows, n, done):
            with dve.Fori(0, n // 4) as q:
                for i in range(4):
                    dve.bn_stats(stats[:, q * 4 + i, :], rows[:, q * 4 + i, :]).then_inc(done, 1)
            dve.wait_ge(done, n)

        def norm_factors(a, n, twice=False):
            var = sem(a + "var")
            inv = sem(a + "inv")

            def begin(dve):
                me, ve, mo, vo = (stats[:, 0:n, i] for i in (1, 2, 4, 5))
                dve.memset(mhalf[:, 0:n], -0.5).then_inc(var, 1)
                dve.tensor_tensor(mean[:, 0:n], me, mo, ALU.add).then_inc(var, 1)
                dve.tensor_tensor(mdif[:, 0:n], me, mo, ALU.subtract).then_inc(var, 1)
                dve.tensor_tensor(veps[:, 0:n], ve, vo, ALU.add).then_inc(var, 1)
                dve.wait_ge(var, 4)
                dve.tensor_scalar(mean[:, 0:n], mean[:, 0:n], 0.5, None, ALU.mult).then_inc(var, 1)
                dve.scalar_tensor_tensor(mdif[:, 0:n], mdif[:, 0:n], 0.25, mdif[:, 0:n], ALU.mult, ALU.mult
                                         ).then_inc(var, 1)
                dve.wait_ge(var, 6)
                dve.scalar_tensor_tensor(vars_[:, 0:n], veps[:, 0:n], 1.0 / D, mdif[:, 0:n], ALU.mult, ALU.add
                                         ).then_inc(var, 1)
                dve.wait_ge(var, 7)
                scale, offset = (1 + EPS, EPS * EPS) if twice else (1.0, EPS)
                dve.tensor_scalar(veps[:, 0:n], vars_[:, 0:n], scale, offset, ALU.mult, ALU.add).then_inc(var, 1)

            def end(dve):
                dve.wait_ge(inv, 1)

            def power(pool):
                pool.wait_ge(var, 8)
                pool.tensor_tensor(rstd[:, 0:n], veps[:, 0:n], mhalf[:, 0:n], ALU.pow).then_inc(inv, 1)

            return begin, end, power

        def slot_embeddings():
            begin, end, power = norm_factors("ms_", CS)
            se_stat = sem("m_se_stat")
            se_step = sem("m_se_step")
            se_ready = sem("m_se_ready")
            se_mm = sem("m_se_mm")
            seT_ready = sem("m_seT_ready")

            def vector(dve):
                dve.wait_ge(loaded_se, 16)
                bn_tiles(dve, SE, CS, se_stat)
                begin(dve)
                dve.wait_ge(loaded_gains, 16 * N_SE)
                for i in range(2):
                    dve.tensor_scalar(sgains[:, i, :], sgains[:, i, :], scl[:, :], None, ALU.mult).then_inc(se_step, 1)
                end(dve)
                for c in range(CS):
                    dve.tensor_scalar(SE[:, c], SE[:, c], mean[:, c:c + 1], rstd[:, c:c + 1],
                                      ALU.subtract, ALU.mult).then_inc(se_step, 1)
                dve.wait_ge(se_step, 2 + CS)

            def affine(pool):
                power(pool)
                pool.wait_ge(se_step, 2 + CS)
                pool.tensor_tensor(SE[:, :, :], SE[:, :, :], sgains[:, 0:1, :].to_broadcast([P, CS, D]),
                                   ALU.mult).then_inc(se_step, 1)
                pool.wait_ge(se_step, 2 + CS + 1)
                pool.tensor_tensor(SE[:, :, :], SE[:, :, :], sgains[:, 1:2, :].to_broadcast([P, CS, D]),
                                   ALU.add).then_inc(se_ready, 1)

            def tensor(pe, banks):
                pe.wait_ge(se_ready, 1)
                for k in range(KD):
                    for c in range(CS):
                        mm = pe.transpose(banks[:, k, c * P:(c + 1) * P], SE[:, c, k * P:(k + 1) * P], ident[:, :])
                mm.then_inc(se_mm, 1)

            def scalar(act, banks):
                act.wait_ge(se_mm, 1)
                for k in range(KD):
                    act.activation(seT[:, k, :], banks[:, k, :], ACT.Copy).then_inc(seT_ready, 1)
                act.wait_ge(seT_ready, KD)

            return vector, tensor, scalar, affine

        def attention(a, layer, masked, first=False, prefetch=None):
            _, Wk, Wv, Wq, Wo, bkc, bqc, bvr = att[layer]
            st = ExitStack()
            with st:
                bob = sb(st, a + "bob", [P, D])
                kT = sb(st, a + "kT", [P, KD, B * S2])
                kblk = sb(st, a + "kblk", [P, B, KD, HC, S2])
                vsb = sb(st, a + "vsb", [P, B, H, VC])
                vblk = sb(st, a + "vblk", [P, B, NCH, VH * VC])
                xn = sb(st, a + "xn", [P, B, D])
                xnT = sb(st, a + "xnT", [P, B, KD, P])
                qT = sb(st, a + "qT", [P, B, KD, P])
                sc = sb(st, a + "sc", [P, B, H, S2])
                pr = sb(st, a + "pr", [P, B, FLAT])
                mx = sb(st, a + "mx", [P, B, H])
                rsum = sb(st, a + "rsum", [P, B, H])
                pT = sb(st, a + "pT", [P, B, NCH, P])
                o = sb(st, a + "o", [P, B, H, DK])
                oT = sb(st, a + "oT", [P, B, KD, P])
                if masked:
                    mi = sb(st, a + "mi", [P, NT, S2], I32)
                    cap = sb(st, a + "cap", [P, NT, S2])
                psS = ps(st, a + "psS", [P, NG, BANK])
                psA = ps(st, a + "psA", [P, 2, 2 * P])
                psP = ps(st, a + "psP", [P, 2, BANK])
                psO = ps(st, a + "psO", [P, BANK])

                mask_ld = sem(a + "mask_ld")
                bob_ld = sem(a + "bob_ld")
                kv_mm = sem(a + "kv_mm")
                kv_sb = sem(a + "kv_sb")
                kv_blk = sem(a + "kv_blk")
                cap_step = sem(a + "cap_step")

                begin, end, power = norm_factors(a, TT)
                banks = psS[:, :, :].rearrange("p g n -> p (g n)").rearrange("p (k n) -> p k n", k=KD)
                if first:
                    se_vector, se_tensor, se_scalar, se_affine = slot_embeddings()
                with nc.Block() as block:
                    @block.sync
                    def _(sp):
                        if first:
                            later_loads = input_loads(sp)
                        sp.dma_start(bob[:, :], t[a + "bo"].partition_broadcast(P)).then_inc(bob_ld, 16)
                        if masked:
                            sp.dma_start(mi[:, :, :], t["mask"].rearrange("a b (t p) k -> p (a b t) k", p=P)
                                         ).then_inc(mask_ld, 16)
                        if first:
                            later_loads()
                        if prefetch is not None:
                            prefetch(sp)

                    @block.tensor
                    def _(pe):
                        pe.wait_ge(ones_ready, 1)
                        pe.wait_ge(loaded_const, 16 * N_CONST)
                        pe.wait_ge(loaded_att[layer], 16 * N_ATT)
                        for m in range(KD):
                            for k in range(KD):
                                mm = pe.matmul(psA[:, m, 0:B * S2], Wk[:, k, m * P:(m + 1) * P], ctxT[:, k, :],
                                               start=k == 0, stop=k == KD - 1)
                        mm.then_inc(kv_mm, 1)
                        for b in range(B):
                            for k in range(KD):
                                pe.matmul(psO[0:S2, b * D:(b + 1) * D], ctxT[:, k, b * S2:(b + 1) * S2], Wv[:, k, :],
                                          start=k == 0, stop=False)
                            mm = pe.matmul(psO[0:S2, b * D:(b + 1) * D], ones[0:1, 0:S2], bvr[:, :], start=False, stop=True)
                        mm.then_inc(kv_mm, 1)
                        pe.wait_ge(kv_sb, 2 + KD + B)
                        for c in range(NCH):
                            mm = pe.matmul(psP[0:CHR[c], c // CPB, c % CPB * VCH:(c % CPB + 1) * VCH],
                                           sel[0:S2, c * P:c * P + CHR[c]],
                                           vsb[0:S2, :, H0[c]:H0[c] + VH, :], start=True, stop=True)
                        mm.then_inc(kv_mm, 1)
                        if first:
                            se_tensor(pe, banks)

                    @block.vector
                    def _(dve):
                        if first:
                            dve.memset(ones[:, :], 1.0).then_inc(ones_ready, 1)
                            se_vector(dve)
                        else:
                            begin(dve)
                        dve.memset(vsb[:, :, :, DK:VC], 1.0).then_inc(kv_sb, 1)
                        dve.memset(vblk[:, :, NCH - 1, :], 0.0).then_inc(kv_sb, 1)
                        dve.wait_ge(loaded_const, 16 * N_CONST)
                        dve.wait_ge(loaded_att[layer], 16 * N_ATT)
                        dve.wait_ge(kv_mm, 1)
                        for m in range(KD):
                            dve.tensor_scalar(kT[:, m, :], psA[:, m, 0:B * S2], bkc[:, m:m + 1], SCALE,
                                              ALU.add, ALU.mult).then_inc(kv_sb, 1)
                        dve.wait_ge(kv_sb, 2 + KD)
                        for b in range(B):
                            for m in range(KD):
                                dve.tensor_tensor(
                                    kblk[:, b, m], kT[:, m:m + 1, b * S2:(b + 1) * S2].to_broadcast([P, HC, S2]),
                                    hmk[:, :].unsqueeze(2).to_broadcast([P, HC, S2]), ALU.mult).then_inc(kv_blk, 1)
                        dve.wait_ge(kv_mm, 2)
                        for b in range(B):
                            dve.tensor_copy(vsb[0:S2, b, :, 0:DK],
                                            psO[0:S2, b * D:(b + 1) * D].rearrange("p (h d) -> p h d", h=H)).then_inc(kv_sb, 1)
                        if first:
                            dve.wait_ge(loaded_x, 16 * B)
                            bn_tiles(dve, X[:, :, :, :].rearrange("p b t d -> p (b t) d"), TT, sem("x_stat"))
                            begin(dve)
                        if masked:
                            dve.wait_ge(mask_ld, 16)
                            dve.tensor_scalar(cap[:, :, :], mi[:, :, :], 0, BIG, ALU.not_equal, ALU.mult
                                              ).then_inc(cap_step, 1)
                            dve.wait_ge(cap_step, 1)
                            dve.tensor_scalar(cap[:, :, :], cap[:, :, :], NEG, None, ALU.add).then_inc(cap_step, 1)
                            dve.wait_ge(cap_step, 2)
                        dve.wait_ge(kv_mm, 3)
                        for b in range(B):
                            for rows, c0, c1 in VPARTS:
                                n = c1 - c0
                                spread = psP[0:rows, c0 // CPB, c0 % CPB * VCH:(c0 % CPB + n) * VCH]
                                dve.tensor_tensor(
                                    vblk[0:rows, b, c0:c1, :].rearrange("p c (h v) -> p c h v", v=VC),
                                    spread.rearrange("p (c b h v) -> p c b h v", b=B, h=VH, v=VC)[:, :, b],
                                    hmv[0:rows, c0 * VH:c1 * VH].rearrange("p (c h) -> p c h", h=VH).unsqueeze(3)
                                    .to_broadcast([rows, n, VH, VC]), ALU.mult).then_inc(kv_blk, 1)
                        dve.wait_ge(kv_blk, (KD + len(VPARTS)) * B)
                        end(dve)

                    @block.scalar
                    def _(act):
                        if first:
                            slot_loads(act)
                            se_scalar(act, banks)

                    @block.gpsimd
                    def _(pool):
                        if first:
                            se_affine(pool)
                        power(pool)

                xn_ready = sem(a + "xn_ready")
                xT_mm = sem(a + "xT_mm")
                xT_ready = sem(a + "xT_ready")
                q_mm = sem(a + "q_mm")
                q_ready = sem(a + "q_ready")
                s_mm = sem(a + "s_mm")
                s_read = sem(a + "s_read")
                s_ready = sem(a + "s_ready")
                p_ready = sem(a + "p_ready")
                pT_mm = sem(a + "pT_mm")
                pT_ready = sem(a + "pT_ready")
                pv_mm = sem(a + "pv_mm")
                o_ready = sem(a + "o_ready")
                y_mm = sem(a + "y_mm")
                y_done = sem(a + "y_done")
                front_step = sem(a + "front_step")
                back_step = sem(a + "back_step")
                oT_mm = sem(a + "oT_mm")
                oT_ready = sem(a + "oT_ready")
                stat_done = sem(a + "stat_done")
                xb_ready = sem(a + "xb_ready")

                with nc.Block() as block:
                    def steps(eng, step):
                        for j in range(2):
                            for s in range(B):
                                step(j, s, B * j + s >= 1, j >= 1, True, True)
                        with eng.Fori(2, NT - 1) as j:
                            for s in range(B):
                                step(j, s, True, True, True, True)
                        for s in range(B):
                            step(NT - 1, s, True, True, s < B - 1, False)

                    @block.vector
                    def _(dve):
                        front = Chain(dve, front_step, 3 if masked else 2)
                        back = Chain(dve, back_step, 1)

                        def norm_in(j, s, u):
                            i = s * NT + j
                            wait(dve, xT_mm, u - 1)
                            dve.tensor_scalar(xn[:, s], X[:, s, j], mean[:, bass.ds(i, 1)], rstd[:, bass.ds(i, 1)],
                                              ALU.subtract, ALU.mult).then_inc(xn_ready, 1)

                        def softmax_in(j, s, u):
                            front.turn(u)
                            raw = psS[:, :, 0:HG * S2].rearrange("p g (h k) -> p g h k", h=HG)
                            rs = sc[:, s].rearrange("p (g h) k -> p g h k", g=NG)
                            mxs = mx[:, s].rearrange("p (g h) -> p g h", g=NG)
                            wait(dve, p_ready, u - 1)
                            src = raw
                            for g in range(NG):
                                dve.wait_ge(s_mm, NG * u + g + 1)
                                if masked:
                                    ins = dve.tensor_tensor(rs[:, g], raw[:, g],
                                                            cap[:, j].unsqueeze(1).to_broadcast([P, HG, S2]), ALU.min)
                                else:
                                    ins = dve.tensor_reduce(mxs[:, g], raw[:, g], AX.X, ALU.max)
                            front.step(ins)
                            if masked:
                                dve.sem_inc(s_read, 1)
                                src = rs
                                front.step(dve.tensor_reduce(mxs, src, AX.X, ALU.max))
                            ins = dve.tensor_tensor(
                                rs, src, mx[:, s].rearrange("p (g h) -> p g h", g=NG).unsqueeze(3)
                                .to_broadcast([P, NG, HG, S2]), ALU.subtract)
                            front.step(ins)
                            if not masked:
                                dve.sem_inc(s_read, 1)
                            dve.sem_inc(s_ready, 1)

                        def normalise(j, s, u):
                            back.turn(u)
                            dve.wait_ge(pv_mm, u + 1)
                            acc = psO[:, 0:H * VC].rearrange("p (h v) -> p h v", v=VC)
                            wait(dve, o_ready, u - 1)
                            back.step(dve.reciprocal(rsum[:, s, :].unsqueeze(2), acc[:, :, DK:VC]))
                            wait(dve, oT_mm, u - 1)
                            dve.tensor_tensor(o[:, s], acc[:, :, 0:DK],
                                              rsum[:, s, :].unsqueeze(2).to_broadcast([P, H, DK]), ALU.mult
                                              ).then_inc(o_ready, 1)

                        def residual(j, s, u):
                            dve.wait_ge(y_mm, u + 1)
                            dve.wait_ge(xb_ready, u + 1)
                            dve.tensor_tensor(X[:, s, j], psP[:, 1, 0:D], X[:, s, j], ALU.add).then_inc(y_done, 1)

                        def stat(j, s, u):
                            dve.wait_ge(y_done, u + 1)
                            dve.bn_stats(stats[:, s * NT + j, :], X[:, s, j]).then_inc(stat_done, 1)

                        def step(j, s, v, w, n, a):
                            u = B * j + s
                            softmax_in(j, s, u)
                            if v:
                                normalise(*before(j, s, 1), u - 1)
                            if a:
                                norm_in(*after(j, s, 2), u + 2)
                            if w:
                                residual(*before(j, s, 2), u - 2)
                                stat(*before(j, s, 2), u - 2)

                        for s in range(B):
                            norm_in(0, s, s)
                        steps(dve, step)
                        U = B * NT
                        normalise(NT - 1, B - 1, U - 1)
                        for s in range(B):
                            residual(NT - 1, s, U - B + s)
                            stat(NT - 1, s, U - B + s)
                        dve.wait_ge(stat_done, U)

                    @block.gpsimd
                    def _(pool):
                        pool.wait_ge(bob_ld, 16)
                        with pool.Fori(0, NT) as j:
                            for s in range(B):
                                pool.wait_ge(xn_ready, B * j + s + 1)
                                pool.tensor_tensor(X[:, s, j], X[:, s, j], bob[:, :], ALU.add).then_inc(xb_ready, 1)

                    @block.scalar
                    def _(act):
                        def input_T(j, s, u):
                            act.wait_ge(xT_mm, u + 1)
                            wait(act, q_mm, u - 1)
                            act.activation(xnT[:, s].rearrange("p k n -> p (k n)"), psA[:, 0, :], ACT.Copy
                                           ).then_inc(xT_ready, 1)

                        def queries(j, s, u):
                            act.wait_ge(q_mm, u + 1)
                            wait(act, s_mm, NG * (u - 1))
                            for m in range(KD):
                                ins = act.activation(qT[:, s, m, :], psA[:, 1, m * P:(m + 1) * P], ACT.Identity,
                                                     bias=bqc[:, m:m + 1])
                            ins.then_inc(q_ready, 1)

                        def exponent(j, s, u):
                            act.wait_ge(s_ready, u + 1)
                            wait(act, pT_mm, 3 * (u - 1))
                            act.activation(pr[:, s, :], sc[:, s].rearrange("p h k -> p (h k)"), ACT.Exp
                                           ).then_inc(p_ready, 1)

                        def probs_T(j, s, u, g):
                            cs = PTG[g]
                            act.wait_ge(pT_mm, 3 * u + g + 1)
                            wait(act, pv_mm, u - 1)
                            full = [c for c in cs if CHR[c] == P]
                            act.activation(pT[:, s, full[0]:full[-1] + 1, :].rearrange("p c n -> p (c n)"),
                                           psP[:, g % 2 if g < 2 else 1, 0:len(full) * P], ACT.Copy).then_inc(pT_ready, 1)
                            for c in cs:
                                if CHR[c] < P:
                                    act.activation(pT[0:CHR[c], s, c, :],
                                                   psP[0:CHR[c], 1, (c - cs[0]) * P:(c - cs[0] + 1) * P],
                                                   ACT.Copy).then_inc(pT_ready, 1)

                        def output_T(j, s, u):
                            act.wait_ge(oT_mm, u + 1)
                            wait(act, y_mm, u - 1)
                            act.activation(oT[:, s].rearrange("p k n -> p (k n)"), psP[:, 0, 0:KD * P], ACT.Copy
                                           ).then_inc(oT_ready, 1)

                        def step(j, s, v, w, n, a):
                            u = B * j + s
                            if v:
                                probs_T(*before(j, s, 1), u - 1, 0)
                                probs_T(*before(j, s, 1), u - 1, 1)
                            if n:
                                input_T(*after(j, s, 1), u + 1)
                            if w:
                                output_T(*before(j, s, 2), u - 2)
                            if v:
                                probs_T(*before(j, s, 1), u - 1, 2)
                            if n:
                                queries(*after(j, s, 1), u + 1)
                            exponent(j, s, u)

                        input_T(0, 0, 0)
                        queries(0, 0, 0)
                        steps(act, step)
                        U = B * NT
                        probs_T(NT - 1, B - 1, U - 1, 0)
                        probs_T(NT - 1, B - 1, U - 1, 1)
                        output_T(NT - 1, 0, U - 2)
                        probs_T(NT - 1, B - 1, U - 1, 2)
                        output_T(NT - 1, B - 1, U - 1)

                    @block.tensor
                    def _(pe):
                        EV = [1, 2, 4]

                        def input_T(j, s, u):
                            pe.wait_ge(xn_ready, u + 1)
                            wait(pe, q_ready, u)
                            for k in range(KD):
                                mm = pe.transpose(psA[:, 0, k * P:(k + 1) * P], xn[:, s, k * P:(k + 1) * P], ident[:, :])
                            mm.then_inc(xT_mm, 1)

                        def queries(j, s, u):
                            pe.wait_ge(xT_ready, u + 1)
                            for m in range(KD):
                                for k in range(KD):
                                    mm = pe.matmul(psA[:, 1, m * P:(m + 1) * P], Wq[:, k, m * P:(m + 1) * P],
                                                   xnT[:, s, k, :], start=k == 0, stop=k == KD - 1)
                            mm.then_inc(q_mm, 1)

                        def scores(j, s, u):
                            pe.wait_ge(q_ready, u + 1)
                            wait(pe, s_read, u)
                            for g in range(NG):
                                m, h = divmod(g * HG, HC)
                                pe.matmul(psS[:, g, 0:HG * S2], qT[:, s, m, :], kblk[:, s, m, h:h + HG, :],
                                          start=True, stop=True).then_inc(s_mm, 1)

                        def probs_T(j, s, u, g):
                            if g == 0:
                                pe.wait_ge(p_ready, u + 1)
                                wait(pe, oT_ready, u - 1)
                            if g == 1:
                                wait(pe, pT_ready, 4 * u)
                                wait(pe, y_done, u - 1)
                            if g == 2:
                                pe.wait_ge(pT_ready, 4 * u + EV[1])
                            cs = PTG[g]
                            for c in cs:
                                mm = pe.transpose(psP[0:CHR[c], g if g < 2 else 1, (c - cs[0]) * P:(c - cs[0] + 1) * P],
                                                  pr[:, s, c * P:c * P + CHR[c]], ident[:, :])
                            mm.then_inc(pT_mm, 1)

                        def values(j, s, u, g):
                            if g == 0:
                                wait(pe, o_ready, u)
                            pe.wait_ge(pT_ready, 4 * u + EV[g])
                            for c in PTG[g]:
                                mm = pe.matmul(psO[:, H0[c] * VC:(H0[c] + VH) * VC], pT[0:CHR[c], s, c, :],
                                               vblk[0:CHR[c], s, c, :], start=c == 0, stop=c == NCH - 1,
                                               skip_group_check=True)
                            if g == len(PTG) - 1:
                                mm.then_inc(pv_mm, 1)

                        def output_T(j, s, u, ev):
                            pe.wait_ge(o_ready, u + 1)
                            pe.wait_ge(pT_ready, ev)
                            for k in range(KD):
                                mm = pe.transpose(psP[:, 0, k * P:(k + 1) * P], o[:, s, k * HC:(k + 1) * HC, :],
                                                  ident[:, :])
                            mm.then_inc(oT_mm, 1)

                        def project(j, s, u, ev):
                            pe.wait_ge(oT_ready, u + 1)
                            pe.wait_ge(pT_ready, ev)
                            for k in range(KD):
                                mm = pe.matmul(psP[:, 1, 0:D], oT[:, s, k, :], Wo[:, k, :], start=k == 0, stop=k == KD - 1)
                            mm.then_inc(y_mm, 1)

                        def step(j, s, v, w, n, a):
                            u = B * j + s
                            scores(j, s, u)
                            if v:
                                probs_T(*before(j, s, 1), u - 1, 0)
                                probs_T(*before(j, s, 1), u - 1, 1)
                            if n:
                                input_T(*after(j, s, 1), u + 1)
                            if w:
                                output_T(*before(j, s, 2), u - 2, 4 * (u - 1) + EV[0])
                            if v:
                                values(*before(j, s, 1), u - 1, 0)
                                probs_T(*before(j, s, 1), u - 1, 2)
                                values(*before(j, s, 1), u - 1, 1)
                                values(*before(j, s, 1), u - 1, 2)
                            if n:
                                queries(*after(j, s, 1), u + 1)
                            if w:
                                project(*before(j, s, 2), u - 2, 4 * u)

                        input_T(0, 0, 0)
                        queries(0, 0, 0)
                        steps(pe, step)
                        U = B * NT
                        probs_T(NT - 1, B - 1, U - 1, 0)
                        probs_T(NT - 1, B - 1, U - 1, 1)
                        output_T(NT - 1, 0, U - 2, 4 * (U - 1) + EV[0])
                        values(NT - 1, B - 1, U - 1, 0)
                        probs_T(NT - 1, B - 1, U - 1, 2)
                        values(NT - 1, B - 1, U - 1, 1)
                        values(NT - 1, B - 1, U - 1, 2)
                        project(NT - 1, 0, U - 2, 4 * U)
                        output_T(NT - 1, B - 1, U - 1, 4 * U)
                        pe.wait_ge(y_done, U - 1)
                        project(NT - 1, B - 1, U - 1, 4 * U)

        def soft_mixture():
            st = ExitStack()
            with st:
                L = sb(st, "m_L", [P, B, NT, NS])
                nmax = sb(st, "m_nmax", [P, B, NT])
                slT = sb(st, "m_slT", [P, KD, B, NS])
                wg = sb(st, "m_wg", [P, RING, KD, F0])
                wu = sb(st, "m_wu", [P, RING, KD, F0])
                wd = sb(st, "m_wd", [P, RING, KF, D])
                bgu = sb(st, "m_bgu", [P, 2, E0, KF])
                bdr = sb(st, "m_bdr", [1, RING, D])
                tok = ExitStack()
                XL = sb(tok, "m_XL", [P, B, NT, D + 1])
                cb = sb(tok, "m_cb", [P, B, NS])
                wg_ld = [sem(f"m_wg_ld{i}") for i in range(RING)]
                b_ld = sem("m_b_ld")
                begin, end, power = norm_factors("m_", TT, twice=True)

                def load_expert(sp, e, s):
                    sp.dma_start(wg[:, s], t["m_Wg"][e].rearrange("(k p) f -> p k f", p=P)).then_inc(wg_ld[s], 16)
                    sp.dma_start(wu[:, s], t["m_Wu"][e].rearrange("(k p) f -> p k f", p=P)).then_inc(wg_ld[s], 16)
                    sp.dma_start(wd[:, s], t["m_Wd"][e].rearrange("(k p) d -> p k d", p=P)).then_inc(wg_ld[s], 16)
                    sp.dma_start(bdr[:, s, :], t["m_bd"].rearrange("(a e) d -> a e d", a=1)[:, e, :]).then_inc(wg_ld[s], 16)

                pre = ExitStack()
                with pre:
                    cm = slT[:, 0]
                    rest = slT[:, 1].rearrange("p b n -> p (b n)")
                    tn, xw = (rest[:, i * B * D:(i + 1) * B * D].rearrange("p (b d) -> p b d", b=B) for i in range(2))
                    cmw = [rest[:, b * NS:(b + 1) * NS].rearrange("p (c n) -> p c n", c=CS) for b in range(B)]
                    xT = sb(pre, "m_xT", [P, B, KD, P])
                    cmx = sb(pre, "m_cmx", [P, B, CS])
                    psT = ps(pre, "m_psT", [P, B, BANK])
                    psL = ps(pre, "m_psL", [P, B, NS])
                    psC = ps(pre, "m_psC", [P, NS])
                    cmT = [psC[:, :], psL[:, 1, :]]
                    tn_ready = sem("m_tn_ready")
                    xl_step = sem("m_xl_step")
                    xl_ready = sem("m_xl_ready")
                    xl_copy = sem("m_xl_copy")
                    xlT_mm = sem("m_xlT_mm")
                    xlT_ready = sem("m_xlT_ready")
                    l_mm = sem("m_l_mm")
                    l_max = sem("m_l_max")
                    l_copy = sem("m_l_copy")
                    cm_step = sem("m_cm_step")
                    cmT_mm = sem("m_cmT_mm")
                    cmw_ready = sem("m_cmw_ready")
                    cb_mm = sem("m_cb_mm")
                    cb_ready = sem("m_cb_ready")
                    with nc.Block() as block:
                        @block.sync
                        def _(sp):
                            sp.dma_start(bgu[:, 0], t["m_bgT"]).then_inc(b_ld, 16)
                            sp.dma_start(bgu[:, 1], t["m_buT"]).then_inc(b_ld, 16)
                            for e in range(RING):
                                load_expert(sp, e, e)

                        @block.vector
                        def _(dve):
                            def norm_in(j, s, u):
                                i = s * NT + j
                                wait(dve, xl_ready, u - 1)
                                dve.tensor_scalar(tn[:, s], X[:, s, j], mean[:, bass.ds(i, 1)], rstd[:, bass.ds(i, 1)],
                                                  ALU.subtract, ALU.mult).then_inc(tn_ready, 1)

                            def maxima(j, s, u):
                                dve.wait_ge(l_copy, u + 1)
                                dve.tensor_reduce(nmax[:, s, bass.ds(j, 1)], L[:, s, j, :], AX.X, ALU.max
                                                  ).then_inc(l_max, 1)
                                dve.wait_ge(cm_step, u + 2)
                                dve.tensor_tensor(cm[:, s, :], cm[:, s, :], L[:, s, j, :], ALU.max).then_inc(cm_step, 1)

                            def step(j, s, v, n, a):
                                u = B * j + s
                                if a:
                                    norm_in(*after(j, s, 2), u + 2)
                                if v:
                                    maxima(*before(j, s, 1), u - 1)

                            begin(dve)
                            dve.memset(cm[:, :, :], -BIG).then_inc(cm_step, 1)
                            dve.memset(XL[:, :, :, D:D + 1], 1.0).then_inc(cm_step, 1)
                            end(dve)
                            dve.wait_ge(cm_step, 2)
                            for s in range(B):
                                norm_in(0, s, s)
                            tile_steps(dve, NT, step)
                            maxima(NT - 1, B - 1, TT - 1)
                            dve.wait_ge(cm_step, 2 + TT)
                            dve.wait_ge(l_max, TT)
                            dve.tensor_scalar(nmax[:, :, :], nmax[:, :, :], -1.0, None, ALU.mult).then_inc(l_max, 1)
                            for b in range(B):
                                dve.wait_ge(cmT_mm, b + 1)
                                dve.tensor_reduce(cmx[:, b, :], cmT[b].rearrange("p (c n) -> p c n", c=CS),
                                                  AX.X, ALU.max).then_inc(cmw_ready, 1)
                                dve.wait_ge(cmw_ready, 2 * b + 1)
                                dve.tensor_copy(cmw[b], cmx[:, b, :].unsqueeze(2).to_broadcast([P, CS, P])
                                                ).then_inc(cmw_ready, 1)
                            dve.wait_ge(l_max, TT + 1)

                        @block.gpsimd
                        def _(pool):
                            gain = Chain(pool, xl_step, B)

                            def affine(j, s, u):
                                pool.wait_ge(tn_ready, u + 1)
                                gain.step(pool.tensor_tensor(tn[:, s], tn[:, s], gains[:, 0, :], ALU.mult))
                                wait(pool, xlT_mm, u - 1)
                                wait(pool, xl_copy, u - 1)
                                pool.tensor_tensor(xw[:, s], tn[:, s], gains[:, 1, :], ALU.add).then_inc(xl_ready, 1)

                            power(pool)
                            gain.turn(0)
                            for s in range(B):
                                affine(0, s, s)
                            with pool.Fori(1, NT) as j:
                                gain.turn(j)
                                for s in range(B):
                                    affine(j, s, B * j + s)

                        @block.tensor
                        def _(pe):
                            def input_T(j, s, u):
                                pe.wait_ge(xl_ready, u + 1)
                                wait(pe, xlT_ready, u - 1)
                                for k in range(KD):
                                    mm = pe.transpose(psT[:, s, k * P:(k + 1) * P],
                                                      xw[:, s, k * P:(k + 1) * P], ident[:, :])
                                mm.then_inc(xlT_mm, 1)

                            def logits(j, s, u):
                                pe.wait_ge(xlT_ready, u + 1)
                                wait(pe, l_copy, u - 1)
                                for q in range(NS // BANK):
                                    for k in range(KD):
                                        mm = pe.matmul(psL[:, s, q * BANK:(q + 1) * BANK], xT[:, s, k, :],
                                                       seT[:, k, q * BANK:(q + 1) * BANK],
                                                       start=k == 0, stop=k == KD - 1)
                                mm.then_inc(l_mm, 1)

                            def step(j, s, v, n, a):
                                if n:
                                    input_T(*after(j, s, 1), B * j + s + 1)
                                logits(j, s, B * j + s)

                            input_T(0, 0, 0)
                            tile_steps(pe, NT, step)
                            pe.wait_ge(cm_step, 2 + TT)
                            pe.wait_ge(l_copy, TT)
                            for b in range(B):
                                for c in range(CS):
                                    mm = pe.transpose(cmT[b][:, c * P:(c + 1) * P], cm[:, b, c * P:(c + 1) * P], ident[:, :])
                                mm.then_inc(cmT_mm, 1)
                            for b in range(B):
                                pe.wait_ge(cmw_ready, 2 * b + 2)
                                wait(pe, cb_ready, b)
                                for c in range(CS):
                                    mm = pe.matmul(psL[:, 0, c * P:(c + 1) * P], cmw[b][:, c, :], ident[:, :],
                                                   start=True, stop=True)
                                mm.then_inc(cb_mm, 1)

                        @block.scalar
                        def _(act):
                            def input_T(j, s, u):
                                act.wait_ge(xlT_mm, u + 1)
                                wait(act, l_mm, u - 1)
                                act.activation(xT[:, s].rearrange("p k n -> p (k n)"), psT[:, s, 0:KD * P], ACT.Copy
                                               ).then_inc(xlT_ready, 1)
                                act.activation(XL[:, s, j, 0:D], xw[:, s, :], ACT.Copy).then_inc(xl_copy, 1)

                            def logits(j, s, u):
                                act.wait_ge(l_mm, u + 1)
                                act.activation(L[:, s, j, :], psL[:, s, :], ACT.Copy).then_inc(l_copy, 1)

                            def step(j, s, v, n, a):
                                if n:
                                    input_T(*after(j, s, 1), B * j + s + 1)
                                logits(j, s, B * j + s)

                            input_T(0, 0, 0)
                            tile_steps(act, NT, step)
                            act.wait_ge(l_copy, TT)
                            act.wait_ge(xl_copy, TT)
                            for b in range(B):
                                act.wait_ge(cb_mm, b + 1)
                                act.activation(cb[:, b, :], psL[:, 0, :], ACT.Copy).then_inc(cb_ready, 1)
                            act.wait_ge(cb_ready, B)

                mid = ExitStack()
                with mid:
                    ed = sb(mid, "m_ed", [P, 2, NS])
                    sl = seT[:, :, :].rearrange("p k n -> p (k n)").rearrange("p (c d) -> p c d", c=CS)
                    rden = sb(mid, "m_rden", [P, CS])
                    acc = ps(mid, "m_acc", [P, CS, BANK])
                    d_ready = sem("m_d_ready")
                    e_ready = sem("m_e_ready")
                    e_used = sem("m_e_used")
                    sl_step = sem("m_sl_step")
                    sl_mm = sem("m_sl_mm")
                    slT_ready = sem("m_slT_ready")
                    with nc.Block() as block:
                        @block.vector
                        def _(dve):
                            def shift(b, j, s, u):
                                wait(dve, e_used, u - 1)
                                dve.tensor_tensor(ed[:, s, :], L[:, b, j, :], cb[:, b, :], ALU.subtract
                                                  ).then_inc(d_ready, 1)

                            for b in range(B):
                                u0 = b * NT
                                for s in range(2):
                                    if b == 0:
                                        shift(b, s, s, s)
                                with dve.Fori(1, NT // 2) as q:
                                    for s in range(2):
                                        shift(b, 2 * q + s, s, u0 + 2 * q + s)
                                if b < B - 1:
                                    for s in range(2):
                                        shift(b + 1, s, s, u0 + NT + s)
                                dve.wait_ge(e_used, u0 + NT)
                                dve.reciprocal(rden[:, :].unsqueeze(2), acc[:, :, D:D + 1]).then_inc(sl_step, 1)
                                dve.wait_ge(sl_step, b * 2 + 1)
                                wait(dve, sl_mm, KD * b)
                                dve.tensor_tensor(sl[:, :, :], acc[:, :, 0:D],
                                                  rden[:, :].unsqueeze(2).to_broadcast([P, CS, D]), ALU.mult
                                                  ).then_inc(sl_step, 1)

                        @block.scalar
                        def _(act):
                            def exponent(s, u):
                                act.wait_ge(d_ready, u + 1)
                                act.activation(ed[:, s, :], ed[:, s, :], ACT.Exp).then_inc(e_ready, 1)

                            for b in range(B):
                                u0 = b * NT
                                for s in range(2):
                                    if b == 0:
                                        exponent(s, s)
                                with act.Fori(1, NT // 2) as q:
                                    for s in range(2):
                                        exponent(s, u0 + 2 * q + s)
                                if b < B - 1:
                                    for s in range(2):
                                        exponent(s, u0 + NT + s)
                                for k in range(KD):
                                    act.wait_ge(sl_mm, KD * b + k + 1)
                                    act.activation(slT[:, k, b, :].rearrange("p (h n) -> p h n", n=BANK),
                                                   acc[:, 2 * k:2 * k + 2, :], ACT.Copy).then_inc(slT_ready, 1)
                            act.wait_ge(slT_ready, KD * B)

                        @block.tensor
                        def _(pe):
                            def add_tile(b, j, s, u, start, stop):
                                pe.wait_ge(e_ready, u + 1)
                                for c in range(CS):
                                    mm = pe.matmul(acc[:, c, 0:D + 1], ed[:, s, c * P:(c + 1) * P],
                                                   XL[:, b, j, :], start=start, stop=stop)
                                mm.then_inc(e_used, 1)

                            for b in range(B):
                                u0 = b * NT
                                wait(pe, slT_ready, KD * b)
                                add_tile(b, 0, 0, u0, True, False)
                                add_tile(b, 1, 1, u0 + 1, False, False)
                                with pe.Fori(1, NT // 2 - 1) as q:
                                    for s in range(2):
                                        add_tile(b, 2 * q + s, s, u0 + 2 * q + s, False, False)
                                add_tile(b, NT - 2, 0, u0 + NT - 2, False, False)
                                add_tile(b, NT - 1, 1, u0 + NT - 1, False, True)
                                pe.wait_ge(sl_step, 2 * b + 2)
                                for k in range(KD):
                                    for c in range(CS):
                                        mm = pe.transpose(acc[:, 2 * k + c // 4, (c % 4) * P:(c % 4 + 1) * P],
                                                          sl[:, c, k * P:(k + 1) * P], ident[:, :])
                                    mm.then_inc(sl_mm, 1)

                tok.close()
                post = ExitStack()
                with post:
                    eos = sb(post, "m_eos", [P, B, CS, D])
                    exps = ExitStack()
                    gu_mm = sem("m_gu_mm")
                    gu_read = sem("m_gu_read")
                    g_act = sem("m_g_act")
                    h_ready = sem("m_h_ready")
                    eo_mm = sem("m_eo_mm")
                    eo_ready = sem("m_eo_ready")
                    eo_moved = [sem(f"m_eo_moved{i}") for i in range(2)]
                    with exps:
                        TOK = B * SL
                        gt = sb(exps, "m_gt", [P, 2, KF, TOK])
                        up = sb(exps, "m_up", [P, 2, KF, TOK])
                        eo = sb(exps, "m_eo", [P, 2, D])
                        psG = ps(exps, "m_psG", [P, 2, 2, KF * TOK])
                        psE = ps(exps, "m_psE", [P, 2, BANK])
                        with nc.Block() as block:
                            def experts(eng, body):
                                for s in range(RING):
                                    body(s, 0, s)
                                with eng.Fori(1, E0 // RING - 1) as q:
                                    for s in range(RING):
                                        body(RING * q + s, q, s)
                                for s in range(RING):
                                    body(E0 - RING + s, E0 // RING - 1, s)

                            @block.sync
                            def _(sp):
                                def fetch(e, q, s):
                                    sp.wait_ge(eo_mm, e - RING + 1)
                                    load_expert(sp, e, s)

                                with sp.Fori(1, E0 // RING) as q:
                                    for s in range(RING):
                                        fetch(RING * q + s, q, s)

                            @block.tensor
                            def _(pe):
                                def gate_up(e, q, s):
                                    pe.wait_ge(wg_ld[s], 64 * q + 64)
                                    wait(pe, gu_read, 2 * (e - 1))
                                    for i, w in enumerate((wg, wu)):
                                        for f in range(KF):
                                            for k in range(KD):
                                                mm = pe.matmul(psG[:, s % 2, i, f * TOK:(f + 1) * TOK],
                                                               w[:, s, k, f * P:(f + 1) * P],
                                                               slT[:, k, :, bass.ds(e * SL, SL)],
                                                               start=k == 0, stop=k == KD - 1)
                                        mm.then_inc(gu_mm, 1)

                                def down(e, q, s):
                                    pe.wait_ge(h_ready, e + 1)
                                    wait(pe, eo_ready, e - 1)
                                    for f in range(KF):
                                        pe.matmul(psE[:, s % 2, 0:D], gt[:, s % 2, f, :], wd[:, s, f, :],
                                                  start=f == 0, stop=False)
                                    pe.matmul(psE[:, s % 2, 0:D], ones[0:1, 0:TOK], bdr[0:1, s, :], start=False, stop=True
                                              ).then_inc(eo_mm, 1)

                                def body(e, q, s):
                                    if not (isinstance(e, int) and e == E0 - 1):
                                        gate_up(e + 1, *((q, s + 1) if s + 1 < RING else (q + 1, 0)))
                                    down(e, q, s)

                                gate_up(0, 0, 0)
                                experts(pe, body)

                            @block.vector
                            def _(dve):
                                def biases(e, s):
                                    for i, dst in enumerate((gt, up)):
                                        dve.wait_ge(gu_mm, 2 * e + i + 1)
                                        wait(dve, eo_mm, e - 1)
                                        dve.tensor_tensor(
                                            dst[:, s % 2], psG[:, s % 2, i, :].rearrange("p (f n) -> p f n", f=KF),
                                            bgu[:, i, e, :].unsqueeze(2).to_broadcast([P, KF, TOK]), ALU.add
                                            ).then_inc(gu_read, 1)

                                def gated(e, s):
                                    dve.wait_ge(g_act, e + 1)
                                    dve.wait_ge(gu_read, 2 * e + 2)
                                    dve.tensor_tensor(gt[:, s % 2], gt[:, s % 2], up[:, s % 2], ALU.mult
                                                      ).then_inc(h_ready, 1)

                                def body(e, q, s):
                                    biases(e, s)
                                    gated(e, s)

                                dve.wait_ge(b_ld, 32)
                                experts(dve, body)
                                dve.wait_ge(h_ready, E0)

                            @block.scalar
                            def _(act):
                                def gelu(e, s):
                                    act.wait_ge(gu_read, 2 * e + 1)
                                    act.activation(gt[:, s % 2], gt[:, s % 2], ACT.Gelu).then_inc(g_act, 1)

                                def outputs(e, n, s):
                                    act.wait_ge(eo_mm, e + 1)
                                    wait(act, eo_moved[s % 2], 32 * n)
                                    act.activation(eo[:, s % 2, :], psE[:, s % 2, 0:D], ACT.Copy).then_inc(eo_ready, 1)

                                def body(e, q, s):
                                    gelu(e, s)
                                    if not (isinstance(e, int) and e == 0):
                                        n = RING // 2 * q + s // 2
                                        outputs(e - 1, n if s % 2 else n - 1, s - 1)

                                experts(act, body)
                                outputs(E0 - 1, E0 // 2 - 1, RING - 1)

                            @block.gpsimd
                            def _(pool):
                                with pool.Fori(0, E0 // 2) as j:
                                    for s in range(2):
                                        e = 2 * j + s
                                        pool.wait_ge(eo_ready, e + 1)
                                        for b in range(B):
                                            pool.dma_start(eos[s * SL:(s + 1) * SL, b, j, :],
                                                           eo[b * SL:(b + 1) * SL, s, :]).then_inc(eo_moved[s], 16)
                                for s in range(2):
                                    pool.wait_ge(eo_moved[s], 32 * (E0 // 2))

                    comb = ExitStack()
                    with comb:
                        ec = wg[:, 0:B].rearrange("p b k f -> p b (k f)")
                        ecT = wu[:, 0:B].rearrange("p b k f -> p b (k f)").rearrange("p b (c n) -> p b c n", c=CS)
                        den = sb(comb, "m_den", [P, B])
                        rdc = sb(comb, "m_rdc", [P, B])
                        psK = ps(comb, "m_psK", [P, B, NS])
                        psY = ps(comb, "m_psY", [P, B, BANK])
                        ec_ready = sem("m_ec_ready")
                        ec_mm = sem("m_ec_mm")
                        ecT_ready = sem("m_ecT_ready")
                        cy_mm = sem("m_cy_mm")
                        cy_step = sem("m_cy_step")
                        cy_done = sem("m_cy_done")
                        cy_stat = sem("m_cy_stat")
                        with nc.Block() as block:
                            @block.scalar
                            def _(act):
                                def exponent(j, s, u):
                                    wait(act, ec_mm, u - 1)
                                    wait(act, cy_step, u - 1)
                                    act.activation(ec[:, s, :], L[:, s, j, :], ACT.Exp, bias=nmax[:, s, bass.ds(j, 1)],
                                                   accum_out=den[:, s:s + 1]).then_inc(ec_ready, 1)

                                for s in range(B):
                                    exponent(0, s, s)
                                with act.Fori(1, NT) as j:
                                    for s in range(B):
                                        exponent(j, s, B * j + s)

                            @block.tensor
                            def _(pe):
                                def weights_T(j, s, u):
                                    pe.wait_ge(ec_ready, u + 1)
                                    wait(pe, ecT_ready, u - 1)
                                    for c in range(CS):
                                        mm = pe.transpose(psK[:, s, c * P:(c + 1) * P], ec[:, s, c * P:(c + 1) * P],
                                                          ident[:, :])
                                    mm.then_inc(ec_mm, 1)

                                def outputs(j, s, u):
                                    pe.wait_ge(ecT_ready, u + 1)
                                    wait(pe, cy_done, u - 1)
                                    for c in range(CS):
                                        mm = pe.matmul(psY[:, s, 0:D], ecT[:, s, c, :], eos[:, s, c, :],
                                                       start=c == 0, stop=c == CS - 1)
                                    mm.then_inc(cy_mm, 1)

                                def step(j, s, v, n, a):
                                    if n:
                                        weights_T(*after(j, s, 1), B * j + s + 1)
                                    outputs(j, s, B * j + s)

                                weights_T(0, 0, 0)
                                tile_steps(pe, NT, step)

                            @block.vector
                            def _(dve):
                                def weights_T(j, s, u):
                                    dve.wait_ge(ec_mm, u + 1)
                                    wait(dve, cy_mm, u - 1)
                                    dve.tensor_copy(ecT[:, s].rearrange("p c n -> p (c n)"), psK[:, s, :]
                                                    ).then_inc(ecT_ready, 1)

                                def residual(j, s, u):
                                    dve.wait_ge(ec_ready, u + 1)
                                    wait(dve, cy_done, u - 1)
                                    dve.reciprocal(rdc[:, s:s + 1], den[:, s:s + 1]).then_inc(cy_step, 1)
                                    dve.wait_ge(cy_step, u + 1)
                                    dve.wait_ge(cy_mm, u + 1)
                                    dve.scalar_tensor_tensor(X[:, s, j], psY[:, s, 0:D], rdc[:, s:s + 1], X[:, s, j],
                                                             ALU.mult, ALU.add).then_inc(cy_done, 1)

                                def stat(j, s, u):
                                    dve.wait_ge(cy_done, u + 1)
                                    dve.bn_stats(stats[:, s * NT + j, :], X[:, s, j]).then_inc(cy_stat, 1)

                                def step(j, s, v, n, a):
                                    u = B * j + s
                                    if n:
                                        weights_T(*after(j, s, 1), u + 1)
                                    residual(j, s, u)
                                    if v:
                                        stat(*before(j, s, 1), u - 1)

                                weights_T(0, 0, 0)
                                tile_steps(dve, NT, step)
                                stat(NT - 1, B - 1, TT - 1)
                                dve.wait_ge(cy_stat, TT)

        def top3_mixture(W, W1, W2, w1_ld, w2_ld):
            st = ExitStack()
            Xf = X[:, :, :, :].rearrange("p b t d -> p (b t) d")
            begin, end, power = norm_factors("f_", TT)
            with st:
                wt = sb(st, "f_wt", [P, R, TOP, TT])
                rows = sb(st, "f_rows", [P, TOP, TT], U32)
                toks = sb(st, "f_toks", [P, 2, LT], U32)
                owner = sb(st, "f_owner", [1, 2, LT], I32)
                dwb = sb(st, "f_dwb", [P, TT, E1])
                Z = sb(st, "f_Z", [P, R, TT, E1])
                hot = sb(st, "f_hot", [P, 2, TOP, TT, E1])
                iota = sb(st, "f_iota", [P, P])
                below = sb(st, "f_below", [P, P])
                allone = sb(st, "f_allone", [P, P])
                tokid = sb(st, "f_tokid", [P, 2, TT, TOP])
                spare = sb(st, "f_spare", [P, LT])
                dest = sb(st, "f_dest", [P, LT], U32)
                pair = sb(st, "f_pair", [P, LT])
                pairi = sb(st, "f_pairi", [P, 2, LT], I32)
                tmp = sb(st, "f_tmp", [P, TOP, TT, E1])
                first = sb(st, "f_first", [P, TT])
                chosen = sb(st, "f_chosen", [P, TT, E1])
                place = sb(st, "f_place", [P, TT, E1])
                tiles = [sb(st, f"f_tiles{i}", [P, TT + 1, E1]) for i in range(2)]
                cnt = sb(st, "f_cnt", [P, E1])
                cnti = sb(st, "f_cnti", [P, E1], I32)
                start = [sb(st, f"f_start{i}", [P, E1 + 1, 1]) for i in range(2)]
                past = sel[:, 0:LT * E1].rearrange("p (i e) -> p i e", e=E1)
                own = sb(st, "f_own", [P, LT])
                pk = sb(st, "f_pk", [P, TOP, TT])
                pki = sb(st, "f_pki", [P, TOP, TT], I32)
                part = sb(st, "f_part", [P, 2, TOP, TT], I32)
                pdiv = sb(st, "f_pdiv", [P, TOP, TT])
                pmod = sb(st, "f_pmod", [P, TOP, TT])
                at_row = sb(st, "f_at_row", [P, AR, TOP, P], BF16)
                at_eq = sb(st, "f_at_eq", [P, AR, TOP, LT], BF16)
                at_tile = sb(st, "f_at_tile", [P, AR, TOP, 2, LT], BF16)

                def over(v):
                    return v.unsqueeze(2).to_broadcast([P, TT, E1])

                def pick(dve, one, r, h):
                    for k in range(TOP):
                        top, z, eq = wt[:, r, k, :], Z[:, r], tmp[:, 0]
                        one.step(dve.tensor_reduce(top, z, AX.X, ALU.max))
                        one.step(dve.tensor_tensor(eq, z, over(top), ALU.is_equal))
                        one.step(dve.scalar_tensor_tensor(eq, eq, -float(E1),
                                                          iota[:, 0:E1].unsqueeze(1).to_broadcast([P, TT, E1]),
                                                          ALU.mult, ALU.add))
                        one.step(dve.tensor_reduce(first[:, :], eq, AX.X, ALU.min))
                        one.step(dve.tensor_tensor(hot[:, h, k], eq, over(first[:, :]), ALU.is_equal))
                        if k < TOP - 1:
                            one.step(dve.scalar_tensor_tensor(z, hot[:, h, k], -BIG, z, ALU.mult, ALU.add))

                def running(dve, one, ab, n):
                    a, b = ab
                    d = 1
                    while d < n - 1:
                        one.step(dve.tensor_copy(b[:, 0:d], a[:, 0:d]), hold=False)
                        one.step(dve.tensor_tensor(b[:, d:n], a[:, d:n], a[:, 0:n - d], ALU.add))
                        a, b = b, a
                        d *= 2
                    return a

                def lists(dve, one, r, counts, count_mm):
                    nb = TT * E1
                    dve.wait_ge(count_mm, 1)
                    one.step(dve.memset(tiles[0][:, 0, :], 0.0), hold=False)
                    one.step(dve.memset(start[0][:, 0:1, :], 0.0), hold=False)
                    one.step(dve.tensor_copy(tiles[0][:, 1:TT + 1, :],
                                             counts[:, nb:2 * nb].rearrange("p (t e) -> p t e", t=TT)))
                    before_tile = running(dve, one, tiles, TT + 1)
                    one.step(dve.tensor_scalar(cnt[:, :], before_tile[:, TT, :], float(P - 1), None, ALU.add))
                    one.step(dve.tensor_copy(cnti[:, :], cnt[:, :]))
                    one.step(dve.tensor_scalar(cnti[:, :], cnti[:, :], 7, None, ALU.arith_shift_right))
                    one.step(dve.tensor_copy(start[0][:, 1:E1 + 1, :], cnti[:, :].unsqueeze(2)))
                    begin = running(dve, one, start, E1 + 1)
                    one.step(dve.tensor_tensor(place[:, :, :], counts[:, 0:nb].rearrange("p (t e) -> p t e", t=TT),
                                               before_tile[:, 0:TT, :], ALU.add))
                    one.step(dve.scalar_tensor_tensor(
                        place[:, :, :], begin[:, 0:E1, 0].unsqueeze(1).to_broadcast([P, TT, E1]), float(P),
                        place[:, :, :], ALU.mult, ALU.add))
                    one.step(dve.tensor_tensor(tmp[:, :, :, :], hot[:, 0],
                                               place[:, :, :].unsqueeze(1).to_broadcast([P, TOP, TT, E1]), ALU.mult))
                    one.step(dve.tensor_reduce(pk[:, :, :], tmp[:, :, :, :], AX.X, ALU.add))
                    one.step(dve.tensor_copy(pki[:, :, :], pk[:, :, :]))
                    one.step(dve.tensor_scalar(part[:, 0], pki[:, :, :], 7, None, ALU.arith_shift_right), hold=False)
                    one.step(dve.tensor_scalar(part[:, 1], pki[:, :, :], P - 1, None, ALU.bitwise_and))
                    one.step(dve.tensor_copy(pdiv[:, :, :], part[:, 0]), hold=False)
                    one.step(dve.tensor_copy(pmod[:, :, :], part[:, 1]))
                    return begin

                def owners(dve, one, r, begin):
                    one.step(dve.tensor_tensor(
                        past[:, :, :], iota[:, 0:LT].unsqueeze(2).to_broadcast([P, LT, E1]),
                        begin[:, 1:E1 + 1, 0].unsqueeze(1).to_broadcast([P, LT, E1]), ALU.is_ge))
                    one.step(dve.tensor_reduce(own[:, :], past[:, :, :], AX.X, ALU.add))
                    one.step(dve.tensor_scalar(own[:, :], own[:, :], float(E1 - 1), None, ALU.min))
                    one.step(dve.tensor_copy(owner[:, r, :], own[0:1, :]))

                def choose(dve, one, chosen_ready):
                    one.step(dve.tensor_tensor(chosen[:, :, :], hot[:, 0, 0], hot[:, 0, 1], ALU.add))
                    one.step(dve.tensor_tensor(chosen[:, :, :], chosen[:, :, :], hot[:, 0, 2], ALU.add))
                    dve.sem_inc(chosen_ready, 1)

                def count(pe, counts, chosen_ready, count_mm):
                    pe.wait_ge(chosen_ready, 1)
                    ct = chosen[:, :, :].rearrange("p t e -> p (t e)")
                    nb = TT * E1
                    pe.matmul(counts[:, 0:nb], below[:, :], ct, start=True, stop=True)
                    pe.matmul(counts[:, nb:2 * nb], allone[:, :], ct, start=True, stop=True).then_inc(count_mm, 1)

                def match_row(dve, i, s, at_used, row_ready):
                    wait(dve, at_used, i - AR + 1)
                    dve.tensor_tensor(
                        at_row[:, s], iota[:, :].unsqueeze(1).to_broadcast([P, TOP, P]),
                        pmod[:, :, bass.ds(i, 1)].to_broadcast([P, TOP, P]), ALU.is_equal).then_inc(row_ready, 1)

                def match_tile(dve, i, s, at_used, at_step):
                    wait(dve, at_used, i - AR + 1)
                    dve.tensor_tensor(
                        at_eq[:, s], iota[:, 0:LT].unsqueeze(1).to_broadcast([P, TOP, LT]),
                        pdiv[:, :, bass.ds(i, 1)].to_broadcast([P, TOP, LT]), ALU.is_equal).then_inc(at_step, 1)

                def weigh_tile(eng, i, s, at_step, tile_ready):
                    eng.wait_ge(at_step, i + 1)
                    for d in range(2):
                        eng.tensor_tensor(at_tile[:, s, :, d, :], at_eq[:, s],
                                          tokid[:, d, i, :].unsqueeze(2).to_broadcast([P, TOP, LT]), ALU.mult
                                          ).then_inc(tile_ready, 1)

                def found_tokens(dve, one, r, found):
                    one.step(dve.tensor_copy(own[:, :], found[:, LT:2 * LT]))
                    one.step(dve.scalar_tensor_tensor(own[:, :], found[:, 0:LT], float(DIGIT), own[:, :],
                                                      ALU.mult, ALU.add))
                    one.step(dve.tensor_scalar(pair[:, :], own[:, :], -1.0, None, ALU.add))
                    one.step(dve.tensor_copy(pairi[:, 0], pair[:, :]))
                    one.step(dve.tensor_scalar(pairi[:, 1], pairi[:, 0], B * N - 1, None, ALU.bitwise_and))
                    one.step(dve.tensor_copy(toks[:, r, :], pairi[:, 1]))
                    if r == 1:
                        one.step(dve.scalar_tensor_tensor(own[:, :], own[:, :], 0.0, spare[:, :],
                                                          ALU.is_equal, ALU.mult))
                        one.step(dve.tensor_tensor(pair[:, :], pair[:, :], own[:, :], ALU.add))
                        one.step(dve.tensor_copy(pairi[:, 0], pair[:, :]))
                        one.step(dve.tensor_copy(dest[:, :], pairi[:, 0]))

                def add_tokens(pe, i, s, found, row_ready, tile_ready, at_used, start, stop):
                    pe.wait_ge(row_ready, i + 1)
                    pe.wait_ge(tile_ready, 2 * i + 2)
                    for k in range(TOP):
                        mm = pe.matmul(found[:, 0:2 * LT], at_row[:, s, k, :], at_tile[:, s, k, :, :],
                                       start=start and k == 0, stop=stop and k == TOP - 1)
                    mm.then_inc(at_used, 1)

                def add_all(pe, found, row_ready, tile_ready, at_used):
                    def quad(j, first, last):
                        for s in range(AR):
                            add_tokens(pe, AR * j + s, s, found, row_ready, tile_ready, at_used,
                                       first and s == 0, last and s == AR - 1)

                    quad(0, True, False)
                    with pe.Fori(1, TT // AR - 1) as j:
                        quad(j, False, False)
                    quad(TT // AR - 1, False, True)

                rt = ExitStack()
                with rt:
                    Pw = sb(rt, "f_Pw", [P, KD, DA])
                    U = sb(rt, "f_U", [DA, R * E1])
                    xn = sb(rt, "f_xn", [P, TT, D])
                    xw = sb(rt, "f_xw", [P, 2, D])
                    xT = sb(rt, "f_xT", [P, 2, KD, P])
                    aT = sb(rt, "f_aT", [DA, 2, P])
                    psT = ps(rt, "f_psT", [P, 2, BANK])
                    psA = ps(rt, "f_psA", [DA, 2, BANK])
                    psZ = ps(rt, "f_psZ", [P, 2, BANK])
                    psN = ps(rt, "f_psN", [P, BANK])
                    psF = ps(rt, "f_psF", [P, BANK])
                    ld = sem("f_ld")
                    xn_ready = sem("f_xn_ready")
                    xw_ready = sem("f_xw_ready")
                    xn_stored = sem("f_xn_stored")
                    xT_mm = sem("f_xT_mm")
                    xT_ready = sem("f_xT_ready")
                    a_mm = sem("f_a_mm")
                    a_ready = sem("f_a_ready")
                    z_mm = sem("f_z_mm")
                    z_ready = sem("f_z_ready")
                    r_step = sem("f_r_step")
                    at_step = sem("f_at_step")
                    chosen_ready = sem("f_chosen_ready")
                    count_mm = sem("f_count_mm")
                    row_ready = sem("f_row_ready")
                    tile_ready = sem("f_tile_ready")
                    at_used = sem("f_at_used")
                    with nc.Block() as block:
                        @block.sync
                        def _(sp):
                            sp.dma_start(Pw[:, :, :], t["f_PwT"].rearrange("(k p) a -> p k a", p=P)).then_inc(ld, 16)
                            sp.dma_start(U[:, :], t["f_UT"]).then_inc(ld, 16)
                            sp.dma_start(iota[:, :], t["c_iota"].partition_broadcast(P)).then_inc(ld, 16)
                            sp.dma_start(below[:, :], t["c_below"]).then_inc(ld, 16)
                            sp.dma_start(tokid[:, :, :, :], t["c_tokid"]).then_inc(ld, 16)
                            sp.dma_start(spare[:, :], t["c_spare"]).then_inc(ld, 16)
                            sp.wait_ge(xn_ready, TT)
                            sp.dma_start(xn_d.rearrange("(t p) d -> p t d", p=P), xn[:, :, :]).then_inc(xn_stored, 16)
                            sp.wait_ge(xn_stored, 16)

                        @block.vector
                        def _(dve):
                            def norm_in(j, s, u):
                                wait(dve, xT_mm, u - 1)
                                for place, ready in ((xw[:, s % 2, :], xw_ready), (xn[:, u, :], xn_ready)):
                                    dve.tensor_scalar(place, Xf[:, u, :], mean[:, bass.ds(u, 1)],
                                                      rstd[:, bass.ds(u, 1)], ALU.subtract, ALU.mult).then_inc(ready, 1)

                            def scores(j, s, u):
                                dve.wait_ge(z_mm, u + 1)
                                dve.tensor_copy(Z[:, :, u, :], psZ[:, s % 2, 0:R * E1].rearrange("p (r e) -> p r e", r=R)
                                                ).then_inc(z_ready, 1)

                            def step(j, s, v, n, a):
                                u = AR * j + s
                                if a:
                                    norm_in(*after(j, s, 2, AR), u + 2)
                                if v:
                                    scores(*before(j, s, 1, AR), u - 1)

                            begin(dve)
                            end(dve)
                            for s in range(2):
                                norm_in(0, s, s)
                            tile_steps(dve, TT // AR, step, AR)
                            scores(TT // AR - 1, AR - 1, TT - 1)
                            dve.wait_ge(ld, 97)
                            dve.wait_ge(z_ready, TT)
                            one = Chain(dve, r_step, 0)
                            one.turn(0)
                            pick(dve, one, 0, 0)
                            choose(dve, one, chosen_ready)
                            first_tile = lists(dve, one, 0, psN, count_mm)
                            for s in range(AR):
                                match_tile(dve, s, s, at_used, at_step)
                                match_row(dve, s, s, at_used, row_ready)
                            one.step(dve.tensor_copy(rows[:, :, :], pki[:, :, :]))
                            owners(dve, one, 0, first_tile)
                            with dve.Fori(1, TT // AR) as j:
                                for s in range(AR):
                                    match_tile(dve, AR * j + s, s, at_used, at_step)
                                    match_row(dve, AR * j + s, s, at_used, row_ready)
                            dve.wait_ge(at_used, TT)
                            found_tokens(dve, one, 0, psF)

                        @block.scalar
                        def _(act):
                            def input_T(j, s, u):
                                act.wait_ge(xT_mm, u + 1)
                                wait(act, a_mm, u - 1)
                                act.activation(xT[:, s % 2].rearrange("p k n -> p (k n)"), psT[:, s % 2, 0:KD * P], ACT.Copy
                                               ).then_inc(xT_ready, 1)

                            def addresses(j, s, u):
                                act.wait_ge(a_mm, u + 1)
                                wait(act, z_mm, u - 1)
                                act.activation(aT[:, s % 2, :], psA[:, s % 2, 0:P], ACT.Copy).then_inc(a_ready, 1)

                            def step(j, s, v, n, a):
                                u = AR * j + s
                                if n:
                                    input_T(*after(j, s, 1, AR), u + 1)
                                addresses(j, s, u)

                            input_T(0, 0, 0)
                            tile_steps(act, TT // AR, step, AR)

                        @block.gpsimd
                        def _(pool):
                            power(pool)
                            pool.memset(allone[:, :], 1.0).then_inc(ld, 1)
                            pool.wait_ge(ld, 97)
                            with pool.Fori(0, TT // AR) as j:
                                for s in range(AR):
                                    weigh_tile(pool, AR * j + s, s, at_step, tile_ready)

                        @block.tensor
                        def _(pe):
                            def input_T(j, s, u):
                                pe.wait_ge(xw_ready, u + 1)
                                wait(pe, xT_ready, u - 1)
                                for k in range(KD):
                                    mm = pe.transpose(psT[:, s % 2, k * P:(k + 1) * P], xw[:, s % 2, k * P:(k + 1) * P],
                                                      ident[:, :])
                                mm.then_inc(xT_mm, 1)

                            def addresses(j, s, u):
                                pe.wait_ge(xT_ready, u + 1)
                                wait(pe, a_ready, u - 1)
                                for k in range(KD):
                                    mm = pe.matmul(psA[:, s % 2, 0:P], Pw[:, k, :], xT[:, s % 2, k, :],
                                                   start=k == 0, stop=k == KD - 1)
                                mm.then_inc(a_mm, 1)

                            def scores(j, s, u):
                                pe.wait_ge(a_ready, u + 1)
                                wait(pe, z_ready, u - 1)
                                pe.matmul(psZ[:, s % 2, 0:R * E1], aT[:, s % 2, :], U[:, :], start=True, stop=True
                                          ).then_inc(z_mm, 1)

                            def step(j, s, v, n, a):
                                u = AR * j + s
                                if n:
                                    input_T(*after(j, s, 1, AR), u + 1)
                                addresses(j, s, u)
                                if v:
                                    scores(*before(j, s, 1, AR), u - 1)

                            pe.wait_ge(ld, 97)
                            input_T(0, 0, 0)
                            tile_steps(pe, TT // AR, step, AR)
                            scores(TT // AR - 1, AR - 1, TT - 1)
                            count(pe, psN, chosen_ready, count_mm)
                            add_all(pe, psF, row_ready, tile_ready, at_used)

                QUAD = 4

                def list_tiles(eng, body):
                    for s in range(QUAD):
                        body(s, 0, s)
                    with eng.Fori(1, LT // QUAD) as q:
                        for s in range(QUAD):
                            body(QUAD * q + s, q, s)
                    for s in range(LT % QUAD):
                        body(LT - LT % QUAD + s, LT // QUAD, s)

                def uses(s):
                    return -(-(LT - s) // QUAD)

                def following(q, s):
                    return (q, s + 1) if s + 1 < QUAD else (q + 1, 0)

                first_st = ExitStack()
                with first_st:
                    den = sb(first_st, "f_den", [P, R, TT])
                    r1_step = sem("f1_r_step")
                    gap_ready = sem("f1_gap_ready")
                    exp_ready = sem("f1_exp_ready")
                    chosen_ready = sem("f2_chosen_ready")
                    xg = sb(first_st, "f_xg", [P, QUAD, D])
                    ix = sb(first_st, "f1_ix", [P, QUAD], U32)
                    xT = sb(first_st, "f1_xT", [P, 2, KD, P])
                    po = sb(first_st, "f_po", [P, QUAD, HID])
                    psT = ps(first_st, "f1_psT", [P, 2, BANK])
                    psH = ps(first_st, "f1_psH", [P, 2, HID])
                    ix_ready = sem("f1_ix_ready")
                    xg_ld = [sem(f"f_xg_ld{i}") for i in range(QUAD)]
                    xT_mm = sem("f1_xT_mm")
                    xT_ready = sem("f1_xT_ready")
                    h_mm = sem("f1_h_mm")
                    po_ready = sem("f_po_ready")
                    po_stored = [sem(f"f_po_stored{i}") for i in range(QUAD)]
                    with nc.Block() as block:
                        @block.gpsimd
                        def _(pool):
                            def gather(i, q, s):
                                wait(pool, xT_mm, i - QUAD + 1)
                                pool.tensor_copy(ix[:, s:s + 1], toks[:, 0, bass.ds(i, 1)]).then_inc(ix_ready, 1)
                                pool.wait_ge(ix_ready, i + 1)
                                pool.nop(nofuse=True)
                                pool.indirect_dma_start(xg[:, s, :], None, xn_d, bass.IndirectOffsetOnAxis(
                                    ap=ix[:, s:s + 1], axis=0)).then_inc(xg_ld[s], 16)

                            list_tiles(pool, gather)

                        @block.tensor
                        def _(pe):
                            def turn(i, q, s):
                                pe.wait_ge(xg_ld[s], 16 * q + 16)
                                wait(pe, xT_ready, i - 1)
                                for k in range(KD):
                                    mm = pe.transpose(psT[:, s % 2, k * P:(k + 1) * P], xg[:, s, k * P:(k + 1) * P],
                                                      ident[:, :])
                                mm.then_inc(xT_mm, 1)

                            def multiply(i, q, s):
                                e = pe.value_load(owner[0:1, 0, bass.ds(i, 1)], min_val=0, max_val=E1 - 1)
                                pe.wait_ge(xT_ready, i + 1)
                                wait(pe, po_ready, i - 1)
                                for c in range(HID // BANK):
                                    for k in range(KD):
                                        mm = pe.matmul(psH[:, s % 2, c * BANK:(c + 1) * BANK], xT[:, s % 2, k, :],
                                                       W1[:, e, k, c * BANK:(c + 1) * BANK], start=k == 0, stop=k == KD - 1)
                                mm.then_inc(h_mm, 1)

                            def tile(i, q, s):
                                if not (isinstance(i, int) and i == LT - 1):
                                    turn(i + 1, *following(q, s))
                                multiply(i, q, s)

                            pe.wait_ge(w1_ld, 16 * E1)
                            turn(0, 0, 0)
                            list_tiles(pe, tile)

                        @block.scalar
                        def _(act):
                            def tokens_T(i, q, s):
                                act.wait_ge(xT_mm, i + 1)
                                wait(act, h_mm, i - 1)
                                act.activation(xT[:, s % 2].rearrange("p k n -> p (k n)"), psT[:, s % 2, 0:KD * P],
                                               ACT.Copy).then_inc(xT_ready, 1)

                            def products(i, q, s):
                                act.wait_ge(h_mm, i + 1)
                                wait(act, po_stored[s], 16 * q)
                                act.activation(po[:, s, :], psH[:, s % 2, :], ACT.Copy).then_inc(po_ready, 1)

                            def tile(i, q, s):
                                if not (isinstance(i, int) and i == LT - 1):
                                    tokens_T(i + 1, *following(q, s))
                                products(i, q, s)

                            tokens_T(0, 0, 0)
                            list_tiles(act, tile)
                            act.wait_ge(gap_ready, 1)
                            flat = wt[:, :, :, :].rearrange("p r k t -> p (r k t)")
                            act.activation(flat, flat, ACT.Exp).then_inc(exp_ready, 1)

                        @block.vector
                        def _(dve):
                            one = Chain(dve, r1_step, 0)
                            one.turn(0)
                            pick(dve, one, 1, 0)
                            pick(dve, one, 2, 1)
                            choose(dve, one, chosen_ready)
                            for k in range(1, TOP):
                                one.step(dve.tensor_tensor(wt[:, :, k, :], wt[:, :, k, :], wt[:, :, 0, :], ALU.subtract),
                                         hold=False)
                            one.hold()
                            one.step(dve.memset(wt[:, :, 0, :], 0.0))
                            dve.sem_inc(gap_ready, 1)
                            dve.wait_ge(exp_ready, 1)
                            one.step(dve.tensor_tensor(den[:, :, :], wt[:, :, 0, :], wt[:, :, 1, :], ALU.add))
                            one.step(dve.tensor_tensor(den[:, :, :], den[:, :, :], wt[:, :, 2, :], ALU.add))
                            one.step(dve.reciprocal(den[:, :, :], den[:, :, :]))
                            for k in range(TOP):
                                one.step(dve.tensor_tensor(wt[:, :, k, :], wt[:, :, k, :], den[:, :, :], ALU.mult),
                                         hold=False)
                            one.hold()
                            for k in range(TOP):
                                one.step(dve.tensor_tensor(tmp[:, k], hot[:, 1, k], over(wt[:, 2, k, :]), ALU.mult),
                                         hold=False)
                            one.hold()
                            one.step(dve.tensor_tensor(dwb[:, :, :], tmp[:, 0], tmp[:, 1], ALU.add))
                            one.step(dve.tensor_tensor(dwb[:, :, :], dwb[:, :, :], tmp[:, 2], ALU.add))

                        @block.sync
                        def _(sp):
                            def store(i, q, s):
                                sp.wait_ge(po_ready, i + 1)
                                sp.dma_start(p1_d[i], po[:, s, :]).then_inc(po_stored[s], 16)

                            list_tiles(sp, store)
                            for s in range(QUAD):
                                sp.wait_ge(po_stored[s], 16 * uses(s))

                W2_FIRST = 1

                def load_w2(eng, e0, e1):
                    for e in range(e0, e1):
                        wait(eng, w2_ld, 16 * e)
                        eng.dma_start(W2[:, e], t["f_W2T"][e]).then_inc(w2_ld, 16)

                comb = ExitStack()
                with comb:
                    g = sb(comb, "f_g", [P, GR, TOP, HID])
                    hs = att[1][0][:, :, :, :].rearrange("p w k d -> p (w k d)").rearrange("p (s h) -> p s h", s=2)
                    ix = sb(comb, "f_ix", [P, GR, TOP], U32)
                    b2 = sb(comb, "f_b2", [E1, D])
                    dw3 = sb(comb, "f_dw3", [P, 2, E1])
                    dwT = sb(comb, "f_dwT", [E1, 2, P])
                    psD = ps(comb, "f_psD", [P, 2, BANK])
                    psB = ps(comb, "f_psB", [P, 2, BANK])
                    b2_ld = sem("f_b2_ld")
                    dw3_ready = sem("f_dw3_ready")
                    dwT_mm = sem("f_dwT_mm")
                    dwT_ready = sem("f_dwT_ready")
                    b_mm = sem("f_b_mm")
                    b_done = sem("f_b_done")
                    psN = ps(comb, "f2_psN", [P, BANK])
                    psF = ps(comb, "f2_psF", [P, BANK])
                    ix_ready = sem("f_ix_ready")
                    g_ld = [sem(f"f_g_ld{i}") for i in range(GR)]
                    s_step = sem("f_s_step")
                    r_step = sem("f2_r_step")
                    at_step = sem("f2_at_step")
                    count_mm = sem("f2_count_mm")
                    row_ready = sem("f2_row_ready")
                    tile_ready = sem("f2_tile_ready")
                    at_used = sem("f2_at_used")
                    h_first = sem("f_h_first")
                    hs_ready = sem("f_hs_ready")
                    hs_stored = [sem(f"f_hs_stored{i}") for i in range(2)]
                    with nc.Block() as block:
                        @block.gpsimd
                        def _(pool):
                            def gather(i, s):
                                wait(pool, hs_ready, i - GR + 1)
                                pool.tensor_copy(ix[:, s, :], rows[:, :, i]).then_inc(ix_ready, 1)
                                pool.wait_ge(ix_ready, i + 1)
                                pool.nop(nofuse=True)
                                for k in range(TOP):
                                    pool.indirect_dma_start(
                                        g[:, s, k, :], None, p1_rows, bass.IndirectOffsetOnAxis(
                                            ap=ix[:, s, k:k + 1], axis=0)).then_inc(g_ld[s], 16)

                            for s in range(GR):
                                gather(s, s)
                            with pool.Fori(1, TT // GR) as q:
                                for s in range(GR):
                                    gather(GR * q + s, s)

                        @block.vector
                        def _(dve):
                            one = Chain(dve, r_step, 0)
                            one.turn(0)
                            owners(dve, one, 1, lists(dve, one, 1, psN, count_mm))
                            sums = Chain(dve, s_step, GR)

                            def tile(i, q, s):
                                dve.wait_ge(g_ld[s], 16 * TOP * (q + 1))
                                dve.wait_ge(h_first, i + 1)
                                h = hs[:, s % 2, :]
                                sums.step(dve.scalar_tensor_tensor(h, g[:, s, 1, :], wt[:, 0, 1, bass.ds(i, 1)], h,
                                                                   ALU.mult, ALU.add))
                                dve.scalar_tensor_tensor(h, g[:, s, 2, :], wt[:, 0, 2, bass.ds(i, 1)], h,
                                                         ALU.mult, ALU.add).then_inc(hs_ready, 1)
                                match_tile(dve, i, s, at_used, at_step)
                                match_row(dve, i, s, at_used, row_ready)
                                weigh_tile(dve, i, s, at_step, tile_ready)
                                dve.wait_ge(b_mm, i + 1)
                                dve.tensor_tensor(Xf[:, i, :], psB[:, s % 2, 0:D], Xf[:, i, :], ALU.add
                                                  ).then_inc(b_done, 1)

                            sums.turn(0)
                            for s in range(GR):
                                tile(s, 0, s)
                            with dve.Fori(1, TT // GR) as q:
                                sums.turn(q)
                                for s in range(GR):
                                    tile(GR * q + s, q, s)
                                sums.end()
                            dve.wait_ge(b_done, TT)
                            dve.wait_ge(at_used, TT)
                            found_tokens(dve, one, 1, psF)

                        @block.tensor
                        def _(pe):
                            def quad(j, first, last):
                                for s in range(AR):
                                    i = AR * j + s
                                    pe.wait_ge(dw3_ready, i + 1)
                                    wait(pe, dwT_ready, i - 1)
                                    pe.transpose(psD[0:E1, s % 2, 0:P], dw3[:, s % 2, :], ident[:, :]).then_inc(dwT_mm, 1)
                                    pe.wait_ge(dwT_ready, i + 1)
                                    wait(pe, b_done, i - 1)
                                    pe.matmul(psB[:, s % 2, 0:D], dwT[:, s % 2, :], b2[:, :], start=True, stop=True
                                              ).then_inc(b_mm, 1)
                                    add_tokens(pe, i, s, psF, row_ready, tile_ready, at_used,
                                               first and s == 0, last and s == AR - 1)

                            count(pe, psN, chosen_ready, count_mm)
                            pe.wait_ge(b2_ld, 16)
                            quad(0, True, False)
                            with pe.Fori(1, TT // AR - 1) as j:
                                quad(j, False, False)
                            quad(TT // AR - 1, False, True)

                        @block.sync
                        def _(sp):
                            sp.dma_start(b2[:, :], t["f_b2"]).then_inc(b2_ld, 16)
                            with sp.Fori(0, TT // 2) as j:
                                for s in range(2):
                                    sp.wait_ge(hs_ready, 2 * j + s + 1)
                                    sp.dma_start(h_d[2 * j + s], hs[:, s, :]).then_inc(hs_stored[s], 16)
                            for s in range(2):
                                sp.wait_ge(hs_stored[s], 16 * (TT // 2))

                        @block.scalar
                        def _(act):
                            def first_row(i, q, s):
                                act.wait_ge(g_ld[s], 16 * TOP * (q + 1))
                                n = GR // 2 * q + s // 2
                                wait(act, hs_stored[s % 2], 16 * n)
                                act.activation(hs[:, s % 2, :], g[:, s, 0, :], ACT.Copy,
                                               scale=wt[:, 0, 0, bass.ds(i, 1)]).then_inc(h_first, 1)

                            def pair(q, s0):
                                for s in (s0, s0 + 1):
                                    i = GR * q + s
                                    wait(act, dwT_mm, i - 1)
                                    act.activation(dw3[:, s % 2, :], dwb[:, i, :], ACT.Copy).then_inc(dw3_ready, 1)
                                for s in (s0, s0 + 1):
                                    i = GR * q + s
                                    first_row(i, q, s)
                                    act.wait_ge(dwT_mm, i + 1)
                                    wait(act, b_mm, i - 1)
                                    act.activation(dwT[:, s % 2, :], psD[0:E1, s % 2, 0:P], ACT.Copy
                                                   ).then_inc(dwT_ready, 1)

                            for s in range(0, GR, 2):
                                pair(0, s)
                            with act.Fori(1, TT // GR) as q:
                                for s in range(0, GR, 2):
                                    pair(q, s)
                            load_w2(act, 0, W2_FIRST)

                sec = ExitStack()
                with sec:
                    hg = sb(sec, "f_hg", [P, QUAD, HID])
                    ix = sb(sec, "f2_ix", [P, QUAD], U32)
                    hT = sb(sec, "f_hT", [P, 2, KH, P])
                    yo = sb(sec, "f_yo", [P, QUAD, D])
                    ox = sb(sec, "f_ox", [P, QUAD], U32)
                    ox_ready = sem("f_ox_ready")
                    psT = ps(sec, "f2_psT", [P, 2, HID])
                    psY = ps(sec, "f2_psY", [P, 2, BANK])
                    ix_ready = sem("f2_ix_ready")
                    hg_ld = [sem(f"f_hg_ld{i}") for i in range(QUAD)]
                    hT_mm = sem("f_hT_mm")
                    hT_ready = sem("f_hT_ready")
                    y_mm = sem("f_y_mm")
                    yo_ready = sem("f_yo_ready")
                    yo_stored = [sem(f"f_yo_stored{i}") for i in range(QUAD)]
                    with nc.Block() as block:
                        @block.gpsimd
                        def _(pool):
                            def gather(i, q, s):
                                wait(pool, hT_mm, i - QUAD + 1)
                                pool.tensor_copy(ix[:, s:s + 1], toks[:, 1, bass.ds(i, 1)]).then_inc(ix_ready, 1)
                                pool.wait_ge(ix_ready, i + 1)
                                pool.nop(nofuse=True)
                                pool.indirect_dma_start(hg[:, s, :], None, h_rows, bass.IndirectOffsetOnAxis(
                                    ap=ix[:, s:s + 1], axis=0)).then_inc(hg_ld[s], 16)

                            def store(i, q, s):
                                pool.wait_ge(yo_ready, i + 1)
                                wait(pool, yo_stored[s], 16 * q)
                                pool.tensor_copy(ox[:, s:s + 1], dest[:, bass.ds(i, 1)]).then_inc(ox_ready, 1)
                                pool.wait_ge(ox_ready, i + 1)
                                pool.nop(nofuse=True)
                                pool.indirect_dma_start(p2_rows, bass.IndirectOffsetOnAxis(ap=ox[:, s:s + 1], axis=0),
                                                        yo[:, s, :], None).then_inc(yo_stored[s], 16)

                            def tile(i, q, s):
                                gather(i, q, s)
                                if not (isinstance(i, int) and i < QUAD):
                                    store(i - QUAD, q - 1, s)

                            list_tiles(pool, tile)
                            for i in range(LT - QUAD, LT):
                                store(i, i // QUAD, i % QUAD)
                            for s in range(QUAD):
                                pool.wait_ge(yo_stored[s], 16 * uses(s))

                        @block.tensor
                        def _(pe):
                            def turn(i, q, s):
                                pe.wait_ge(hg_ld[s], 16 * q + 16)
                                wait(pe, hT_ready, i - 1)
                                for k in range(KH):
                                    mm = pe.transpose(psT[:, s % 2, k * P:(k + 1) * P], hg[:, s, k * P:(k + 1) * P],
                                                      ident[:, :])
                                mm.then_inc(hT_mm, 1)

                            def multiply(i, q, s):
                                e = pe.value_load(owner[0:1, 1, bass.ds(i, 1)], min_val=0, max_val=E1 - 1)
                                pe.wait_ge(w2_ld, e * 16 + 16)
                                pe.wait_ge(hT_ready, i + 1)
                                wait(pe, yo_ready, i - 1)
                                for k in range(KH):
                                    mm = pe.matmul(psY[:, s % 2, 0:D], hT[:, s % 2, k, :], W2[:, e, k, :],
                                                   start=k == 0, stop=k == KH - 1)
                                mm.then_inc(y_mm, 1)

                            def tile(i, q, s):
                                if not (isinstance(i, int) and i == LT - 1):
                                    turn(i + 1, *following(q, s))
                                multiply(i, q, s)

                            turn(0, 0, 0)
                            list_tiles(pe, tile)

                        @block.scalar
                        def _(act):
                            def evacuate(i, q, s):
                                act.wait_ge(hT_mm, i + 1)
                                wait(act, y_mm, i - 1)
                                act.activation(hT[:, s % 2].rearrange("p k n -> p (k n)"), psT[:, s % 2, :], ACT.Gelu
                                               ).then_inc(hT_ready, 1)

                            list_tiles(act, evacuate)

                        @block.vector
                        def _(dve):
                            def evacuate(i, q, s):
                                dve.wait_ge(y_mm, i + 1)
                                wait(dve, yo_stored[s], 16 * q)
                                dve.tensor_copy(yo[:, s, :], psY[:, s % 2, 0:D]).then_inc(yo_ready, 1)

                            list_tiles(dve, evacuate)

                        @block.sync
                        def _(sp):
                            sp.wait_ge(hg_ld[1], 16)
                            load_w2(sp, W2_FIRST, E1)

                fin = ExitStack()
                with fin:
                    SETS = 4
                    TURNS = TT // (2 * SETS)
                    g = W[:, 0:TT * TOP * D].rearrange("p (i k d) -> p i k d", k=TOP, d=D)
                    gy_ld = [sem(f"f_gy_ld{i}") for i in range(SETS)]
                    o_step = sem("f_o_step")
                    o_ready = sem("f_o_ready")
                    op_step = sem("f_op_step")
                    op_ready = sem("f_op_ready")
                    stored = sem("f_stored")
                    with nc.Block() as block:
                        @block.sync
                        def _(sp):
                            for j in range(TURNS):
                                for s in range(SETS):
                                    i = 2 * (SETS * j + s)
                                    wait(sp, gy_ld[s], 32 * j)
                                    for n in range(2):
                                        sp.dma_start(g[:, i + n], p2_d[i + n]).then_inc(gy_ld[s], 16)

                        @block.vector
                        def _(dve):
                            adds = Chain(dve, o_step, SETS // 2 * 3 * (TOP - 1))
                            with dve.Fori(0, TURNS) as j:
                                adds.turn(j)
                                for s in range(0, SETS, 2):
                                    for n in (s, s + 1):
                                        dve.wait_ge(gy_ld[n], 32 * j + 32)
                                    i = 2 * (SETS * j + s)
                                    for k in range(TOP):
                                        for n in range(1, 4):
                                            ins = dve.scalar_tensor_tensor(Xf[:, i + n, :], g[:, i + n, k, :],
                                                                           wt[:, 1, k, bass.ds(i + n, 1)],
                                                                           Xf[:, i + n, :], ALU.mult, ALU.add)
                                            if k < TOP - 1:
                                                adds.step(ins, hold=False)
                                            else:
                                                ins.then_inc(o_ready, 1)
                                        if k < TOP - 1:
                                            adds.hold()
                                adds.end()

                        @block.gpsimd
                        def _(pool):
                            adds = Chain(pool, op_step, SETS // 2 * TOP)
                            with pool.Fori(0, TURNS) as j:
                                adds.turn(j)
                                for s in range(0, SETS, 2):
                                    pool.wait_ge(gy_ld[s], 32 * j + 32)
                                    i = 2 * (SETS * j + s)
                                    adds.step(pool.tensor_tensor(
                                        g[:, i], g[:, i], wt[:, 1, :, bass.ds(i, 1)].to_broadcast([P, TOP, D]), ALU.mult))
                                    for k in range(TOP):
                                        ins = pool.tensor_tensor(Xf[:, i, :], g[:, i, k, :], Xf[:, i, :], ALU.add)
                                        if k < TOP - 1:
                                            adds.step(ins)
                                        else:
                                            ins.then_inc(op_ready, 1)
                                adds.end()

                        @block.scalar
                        def _(act):
                            with act.Fori(0, TT // 4) as j:
                                for n in range(1, 4):
                                    act.wait_ge(o_ready, 3 * j + n)
                                    act.dma_start(out_tiles[4 * j + n], Xf[:, 4 * j + n, :]).then_inc(stored, 16)
                                act.wait_ge(op_ready, j + 1)
                                act.dma_start(out_tiles[4 * j], Xf[:, 4 * j, :]).then_inc(stored, 16)
                            act.wait_ge(stored, 16 * TT)

        with a0_st, se_st, stage():
            attention("a0_", 0, True, first=True)
        with slots, stage():
            soft_mixture()
        W = sb(ctx, "W", [P, E1 * KD * HID])
        W1 = W[:, :].rearrange("p (e k h) -> p e k h", e=E1, k=KD)
        W2 = W[:, :].rearrange("p (e k d) -> p e k d", e=E1, k=KH)
        w1_ld = sem("f_w1_ld")
        w2_ld = sem("f_w2_ld")

        def load_w1(sp):
            for e in range(E1):
                sp.dma_start(W1[:, e], t["f_W1T"][e].rearrange("(k p) h -> p k h", p=P)).then_inc(w1_ld, 16)

        with stage():
            attention("a1_", 1, False, prefetch=load_w1)
        with stage():
            top3_mixture(W, W1, W2, w1_ld, w2_ld)


def kernel(**inputs):
    import numpy as np
    import concourse.bacc as bacc
    from concourse.bass_utils import run_bass_kernel_spmd

    def flip(a):
        return np.ascontiguousarray(np.swapaxes(np.asarray(a), -1, -2))

    def keep(a):
        return np.ascontiguousarray(np.asarray(a))

    def columns(a):
        return flip(np.asarray(a).reshape(-1, P))

    def hidden(a):
        return keep(np.asarray(a).reshape(E0, KF, P).transpose(2, 0, 1))

    pairs = np.arange(1, 1 + B * N * TOP).reshape(TOP, B * NT, P).transpose(2, 1, 0)
    flat = np.arange(FLAT)
    hmv = np.zeros((P, NCH, VH), np.float32)
    for c in range(NCH):
        for v in range(VH):
            hmv[:CHR[c], c, v] = (flat[c * P:c * P + CHR[c]] // S2 == H0[c] + v)
    arrays = {
        "x": keep(inputs["x"]),
        "ctxT": flip(np.asarray(inputs["ctx_1024"]).reshape(B * S2, D)),
        "mask": keep(inputs["mask_1x1xSxS2_ik0"]),
        "a0_WqT": flip(inputs["L0_xattn_Wq"]), "a0_WkT": flip(inputs["L0_xattn_Wk"]),
        "a0_WvT": flip(inputs["L0_xattn_Wv"]), "a0_WoT": flip(inputs["L0_xattn_Wo"]),
        "a0_bq": columns(inputs["L0_xattn_bq"]), "a0_bk": columns(inputs["L0_xattn_bk"]),
        "a0_bv": keep(inputs["L0_xattn_bv"]), "a0_bo": keep(inputs["L0_xattn_bo"]),
        "a1_Wq": keep(inputs["L1_xattn_Wq"]), "a1_Wk": keep(inputs["L1_xattn_Wkv"][:, :D]),
        "a1_Wv": keep(inputs["L1_xattn_Wkv"][:, D:]), "a1_Wo": keep(inputs["L1_xattn_Wproj"]),
        "a1_bq": columns(inputs["L1_xattn_bq"]), "a1_bk": columns(inputs["L1_xattn_bkv"][:D]),
        "a1_bv": keep(inputs["L1_xattn_bkv"][D:]), "a1_bo": keep(inputs["L1_xattn_bproj"]),
        "m_ng": keep(inputs["L0_ffn_norm_g"]), "m_nb": keep(inputs["L0_ffn_norm_b"]),
        "m_sg": keep(inputs["L0_ffn_slot_g"]), "m_sb": keep(inputs["L0_ffn_slot_b"]),
        "m_scale": keep(inputs["L0_ffn_scale"]),
        "m_se": keep(np.asarray(inputs["L0_ffn_slot_embeds"]).reshape(NS, D)),
        "m_Wg": keep(inputs["L0_ffn_Wg"]), "m_Wu": keep(inputs["L0_ffn_Wu"]), "m_Wd": keep(inputs["L0_ffn_Wd"]),
        "m_bgT": hidden(inputs["L0_ffn_bg"]), "m_buT": hidden(inputs["L0_ffn_bu"]), "m_bd": keep(inputs["L0_ffn_bd"]),
        "f_PwT": flip(inputs["L1_ffn_P_w"]),
        "f_UT": flip(np.concatenate([np.asarray(inputs["L1_ffn_U%d" % i]) for i in (1, 2, 3)])),
        "f_W1T": flip(inputs["L1_ffn_W1"]),
        "f_W2T": keep(np.asarray(inputs["L1_ffn_W2"]).reshape(E1, D, KH, P).transpose(0, 3, 2, 1)),
        "f_b2": keep(inputs["L1_ffn_b2"]),
        "c_iota": np.arange(P, dtype=np.float32),
        "c_below": np.triu(np.ones((P, P), np.float32), 1),
        "c_tokid": np.stack([pairs // DIGIT, pairs % DIGIT], 1).astype(np.float32),
        "c_spare": np.arange(1 + B * N * TOP, 1 + B * N * TOP + LT * P, dtype=np.float32).reshape(LT, P).T.copy(),
        "c_ident": np.eye(P, dtype=np.float32),
        "c_sel": (flat[None, :] % S2 == np.arange(S2)[:, None]).astype(np.float32),
        "c_hmk": (np.arange(P)[:, None] // DK == np.arange(HC)[None, :]).astype(np.float32),
        "c_hmv": hmv.reshape(P, NCH * VH),
    }
    nc = bacc.Bacc("TRN2", target_bir_lowering=False, num_devices=1)
    aps = {n: nc.dram_tensor("in_" + n, a.shape, mybir.dt.from_np(a.dtype), kind="ExternalInput").ap()
           for n, a in arrays.items()}
    out = nc.dram_tensor("out", (B, N, D), F32, kind="ExternalOutput").ap()
    build(nc, aps, out)
    r = run_bass_kernel_spmd(nc, [{"in_" + n: a for n, a in arrays.items()}], core_ids=[0])
    return r.results[0]["out"]
```
